# Optimizing a Trainium2 kernel written in Bass

```python
import numpy as np
import jax
import jax.numpy as jnp

def _softmax(x, axis=-1):
    return jax.nn.softmax(x, axis=axis)

def _gelu(x):
    return jax.nn.gelu(x, approximate=True)

def _silu(x):
    return jax.nn.silu(x)

def _sigmoid(x):
    return jax.nn.sigmoid(x)

def _layernorm(x, axis=-1, eps=1e-05):
    m = jnp.mean(x, axis=axis, keepdims=True)
    v = jnp.var(x, axis=axis, keepdims=True)
    return (x - m) / jnp.sqrt(v + eps)

def _scatter_add(tgt, idx, src, axis=0):
    return tgt.at[idx].add(src)

def _segment_sum(src, seg, n):
    return jax.ops.segment_sum(src, seg, n)
kernel_name = 'mk_xattn_ffn_d2_seqx_r8_412e62'

def setup_inputs(seed: int=0):
    np.random.seed(seed)
    _w = jnp.asarray

    def _rec_inputs():
        import jax
        import jax.numpy as jnp
        _rk = jax.random.key(seed)
        x = 7.22e-05 + 1 * jax.random.normal(jax.random.fold_in(_rk, 1), (8, 128, 256), jnp.float32)
        _lenS = 128 - jax.random.randint(jax.random.fold_in(_rk, 7), (8,), 0, max(1, 128 // 4) + 1, jnp.int32)
        _lenS2 = 128 - jax.random.randint(jax.random.fold_in(_rk, 8), (8,), 0, max(1, 128 // 4) + 1, jnp.int32)
        _ctx_2048P = jax.random.normal(jax.random.fold_in(_rk, 11), (8, 16, 256), jnp.float32)
        _ctx_2048c = jax.random.dirichlet(jax.random.fold_in(_rk, 511), 0.3 * jnp.ones((16,), jnp.float32), (8, 128))
        _ctx_2048t = jnp.einsum('bsk,bkd->bsd', _ctx_2048c, _ctx_2048P)
        _ctx_2048t = _ctx_2048t * jax.lax.rsqrt(jnp.mean(jnp.square(_ctx_2048t)) + 1e-12) * 0.953939
        ctx_2048 = 4.13588e-05 + 0.999923 * (_ctx_2048t + 0.3 * jax.random.normal(jax.random.fold_in(_rk, 611), (8, 128, 256), jnp.float32))
        return (x, ctx_2048)
    x, ctx_2048 = _rec_inputs()

    def _L0_xattn_setup():
        import jax, jax.numpy as jnp
        import numpy as np
        B, D, N, H = (4, 128, 256, 16)
        HD = D // H

        def rotate_half(x):
            x1 = x[..., 0::2]
            x2 = x[..., 1::2]
            return jnp.stack((-x2, x1), axis=-1).reshape(x.shape)

        def apply_cached_rotary_emb(freqs, t):
            return t * freqs[0] + rotate_half(t) * freqs[1]
        key = jax.random.key(seed)
        ks = jax.random.split(key, 13)
        s = 1.0 / np.sqrt(D)
        inp = {'query': jax.random.normal(ks[0], (B, D, N), jnp.float32), 'key': jax.random.normal(ks[1], (B, D, N), jnp.float32), 'value': jax.random.normal(ks[2], (B, D, N), jnp.float32), 'encoding': jax.random.normal(ks[3], (2, 1, 1, N, HD), jnp.float32), 'Wq': jax.random.normal(ks[4], (D, D), jnp.float32) * s, 'bq': jax.random.normal(ks[5], (D,), jnp.float32) * s, 'Wk': jax.random.normal(ks[6], (D, D), jnp.float32) * s, 'bk': jax.random.normal(ks[7], (D,), jnp.float32) * s, 'Wv': jax.random.normal(ks[8], (D, D), jnp.float32) * s, 'bv': jax.random.normal(ks[9], (D,), jnp.float32) * s, 'Wm': jax.random.normal(ks[10], (D, D), jnp.float32) * s, 'bm': jax.random.normal(ks[11], (D,), jnp.float32) * s}
        return inp
    _L0_xattn_all = _L0_xattn_setup()
    _L0_xattn_in = {k: v for k, v in _L0_xattn_all.items() if k in ('encoding', 'Wq', 'bq', 'Wk', 'bk', 'Wv', 'bv', 'Wm', 'bm')}
    del _L0_xattn_all

    def _L0_ffn_setup():
        import jax, jax.numpy as jnp
        import numpy as np
        HIDDEN = 256
        MOE_INTER = 128
        SHARED_INTER = 512
        N_EXPERTS = 16
        TOP_K = 2
        N_GROUP = 4
        TOPK_GROUP = 2
        NORM_TOPK_PROB = True
        ROUTED_SCALING = 1.0

        def relu2(x):
            r = jax.nn.relu(x)
            return r * r

        def _get_topk_indices(scores, e_bias):
            T, E = scores.shape
            s = scores + e_bias[None, :]
            gsz = E // N_GROUP
            group_scores = jax.lax.top_k(s.reshape(T, N_GROUP, gsz), 2)[0].sum(-1)
            group_idx = jax.lax.top_k(group_scores, TOPK_GROUP)[1]
            group_mask = jnp.zeros((T, N_GROUP), dtype=bool).at[jnp.arange(T)[:, None], group_idx].set(True)
            score_mask = jnp.repeat(group_mask, gsz, axis=1)
            masked = jnp.where(score_mask, s, 0.0)
            topk_indices = jax.lax.top_k(masked, TOP_K)[1]
            return jax.lax.stop_gradient(topk_indices)

        def _router(x_flat, router_weight, e_bias):
            logits = jnp.einsum('th,eh->te', x_flat.astype(jnp.float32), router_weight.astype(jnp.float32))
            scores = jax.nn.sigmoid(logits)
            topk_indices = _get_topk_indices(scores, e_bias)
            topk_weights = jnp.take_along_axis(scores, topk_indices, axis=1)
            if NORM_TOPK_PROB:
                topk_weights = topk_weights / (topk_weights.sum(-1, keepdims=True) + 1e-20)
            return (topk_indices, topk_weights * ROUTED_SCALING)
        key = jax.random.key(seed)
        ks = jax.random.split(key, 6)
        s = 0.02
        hidden_states = jax.random.normal(ks[0], (1, 256, HIDDEN), dtype=jnp.float32)
        router_weight = jax.random.normal(ks[1], (N_EXPERTS, HIDDEN), dtype=jnp.float32) * s
        e_bias = jnp.zeros((N_EXPERTS,), dtype=jnp.float32)
        w_up = jax.random.normal(ks[2], (N_EXPERTS, HIDDEN, MOE_INTER), dtype=jnp.float32) * s
        w_down = jax.random.normal(ks[3], (N_EXPERTS, MOE_INTER, HIDDEN), dtype=jnp.float32) * s
        shared_up = jax.random.normal(ks[4], (HIDDEN, SHARED_INTER), dtype=jnp.float32) * s
        shared_down = jax.random.normal(ks[5], (SHARED_INTER, HIDDEN), dtype=jnp.float32) * s
        return {'hidden_states': hidden_states, 'router_weight': router_weight, 'e_bias': e_bias, 'w_up': w_up, 'w_down': w_down, 'shared_up': shared_up, 'shared_down': shared_down}
    _L0_ffn_all = _L0_ffn_setup()
    _L0_ffn_in = {k: v for k, v in _L0_ffn_all.items() if k in ('router_weight', 'e_bias', 'w_up', 'w_down', 'shared_up', 'shared_down')}
    del _L0_ffn_all

    def _L1_xattn_setup():
        import jax, jax.numpy as jnp
        import numpy as np
        DIM = 256
        NHEADS = 32
        HEAD_DIM = DIM // NHEADS
        EPS = 1e-06

        def _rmsnorm(t):
            return t * jax.lax.rsqrt(jnp.mean(t * t, axis=-1, keepdims=True) + EPS)
        key = jax.random.key(seed)
        kx, kc, kq, kk, kv = jax.random.split(key, 5)
        x = jax.random.normal(kx, (2, 512, DIM), dtype=jnp.float32)
        context = jax.random.normal(kc, (2, 64, DIM), dtype=jnp.float32)
        std = 0.02
        Wq = jax.random.normal(kq, (DIM, DIM), dtype=jnp.float32) * std
        Wk = jax.random.normal(kk, (DIM, DIM), dtype=jnp.float32) * std
        Wv = jax.random.normal(kv, (DIM, DIM), dtype=jnp.float32) * std
        return {'x': x, 'context': context, 'Wq': Wq, 'Wk': Wk, 'Wv': Wv}
    _L1_xattn_all = _L1_xattn_setup()
    _L1_xattn_in = {k: v for k, v in _L1_xattn_all.items() if k in ('Wq', 'Wk', 'Wv')}
    del _L1_xattn_all

    def _L1_ffn_setup():
        import jax, jax.numpy as jnp
        import numpy as np
        D_IN = 256
        D_OUT = 256
        RANK = 16
        N_EXPERTS = 16
        MAX_EXPERTS = 32
        ROUTER_HID = 64
        TOPK = 2
        ALPHA = 1.0

        def _forward(x, W, bias, rw1, rb1, rw2, rb2, A, B, gates):
            lead = x.shape[:-1]
            x_flat = x.reshape(-1, D_IN)
            n = x_flat.shape[0]
            feat = jax.lax.stop_gradient(x_flat)
            h = jax.nn.silu(feat @ rw1.T + rb1)
            logits = (h @ rw2.T + rb2)[:, :N_EXPERTS] + gates[None, :]
            topv, topi = jax.lax.top_k(logits, TOPK)
            sm = jax.nn.softmax(topv, axis=-1)
            rows = jnp.arange(n)[:, None]
            coeff = jnp.zeros_like(logits).at[rows, topi].set(sm)
            base = x_flat @ W.T + bias
            xa = jnp.einsum('ni,eri->ner', x_flat, A)
            wxa = xa * coeff[:, :, None]
            delta = jnp.einsum('ner,eor->no', wxa, B)
            out = base + ALPHA * delta
            return out.reshape(*lead, D_OUT)
        key = jax.random.key(seed)
        ks = jax.random.split(key, 10)
        s = 0.02
        x = jax.random.normal(ks[0], (4, 512, D_IN), dtype=jnp.float32)
        W = jax.random.normal(ks[1], (D_OUT, D_IN), dtype=jnp.float32) * s
        bias = jax.random.normal(ks[2], (D_OUT,), dtype=jnp.float32) * s
        rw1 = jax.random.normal(ks[3], (ROUTER_HID, D_IN), dtype=jnp.float32) * s
        rb1 = jnp.zeros((ROUTER_HID,), dtype=jnp.float32)
        rw2 = jax.random.normal(ks[4], (MAX_EXPERTS, ROUTER_HID), dtype=jnp.float32) * s
        rb2 = jnp.zeros((MAX_EXPERTS,), dtype=jnp.float32)
        A = jax.random.normal(ks[5], (N_EXPERTS, RANK, D_IN), dtype=jnp.float32) * s
        B = jax.random.normal(ks[6], (N_EXPERTS, D_OUT, RANK), dtype=jnp.float32) * s
        gates = jnp.ones((N_EXPERTS,), dtype=jnp.float32)
        return {'x': x, 'W': W, 'bias': bias, 'rw1': rw1, 'rb1': rb1, 'rw2': rw2, 'rb2': rb2, 'A': A, 'B': B, 'gates': gates}
    _L1_ffn_all = _L1_ffn_setup()
    _L1_ffn_in = {k: v for k, v in _L1_ffn_all.items() if k in ('W', 'bias', 'rw1', 'rb1', 'rw2', 'rb2', 'A', 'B', 'gates')}
    del _L1_ffn_all
    return {'x': x, 'ctx_2048': ctx_2048, 'L0_xattn_encoding': _L0_xattn_in['encoding'], 'L0_xattn_Wq': _L0_xattn_in['Wq'], 'L0_xattn_bq': _L0_xattn_in['bq'], 'L0_xattn_Wk': _L0_xattn_in['Wk'], 'L0_xattn_bk': _L0_xattn_in['bk'], 'L0_xattn_Wv': _L0_xattn_in['Wv'], 'L0_xattn_bv': _L0_xattn_in['bv'], 'L0_xattn_Wm': _L0_xattn_in['Wm'], 'L0_xattn_bm': _L0_xattn_in['bm'], 'L0_ffn_router_weight': _L0_ffn_in['router_weight'], 'L0_ffn_e_bias': _L0_ffn_in['e_bias'], 'L0_ffn_w_up': _L0_ffn_in['w_up'], 'L0_ffn_w_down': _L0_ffn_in['w_down'], 'L0_ffn_shared_up': _L0_ffn_in['shared_up'], 'L0_ffn_shared_down': _L0_ffn_in['shared_down'], 'L1_xattn_Wq': _L1_xattn_in['Wq'], 'L1_xattn_Wk': _L1_xattn_in['Wk'], 'L1_xattn_Wv': _L1_xattn_in['Wv'], 'L1_ffn_W': _L1_ffn_in['W'], 'L1_ffn_bias': _L1_ffn_in['bias'], 'L1_ffn_rw1': _L1_ffn_in['rw1'], 'L1_ffn_rb1': _L1_ffn_in['rb1'], 'L1_ffn_rw2': _L1_ffn_in['rw2'], 'L1_ffn_rb2': _L1_ffn_in['rb2'], 'L1_ffn_A': _L1_ffn_in['A'], 'L1_ffn_B': _L1_ffn_in['B'], 'L1_ffn_gates': _L1_ffn_in['gates']}

def reference(x, ctx_2048, L0_xattn_encoding, L0_xattn_Wq, L0_xattn_bq, L0_xattn_Wk, L0_xattn_bk, L0_xattn_Wv, L0_xattn_bv, L0_xattn_Wm, L0_xattn_bm, L0_ffn_router_weight, L0_ffn_e_bias, L0_ffn_w_up, L0_ffn_w_down, L0_ffn_shared_up, L0_ffn_shared_down, L1_xattn_Wq, L1_xattn_Wk, L1_xattn_Wv, L1_ffn_W, L1_ffn_bias, L1_ffn_rw1, L1_ffn_rb1, L1_ffn_rw2, L1_ffn_rb2, L1_ffn_A, L1_ffn_B, L1_ffn_gates):
    import jax
    import jax.numpy as jnp

    def _L0_xattn_ref(query, key, value, encoding, Wq, bq, Wk, bk, Wv, bv, Wm, bm):
        import jax, jax.numpy as jnp
        import numpy as np
        B, D, N, H = (4, 128, 256, 16)
        HD = D // H

        def rotate_half(x):
            x1 = x[..., 0::2]
            x2 = x[..., 1::2]
            return jnp.stack((-x2, x1), axis=-1).reshape(x.shape)

        def apply_cached_rotary_emb(freqs, t):
            return t * freqs[0] + rotate_half(t) * freqs[1]
        b, d_model, n = query.shape

        def proj(W, bias, x):
            return jnp.einsum('oi,bin->bon', W, x) + bias[None, :, None]
        q = proj(Wq, bq, query).reshape(b, HD, H, n)
        k = proj(Wk, bk, key).reshape(b, HD, H, n)
        v = proj(Wv, bv, value).reshape(b, HD, H, n)
        q = jnp.transpose(apply_cached_rotary_emb(encoding, jnp.transpose(q, (0, 2, 3, 1))), (0, 3, 1, 2))
        k = jnp.transpose(apply_cached_rotary_emb(encoding, jnp.transpose(k, (0, 2, 3, 1))), (0, 3, 1, 2))
        scores = jnp.einsum('bdhn,bdhm->bhnm', q, k) / np.float32(np.sqrt(HD))
        prob = jax.nn.softmax(scores, axis=-1)
        x = jnp.einsum('bhnm,bdhm->bdhn', prob, v)
        out = jnp.einsum('oi,bin->bon', Wm, x.reshape(b, d_model, n)) + bm[None, :, None]
        return out

    def _L0_ffn_ref(hidden_states, router_weight, e_bias, w_up, w_down, shared_up, shared_down):
        import jax, jax.numpy as jnp
        import numpy as np
        HIDDEN = 256
        MOE_INTER = 128
        SHARED_INTER = 512
        N_EXPERTS = 16
        TOP_K = 2
        N_GROUP = 4
        TOPK_GROUP = 2
        NORM_TOPK_PROB = True
        ROUTED_SCALING = 1.0

        def relu2(x):
            r = jax.nn.relu(x)
            return r * r

        def _get_topk_indices(scores, e_bias):
            T, E = scores.shape
            s = scores + e_bias[None, :]
            gsz = E // N_GROUP
            group_scores = jax.lax.top_k(s.reshape(T, N_GROUP, gsz), 2)[0].sum(-1)
            group_idx = jax.lax.top_k(group_scores, TOPK_GROUP)[1]
            group_mask = jnp.zeros((T, N_GROUP), dtype=bool).at[jnp.arange(T)[:, None], group_idx].set(True)
            score_mask = jnp.repeat(group_mask, gsz, axis=1)
            masked = jnp.where(score_mask, s, 0.0)
            topk_indices = jax.lax.top_k(masked, TOP_K)[1]
            return jax.lax.stop_gradient(topk_indices)

        def _router(x_flat, router_weight, e_bias):
            logits = jnp.einsum('th,eh->te', x_flat.astype(jnp.float32), router_weight.astype(jnp.float32))
            scores = jax.nn.sigmoid(logits)
            topk_indices = _get_topk_indices(scores, e_bias)
            topk_weights = jnp.take_along_axis(scores, topk_indices, axis=1)
            if NORM_TOPK_PROB:
                topk_weights = topk_weights / (topk_weights.sum(-1, keepdims=True) + 1e-20)
            return (topk_indices, topk_weights * ROUTED_SCALING)
        orig_shape = hidden_states.shape
        x = hidden_states.reshape(-1, HIDDEN)
        T = x.shape[0]
        topk_indices, topk_weights = _router(x, router_weight, e_bias)
        combine = jnp.zeros((T, N_EXPERTS), dtype=topk_weights.dtype).at[jnp.arange(T)[:, None], topk_indices].add(topk_weights)
        h1 = jnp.einsum('th,ehi->tei', x, w_up)
        a = relu2(h1) * combine[:, :, None]
        routed = jnp.einsum('tei,eih->th', a, w_down)
        shared = relu2(hidden_states @ shared_up) @ shared_down
        return routed.reshape(orig_shape) + shared

    def _L1_xattn_ref(x, context, Wq, Wk, Wv):
        import jax, jax.numpy as jnp
        import numpy as np
        DIM = 256
        NHEADS = 32
        HEAD_DIM = DIM // NHEADS
        EPS = 1e-06

        def _rmsnorm(t):
            return t * jax.lax.rsqrt(jnp.mean(t * t, axis=-1, keepdims=True) + EPS)
        b, n, _ = x.shape
        m = context.shape[1]
        q = x @ Wq.T
        k_raw = context @ Wk.T
        v_raw = context @ Wv.T
        q = q.reshape(b, n, NHEADS, HEAD_DIM).transpose(0, 2, 1, 3)
        kv = jnp.concatenate([k_raw, v_raw], axis=-1)
        kv = kv.reshape(b, m, NHEADS, HEAD_DIM, 2)
        k = kv[..., 0].transpose(0, 2, 1, 3)
        v = kv[..., 1].transpose(0, 2, 1, 3)
        q = _rmsnorm(q)
        k = _rmsnorm(k)
        scale = HEAD_DIM ** (-0.5)
        scores = jnp.einsum('bhnd,bhmd->bhnm', q, k) * scale
        attn = jax.nn.softmax(scores, axis=-1)
        out = jnp.einsum('bhnm,bhmd->bhnd', attn, v)
        return out.transpose(0, 2, 1, 3).reshape(b, n, NHEADS * HEAD_DIM)

    def _L1_ffn_ref(x, W, bias, rw1, rb1, rw2, rb2, A, B, gates):
        import jax, jax.numpy as jnp
        import numpy as np
        D_IN = 256
        D_OUT = 256
        RANK = 16
        N_EXPERTS = 16
        MAX_EXPERTS = 32
        ROUTER_HID = 64
        TOPK = 2
        ALPHA = 1.0

        def _forward(x, W, bias, rw1, rb1, rw2, rb2, A, B, gates):
            lead = x.shape[:-1]
            x_flat = x.reshape(-1, D_IN)
            n = x_flat.shape[0]
            feat = jax.lax.stop_gradient(x_flat)
            h = jax.nn.silu(feat @ rw1.T + rb1)
            logits = (h @ rw2.T + rb2)[:, :N_EXPERTS] + gates[None, :]
            topv, topi = jax.lax.top_k(logits, TOPK)
            sm = jax.nn.softmax(topv, axis=-1)
            rows = jnp.arange(n)[:, None]
            coeff = jnp.zeros_like(logits).at[rows, topi].set(sm)
            base = x_flat @ W.T + bias
            xa = jnp.einsum('ni,eri->ner', x_flat, A)
            wxa = xa * coeff[:, :, None]
            delta = jnp.einsum('ner,eor->no', wxa, B)
            out = base + ALPHA * delta
            return out.reshape(*lead, D_OUT)
        return _forward(x, W, bias, rw1, rb1, rw2, rb2, A, B, gates)
    x = x + _L0_xattn_ref(_layernorm(x, axis=-1), ctx_2048, ctx_2048, L0_xattn_encoding, L0_xattn_Wq, L0_xattn_bq, L0_xattn_Wk, L0_xattn_bk, L0_xattn_Wv, L0_xattn_bv, L0_xattn_Wm, L0_xattn_bm)
    x = x + _L0_ffn_ref(_layernorm(x, axis=-1), L0_ffn_router_weight, L0_ffn_e_bias, L0_ffn_w_up, L0_ffn_w_down, L0_ffn_shared_up, L0_ffn_shared_down)
    x = x + _L1_xattn_ref(_layernorm(x, axis=-1), ctx_2048, L1_xattn_Wq, L1_xattn_Wk, L1_xattn_Wv)
    x = x + _L1_ffn_ref(_layernorm(x, axis=-1), L1_ffn_W, L1_ffn_bias, L1_ffn_rw1, L1_ffn_rb1, L1_ffn_rw2, L1_ffn_rb2, L1_ffn_A, L1_ffn_B, L1_ffn_gates)
    return x

_drawn_inputs = setup_inputs


def setup_inputs(seed=0):
    import zlib

    import numpy as np

    out = dict(_drawn_inputs(seed))
    spreads = {'L0_ffn_e_bias': (0.0, 0.398),
     'L1_ffn_rb1': (0.0, 0.8),
     'L1_ffn_rb2': (0.0, 0.727),
     'L1_ffn_gates': (1.0, 0.6)}
    factors = {'L0_ffn_router_weight': 5.212,
     'L0_ffn_w_up': 3.658,
     'L0_ffn_w_down': 3.335,
     'L1_ffn_bias': 3.428,
     'L1_ffn_rw1': 8.0,
     'L1_ffn_rw2': 8.0,
     'L1_ffn_A': 3.847,
     'L1_ffn_B': 3.905}
    for name, (base, spread) in spreads.items():
        noise = np.random.default_rng([zlib.crc32(name.encode()), seed]).standard_normal(out[name].shape)
        drawn = base * np.exp(spread * noise) if base else spread * noise
        out[name] = jnp.asarray(drawn.astype(out[name].dtype))
    for name, factor in factors.items():
        out[name] = (out[name] * factor).astype(out[name].dtype)
    return out
```

```python
from contextlib import ExitStack

import numpy as np

import concourse.bass as bass
from concourse import mybir

F32 = mybir.dt.float32
BF16 = mybir.dt.bfloat16
I32 = mybir.dt.int32
ALU = mybir.AluOpType
ACT = mybir.ActivationFunctionType
AX_X = mybir.AxisListType.X

P = 128
NB = 8
D = 256
HD = 8
LN_EPS = 1e-5
RMS_EPS = 1e-6
SCALE = HD ** -0.5
TERMS = 6
ROWS = 64
TERM_PARTS = ((0, 0, 0, 1, 1, 2), (0, 1, 2, 0, 1, 0))
PAIRS = 8
NE = 16
INTER = 128
SHARED = 512
NCH = NE + SHARED // INTER
TOK = NB * P
HALF = TOK // 2
RH = 64
RSQRT_GUESS = 0x5F3759DF


class Steps:

    def __init__(self, eng, sem):
        self.eng, self.sem, self.base, self.n = eng, sem, 0, 0

    def then(self, ins):
        self.n += 1
        ins.then_inc(self.sem, 1)
        self.eng.wait_ge(self.sem, self.base + self.n)

    def enter(self, i, per):
        self.start, self.per, self.base, self.n = self.base + self.n, per, self.base + self.n + i * per, 0

    def leave(self, times):
        assert self.n == self.per, self.n
        self.base, self.n = self.start + times * self.per, 0


def build(nc, t, out, phases=4):
    with ExitStack() as ctx:
        def sb(name, shape, dt=F32):
            return ctx.enter_context(nc.sbuf_tensor(name, shape, dt))

        def sem(name):
            return ctx.enter_context(nc.semaphore(name))

        psum = ctx.enter_context(nc.psum_tensor("psum", [P, 8, 512], F32))

        xall = sb("xall", [P, NB, D])
        wa = sb("wa", [P, 6, P])
        cols = sb("cols", [P, 8])
        rope = sb("rope", [P, 2, D])
        rope_in = sb("rope_in", [P, D])
        eye = sb("eye", [P, P])
        eye16 = sb("eye16", [P, P], BF16)
        ctxb = [sb(f"ctx{i}", [P, D]) for i in range(2)]
        xn = [sb(f"xn{i}", [P, D]) for i in range(2)]
        stats = sb("stats", [P, NB, 6])
        mv = sb("mv", [P, NB, 2])
        rstd = sb("rstd", [P, NB])
        rs_v = sb("rs_v", [P, 64])
        rs_a = sb("rs_a", [P, 64])
        rope_ab = sb("rope_ab", [P, 2, 2, D])
        qk = sb("qk", [P, 2, D])
        qk_rest = sb("qk_rest", [P, 2, D])
        parts = [sb(f"parts{i}", [P, 2, 3, D], BF16) for i in range(2)]
        qstk = [sb(f"qstk{i}", [P, PAIRS, D], BF16) for i in range(2)]
        kstk = [sb(f"kstk{i}", [P, 2, PAIRS, D], BF16) for i in range(2)]
        fill = sb("fill", [P, 2, 2, D], BF16)
        mx = sb("mx", [P, 2, 2, 8])
        mneg = sb("mneg", [P, 2, 2, 8])
        zeros = sb("zeros", [P, 2, 8])
        mpart = sb("mpart", [P, 2, 2, 24], BF16)
        mT = sb("mT", [24, 2, D], BF16)
        prob = [sb(f"prob{i}", [P, 2 * 512]) for i in range(2)]
        vt = [sb(f"vt{i}", [P, 2, 16, 32]) for i in range(2)]
        pvT = [sb(f"pvT{i}", [P, 512]) for i in range(2)]
        den = [sb(f"den{i}", [P, 16]) for i in range(2)]
        o2 = sb("o2", [P, 2 * P])
        o3 = sb("o3", [P, 2 * P])
        cb = sb("cb", [P, 1])
        wup = sb("wup", [P, 2, NCH, INTER])
        wdn = sb("wdn", [P, NCH, D])
        wr = sb("wr", [P, 2, NE])
        rows = sb("rows", [P, 4 * NE + D])
        sel = sb("sel", [3 * NE, NE, P], BF16)
        xnT = sb("xnT", [P, 2, TOK])
        lgT = sb("lgT", [NE, TOK])
        sc = sb("sc", [P, NB, NE])
        sel_s = sb("sel_s", [P, NB, NE])
        pair_sum = sb("pair_sum", [P, NB * 4, 6])
        gsum = sb("gsum", [P, NB, 4])
        hot = [sb(f"hot{i}", [P, NB, NE]) for i in range(2)]
        hot_t = sb("hot_t", [P, NB, NE])
        top = [sb(f"top{i}", [P, NB]) for i in range(2)]
        top_i = sb("top_i", [P, NB])
        comb = sb("comb", [P, NB, NE])
        comb16 = sb("comb16", [P, NB, 3, NE], BF16)
        combT = sb("combT", [3 * NE, TOK], BF16)
        rel = [sb(f"rel{i}", [P, HALF]) for i in range(2)]
        wrel = sb("wrel", [P, HALF])
        act2 = [sb(f"act2{i}", [P, HALF]) for i in range(2)]
        wc = sb("wc", [P, 2, 3 * D])
        ctxT = [sb(f"ctxT{i}", [P, 2, P]) for i in range(2)]
        xT1 = sb("xT1", [P, 2, P])
        sq = sb("sq", [P, 2 * D])
        ss = sb("ss", [P, 64])
        rs = sb("rs", [P, 64])
        qkn = sb("qkn", [P, 2, D])
        wd = sb("wd", [P, 2, 2 * D])
        wb = sb("wb", [P, 2, D])
        w1 = sb("w1", [P, 2, RH])
        w2 = sb("w2", [RH, NE])
        nrb1 = sb("nrb1", [RH, 2])
        eh = sb("eh", [RH, HALF])
        zh = sb("zh", [RH, HALF])
        wxa = [sb(f"wxa{i}", [P, D]) for i in range(4)]
        wxaT = [sb(f"wxaT{i}", [P, 2, P]) for i in range(2)]
        scr = nc.dram_tensor("stack_scratch", (2, 2, 2, P, 4, D), BF16, kind="Internal").ap()

        x_in = sem("x_in")
        w_in = sem("w_in")
        ctx_in = [sem(f"ctx_in{i}") for i in range(2)]
        xn_ready = sem("xn_ready")
        misc_full = sem("misc_full")
        misc_free = sem("misc_free")
        st_full = sem("st_full")
        exp_done = sem("exp_done")
        pv_done = sem("pv_done")
        pv_free = sem("pv_free")
        qk_ready = sem("qk_ready")
        hi_done = sem("hi_done")
        rest_done = sem("rest_done")
        mid_done = sem("mid_done")
        lo_done = sem("lo_done")
        parts_out = [sem(f"parts_out{i}") for i in range(2)]
        stack_in = [[sem(f"stack_in{i}{h}") for h in range(2)] for i in range(2)]
        neg_done = sem("neg_done")
        mrow_in = [sem(f"mrow_in{h}") for h in range(2)]
        o3_ready = sem("o3_ready")
        init = sem("init")
        fill_set = sem("fill_set")
        fill_out = sem("fill_out")
        out_done = sem("out_done")
        w2_in = sem("w2_in")
        sig_ready = sem("sig_ready")
        h_full = sem("h_full")
        relu_done = sem("relu_done")
        a_done = sem("a_done")
        acc_full = sem("acc_full")
        acc_free = sem("acc_free")
        sq_done = sem("sq_done")
        eh_done = sem("eh_done")
        gap_done = sem("gap_done")
        egap_done = sem("egap_done")
        dve_step = sem("dve_step")
        pool_step = sem("pool_step")

        def misc(u):
            return psum[:, 4 + u % 2, :]

        def exp_buf(k):
            return psum[:, 2 * (k % 2):2 * (k % 2) + 2, :]

        def pv_bank(i):
            return psum[:, 6 + i, :]

        def a_uses(step, m, pqk):
            u = [("max", step, 0), ("max", step, 1)] if m and step < PAIRS else []
            u += [("q",)] if pqk and step == 1 else []
            u += [("k",)] if pqk and step == 2 else []
            u += [("v",)] if m and step == 4 else []
            u += [("maxT", 0)] if m and step == 5 else []
            u += [("wm",)] if step == PAIRS else []
            u += [("maxT", 1)] if m and step == PAIRS else []
            return u

        def a_index(m, pqk, use):
            return [x for step in range(PAIRS + 1) for x in a_uses(step, m, pqk)].index(use)

        PROLOGUE = [("cb", 0), ("q", 0), ("k", 0), ("v", 0), ("q", 1), ("k", 1)]
        N_PRO = len(PROLOGUE) + 2 * PAIRS + 2
        PER_A = a_index(True, True, ("maxT", 1)) + 1
        NO_PQK = a_index(True, False, ("maxT", 1)) + 1
        assert N_PRO % 2 == 0 and PER_A % 2 == 0 and NO_PQK % 2 == 0
        A_END = N_PRO + PER_A * (NB - 2) + NO_PQK + 1

        def a_base(b):
            return N_PRO + PER_A * b if not isinstance(b, int) or b < NB - 1 else A_END - 1

        B_USES = [("xT", b) for b in range(NB)] + [("lgT", 0), ("lgT", 1), ("lg",), ("combT",)]
        B_END = A_END + len(B_USES)
        C_PRO = [("xT", 0), ("cT", 0), ("qk", 0), ("qkT", 0), ("xT", 1), ("cT", 1), ("qk", 1), ("qkT", 1), ("v", 0)]
        C_STEPS = 4

        def c_uses(step, m, pqk):
            u = [("xT",), ("cT",)] if pqk and step == 0 else []
            u += [("qk",)] if pqk and step == 1 else []
            u += [("v",)] if m and step == 2 else []
            u += [("qkT",)] if pqk and step == 3 else []
            u += [("o",)] if step == C_STEPS else []
            return u

        def c_index(m, pqk, use):
            return [x for step in range(C_STEPS + 1) for x in c_uses(step, m, pqk)].index(use)

        PER_C = c_index(True, True, ("o",)) + 1
        C_FIRST = B_END + len(C_PRO)
        C_END = C_FIRST + PER_C * (NB - 2) + 2 + 1

        def c_base(b):
            return C_FIRST + PER_C * b if not isinstance(b, int) or b < NB - 1 else C_END - 1

        D_USES = [("xT", 0), ("xT", 1), ("xT", 2), ("xT", 3), ("h", 0), ("lg", 0), ("xa", 0), ("xa", 1),
                  ("wT", 0), ("xa", 2), ("wT", 1), ("o", 0), ("xa", 3), ("wT", 2), ("o", 1), ("wT", 3),
                  ("o", 2), ("o", 3)]
        D_RING = 6
        PER_D = len(D_USES)
        assert PER_D % D_RING == 0 and PER_C % 2 == 0

        block = ctx.enter_context(nc.Block())

        @block.sync
        def _(sp):
            def by_channel(par, ten, term):
                return scr[par, ten].rearrange("h (r t) p n -> t (h r) p n", t=8)[term]

            sp.dma_start(xall[:], t["x"].rearrange("b p d -> p b d")).then_inc(x_in, 16)
            sp.dma_start(ctxb[0][:], t["ctx"][0]).then_inc(ctx_in[0], 16)
            sp.dma_start(wa[:], t["wa"].rearrange("p (w c) -> p w c", w=6)).then_inc(w_in, 16)
            sp.dma_start(cols[:], t["cols"]).then_inc(w_in, 16)
            sp.dma_start(rope[:, 0, :], t["rope"][:, 0:D]).then_inc(w_in, 16)
            sp.dma_start(rope_in[:], t["rope"][:, D:2 * D]).then_inc(w_in, 16)
            sp.dma_start(eye16[:], t["eye16"]).then_inc(w_in, 16)
            sp.dma_start(ctxb[1][:], t["ctx"][1]).then_inc(ctx_in[1], 16)
            sp.wait_ge(fill_set, 4)
            for ten in range(2):
                for par in range(2):
                    for term in range(TERMS, 8):
                        sp.dma_start(by_channel(par, ten, term), fill[:, ten, term - TERMS, :]).then_inc(fill_out, 16)

            def parts_to_dram(b, par):
                sp.wait_ge(lo_done, b + 1)
                for ten in range(2):
                    for term, part in enumerate(TERM_PARTS[ten]):
                        sp.dma_start(by_channel(par, ten, term), parts[par][:, ten, part, :]).then_inc(parts_out[par], 16)

            def stack_from_dram(nth, par, half):
                sp.wait_ge(parts_out[par], nth * 192)
                sp.dma_start(qstk[par][:, 4 * half:4 * half + 4, :], scr[par, 0, half]).then_inc(stack_in[par][half], 16)
                for s in range(2):
                    rows = slice(ROWS * s, ROWS * s + ROWS)
                    sp.dma_start(kstk[par][rows, s, 4 * half:4 * half + 4, :], scr[par, 1, half, rows]
                                 ).then_inc(stack_in[par][half], 16)

            def max_rows(ready, par, half):
                sp.wait_ge(misc_free, ready)
                for s in range(2):
                    r = ROWS * s + TERMS
                    sp.dma_start(qstk[par][r:r + 17:8, 4 * half:4 * half + 4, :],
                                 mT[12 * s:12 * s + 12, half, :]).then_inc(mrow_in[half], 16)

            sp.wait_ge(fill_out, 128)
            sp.wait_ge(init, 2)
            for b in range(2):
                parts_to_dram(b, b)
                for half in range(2):
                    stack_from_dram(1, b, half)
            for half in range(2):
                max_rows(N_PRO - 1 + half, 0, half)

            def slot(i, par, m, pqk):
                b = 2 * i + par
                if pqk:
                    sp.wait_ge(misc_free, a_base(b))
                    sp.dma_start(ctxb[par][:], t["ctx"][b + 2]).then_inc(ctx_in[par], 16)
                if m:
                    max_rows(a_base(b) + a_index(m, pqk, ("maxT", 0)) + 1, 1 - par, 0)
                if pqk:
                    parts_to_dram(b + 2, par)
                    sp.wait_ge(st_full, b * PAIRS + 4)
                    stack_from_dram(i + 2, par, 0)
                    sp.wait_ge(st_full, b * PAIRS + 8)
                    stack_from_dram(i + 2, par, 1)
                if m:
                    max_rows(a_base(b) + a_index(m, pqk, ("maxT", 1)) + 1, 1 - par, 1)

            with sp.Fori(0, 3) as i:
                for par in range(2):
                    slot(i, par, True, True)
            slot(3, 0, True, False)
            if phases <= 2:
                sp.wait_ge(misc_free, A_END)
                if phases == 2:
                    sp.wait_ge(acc_free, 3)
                sp.dma_start(out.rearrange("b p d -> p b d"), xall[:]).then_inc(out_done, 16)
                sp.wait_ge(out_done, 16)
                return

            for b in range(2):
                sp.wait_ge(misc_free, a_base(6 + b))
                sp.dma_start(ctxb[b][:], t["ctx"][b]).then_inc(ctx_in[b], 16)
            for b in range(2):
                sp.wait_ge(misc_free, B_END + 4 * b + 2)
                sp.dma_start(ctxb[b][:], t["ctx"][b + 2]).then_inc(ctx_in[b], 16)
                parts_to_dram(NB + b, b)
                for half in range(2):
                    stack_from_dram(5, b, half)

            def slot_c(i, par, pqk, load):
                b = 2 * i + par
                if load:
                    sp.wait_ge(misc_free, c_base(b) + 2)
                    sp.dma_start(ctxb[par][:], t["ctx"][b + 4]).then_inc(ctx_in[par], 16)
                if pqk:
                    parts_to_dram(NB + b + 2, par)
                    for half in range(2):
                        sp.wait_ge(st_full, NB * PAIRS + b * C_STEPS + 2 * (half + 1))
                        stack_from_dram(i + 6, par, half)

            with sp.Fori(0, 2) as i:
                for par in range(2):
                    slot_c(i, par, True, True)
            for par in range(2):
                slot_c(2, par, True, False)

            if phases == 3:
                sp.wait_ge(misc_free, C_END)
                sp.dma_start(out.rearrange("b p d -> p b d"), xall[:]).then_inc(out_done, 16)
                sp.wait_ge(out_done, 16)
                return

            for b in range(NB):
                sp.wait_ge(misc_free, C_END + PER_D * (b // 4) + D_USES.index(("o", b % 4)) + 1)
                sp.dma_start(out[b], xall[:, b, :]).then_inc(out_done, 16)
            sp.wait_ge(out_done, 16 * NB)

        @block.tensor
        def _(pe):
            def project(par, w, bank):
                src = xn[par] if w == 0 else ctxb[par]
                for r in range(2):
                    last = nc.tensor.matmul(bank[:, r * D:(r + 1) * D], wa[:, w + r, :], src[:],
                                            start=True, stop=True)
                last.then_inc(misc_full, 1)

            def values(par, bank):
                for mb in range(2):
                    last = nc.tensor.matmul(bank[:, mb * P:(mb + 1) * P], ctxb[par][:, mb * P:(mb + 1) * P],
                                            wa[:, 4, :], start=True, stop=True)
                last.then_inc(misc_full, 1)

            def max_scores(par, pair, s, bank):
                for nb in range(2):
                    last = nc.tensor.matmul(bank[:, nb * D:(nb + 1) * D],
                                            qstk[par][:, pair, nb * P:(nb + 1) * P], kstk[par][:, s, pair, :],
                                            start=True, stop=True)
                last.then_inc(misc_full, 1)

            def max_transpose(half, bank):
                o = bank.bitcast(BF16)
                for nb in range(2):
                    last = nc.tensor.transpose(o[0:24, nb * P:(nb + 1) * P], mpart[:, half, nb, :], eye16[:])
                last.then_inc(misc_full, 1)

            def scores(b, par, k, first=False):
                if not first:
                    pe.wait_ge(exp_done, b * PAIRS + k)
                if k % 4 == 0:
                    pe.wait_ge(mrow_in[k // 4], 32 * (b + 1))
                for s in range(2):
                    for mb in range(2):
                        last = nc.tensor.matmul(exp_buf(k)[:, s, mb * D:(mb + 1) * D],
                                                kstk[par][:, s, k, mb * P:(mb + 1) * P], qstk[par][:, k, :],
                                                start=True, stop=True)
                last.then_inc(st_full, 1)

            def pv(b, par, k):
                pe.wait_ge(exp_done, b * PAIRS + k + 2)
                if k % 4 == 0:
                    pe.wait_ge(pv_free, 2 * b + 1 + k // 4)
                for s in range(2):
                    j, g = 2 * (k % 2) + s, k // 2
                    for mb in range(2):
                        last = nc.tensor.matmul(
                            pv_bank(g // 2)[32 * j:32 * j + 32, (g % 2) * D:(g % 2 + 1) * D],
                            vt[par][:, mb, 2 * k + s, :],
                            prob[k % 2][:, (2 * s + mb) * D:(2 * s + mb + 1) * D],
                            start=(mb == 0), stop=(mb == 1))
                last.then_inc(pv_done, 1)

            pe.wait_ge(w_in, 16 * 6)
            nc.tensor.matmul(misc(0)[:, 0:1], wa[:, 5, :], cols[:, 4:5], start=True, stop=True).then_inc(misc_full, 1)
            for u, (kind, b) in list(enumerate(PROLOGUE))[1:]:
                if u > 1:
                    pe.wait_ge(misc_free, u - 1)
                if kind == "q":
                    pe.wait_ge(xn_ready, b + 1)
                    project(b, 0, misc(u))
                elif kind == "k":
                    pe.wait_ge(ctx_in[b], 16)
                    project(b, 2, misc(u))
                else:
                    values(0, misc(u))
            u = len(PROLOGUE)
            pe.wait_ge(init, 2)
            for half in range(2):
                pe.wait_ge(stack_in[0][half], 48)
                for n in range(8):
                    pe.wait_ge(misc_free, u - 1)
                    max_scores(0, 4 * half + n // 2, n % 2, misc(u))
                    u += 1
            for half in range(2):
                pe.wait_ge(misc_free, u - 1)
                pe.wait_ge(neg_done, half + 1)
                max_transpose(half, misc(u))
                u += 1
            scores(0, 0, 0, first=True)

            def slot(i, par, m, pqk):
                b = 2 * i + par
                n = 0
                for step in range(PAIRS + 1):
                    if step < PAIRS - 1:
                        scores(b, par, step + 1)
                    elif step == PAIRS - 1 and m:
                        scores(b + 1, 1 - par, 0)
                    for use in a_uses(step, m, pqk):
                        pe.wait_ge(misc_free, a_base(b) + n - 1)
                        bank = misc(n)
                        if use[0] == "max":
                            if use[1] % 4 == 0:
                                pe.wait_ge(stack_in[1 - par][use[1] // 4], 48 * (i + 1 + par))
                            max_scores(1 - par, use[1], use[2], bank)
                        elif use[0] == "q":
                            pe.wait_ge(xn_ready, b + 3)
                            project(par, 0, bank)
                        elif use[0] == "k":
                            pe.wait_ge(ctx_in[par], 16 * (i + 2))
                            project(par, 2, bank)
                        elif use[0] == "v":
                            values(1 - par, bank)
                        elif use[0] == "maxT":
                            pe.wait_ge(neg_done, 2 * (b + 1) + use[1] + 1)
                            max_transpose(use[1], bank)
                        else:
                            pe.wait_ge(o3_ready, b + 1)
                            nc.tensor.matmul(bank[:, 0:D], wa[:, 5, :], o3[:], start=True, stop=True
                                             ).then_inc(misc_full, 1)
                        n += 1
                    if step < PAIRS:
                        pv(b, par, step)

            with pe.Fori(0, 3) as i:
                for par in range(2):
                    slot(i, par, True, True)
            slot(3, 0, True, False)
            slot(3, 1, False, False)
            if phases < 2:
                return

            def transposes(blocks, bank):
                for n, blk in enumerate(blocks):
                    last = nc.tensor.transpose(bank[:, n * P:(n + 1) * P], blk, eye[:])
                last.then_inc(misc_full, 1)

            pe.wait_ge(misc_free, A_END)
            pe.wait_ge(w2_in, 16 * 11)
            for n, use in enumerate(B_USES):
                u = A_END + n
                pe.wait_ge(misc_free, u - 1)
                bank = misc(u)
                if use[0] == "xT":
                    pe.wait_ge(xn_ready, NB + use[1] + 1)
                    transposes([xn[use[1] % 2][:, f * P:(f + 1) * P] for f in range(2)], bank)
                elif use[0] == "lgT":
                    if use[1] == 0:
                        pe.wait_ge(misc_free, u)
                    for f in range(2):
                        last = nc.tensor.matmul(bank[0:NE, :], wr[:, f, :],
                                                xnT[:, f, use[1] * HALF:(use[1] + 1) * HALF],
                                                start=(f == 0), stop=(f == 1))
                    last.then_inc(misc_full, 1)
                elif use[0] == "lg":
                    pe.wait_ge(misc_free, u)
                    for b in range(NB):
                        last = nc.tensor.transpose(bank[:, b * NE:(b + 1) * NE], lgT[:, b * P:(b + 1) * P],
                                                   eye[0:NE, 0:NE])
                    last.then_inc(misc_full, 1)
                else:
                    pe.wait_ge(misc_free, u)
                    for b in range(NB):
                        last = nc.tensor.transpose(bank.bitcast(BF16)[0:3 * NE, b * P:(b + 1) * P],
                                                   comb16[:, b].rearrange("p q e -> p (q e)"), eye16[:])
                    last.then_inc(misc_full, 1)
            pe.wait_ge(misc_free, B_END)

            def up(c, e):
                for f in range(2):
                    last = nc.tensor.matmul(psum[:, e % 2, :], wup[:, f, e, :],
                                            xnT[:, f, bass.ds(c * HALF, HALF)], start=(f == 0), stop=(f == 1))
                if e < NE:
                    last = nc.tensor.matmul(psum[:, 2 + e % 2, :], sel[:, e, :], combT[:, bass.ds(c * HALF, HALF)],
                                            start=True, stop=True)
                last.then_inc(h_full, 1)

            def down(c, e):
                pe.wait_ge(a_done, c * NCH + e + 1)
                if e == 0:
                    pe.wait_ge(acc_free, c + 1)
                for j in range(4):
                    last = nc.tensor.matmul(psum[:, 6 + j // 2, (j % 2) * D:(j % 2 + 1) * D],
                                            act2[e % 2][:, j * P:(j + 1) * P], wdn[:, e, :],
                                            start=(e == 0 and j % 2 == 0), stop=(e == NCH - 1),
                                            skip_group_check=True)
                if e == NCH - 1:
                    last.then_inc(acc_full, 1)

            with pe.Fori(0, 2) as c:
                up(c, 0)
                for e in range(NCH):
                    if e + 1 < NCH:
                        up(c, e + 1)
                    down(c, e)
            if phases < 3:
                return

            def c_use(kind, b, par, bank, u):
                if kind == "xT":
                    pe.wait_ge(xn_ready, 2 * NB + b + 1)
                    transposes([xn[par][:, f * P:(f + 1) * P] for f in range(2)], bank)
                elif kind == "cT":
                    transposes([ctxb[par][:, f * P:(f + 1) * P] for f in range(2)], bank)
                elif kind == "qk":
                    pe.wait_ge(misc_free, u)
                    for ten, src in enumerate((xT1, ctxT[par])):
                        for f in range(2):
                            last = nc.tensor.matmul(bank[:, ten * D:(ten + 1) * D], src[:, f, :],
                                                    wc[:, f, ten * D:(ten + 1) * D], start=(f == 0), stop=(f == 1))
                    last.then_inc(misc_full, 1)
                elif kind == "qkT":
                    transposes([qkn[:, ten, f * P:(f + 1) * P] for ten in range(2) for f in range(2)], bank)
                elif kind == "v":
                    for f in range(2):
                        last = nc.tensor.matmul(bank[:, 0:D], ctxT[par][:, f, :], wc[:, f, 2 * D:3 * D],
                                                start=(f == 0), stop=(f == 1))
                    last.then_inc(misc_full, 1)
                else:
                    pe.wait_ge(o3_ready, NB + b + 1)
                    transposes([o3[:, f * P:(f + 1) * P] for f in range(2)], bank)

            def scores_c(b, par, k, first=False):
                if not first:
                    pe.wait_ge(exp_done, NB * PAIRS + b * C_STEPS + k)
                buf = exp_buf(k).rearrange("p a n -> p (a n)")
                for pp in range(2):
                    for ch in range(2):
                        for s in range(2):
                            h = 4 * pp + 2 * ch + s
                            last = nc.tensor.matmul(buf[:, h * P:(h + 1) * P],
                                                    kstk[par][:, s, 2 * k + pp, ch * P:(ch + 1) * P],
                                                    qstk[par][:, 2 * k + pp, ch * P:(ch + 1) * P],
                                                    start=True, stop=True)
                last.then_inc(st_full, 1)

            def pv_c(b, par, k):
                pe.wait_ge(exp_done, NB * PAIRS + b * C_STEPS + k + 2)
                if k % 2 == 0:
                    pe.wait_ge(pv_free, 2 * NB + 2 * b + k // 2 + 1)
                v = vt[par][:].rearrange("m a h r -> m (a h) r")
                for pp in range(2):
                    for j in range(4):
                        h = 4 * pp + j
                        g = 2 * (k % 2) + pp
                        last = nc.tensor.matmul(pv_bank(k // 2)[32 * j:32 * j + 32, g * P:(g + 1) * P],
                                                v[:, 8 * k + h, :], prob[k % 2][:, h * P:(h + 1) * P],
                                                start=True, stop=True)
                last.then_inc(pv_done, 1)

            for n, (kind, b) in enumerate(C_PRO):
                u = B_END + n
                pe.wait_ge(misc_free, u if kind == "qkT" else u - 1)
                if kind == "cT":
                    pe.wait_ge(ctx_in[b], 16 * 5)
                c_use(kind, b, b, misc(u), u)
            for half in range(2):
                pe.wait_ge(stack_in[0][half], 48 * 5)
            scores_c(0, 0, 0)

            def slot_c(i, par, m, pqk):
                b = 2 * i + par
                n = 0
                for step in range(C_STEPS + 1):
                    if step < C_STEPS - 1:
                        scores_c(b, par, step + 1)
                    elif step == C_STEPS - 1 and m:
                        for half in range(2):
                            pe.wait_ge(stack_in[1 - par][half], 48 * (i + par + 5))
                        scores_c(b + 1, 1 - par, 0)
                    for (kind,) in c_uses(step, m, pqk):
                        u = c_base(b) + n
                        pe.wait_ge(misc_free, u - 1)
                        if kind == "qkT":
                            pe.wait_ge(misc_free, c_base(b) + c_index(m, pqk, ("qk",)) + 1)
                        if kind == "cT":
                            pe.wait_ge(ctx_in[par], 16 * (i + 6))
                        ahead = {"v": 1, "o": 0}.get(kind, 2)
                        c_use(kind, b + ahead, (par + ahead) % 2, misc(C_FIRST + n), u)
                        n += 1
                    if step < C_STEPS:
                        pv_c(b, par, step)

            with pe.Fori(0, 3) as i:
                for par in range(2):
                    slot_c(i, par, True, True)
            slot_c(3, 0, True, False)
            slot_c(3, 1, False, False)
            if phases < 4:
                return

            pe.wait_ge(misc_free, C_END)
            with pe.Fori(0, 2) as c:
                for n, (kind, j) in enumerate(D_USES):
                    u = C_END + c * PER_D + n
                    pe.wait_ge(misc_free, u - D_RING + 1)
                    bank = psum[:, n % D_RING, :]
                    mine = xnT[:, :, j * P:(j + 1) * P]
                    if kind == "xT":
                        pe.wait_ge(xn_ready, 3 * NB + 4 * c + j + 1)
                        transposes([xn[j % 2][:, f * P:(f + 1) * P] for f in range(2)], bank)
                    elif kind == "h":
                        pe.wait_ge(misc_free, u)
                        for f in range(2):
                            last = nc.tensor.matmul(bank[0:RH, :], w1[:, f, :], xnT[:, f, 0:HALF],
                                                    start=(f == 0), stop=(f == 1))
                        last.then_inc(misc_full, 1)
                    elif kind == "lg":
                        pe.wait_ge(misc_free, u)
                        for q in range(4):
                            last = nc.tensor.matmul(bank[:, q * NE:(q + 1) * NE], eh[:, q * P:(q + 1) * P], w2[:],
                                                    start=True, stop=True)
                        last.then_inc(misc_full, 1)
                    elif kind == "xa":
                        for f in range(2):
                            last = nc.tensor.matmul(bank[:, 0:D], mine[:, f, :], wd[:, f, D:2 * D],
                                                    start=(f == 0), stop=(f == 1))
                        last.then_inc(misc_full, 1)
                    elif kind == "wT":
                        pe.wait_ge(misc_free, C_END + c * PER_D + D_USES.index(("xa", j)) + 1)
                        transposes([wxa[j][:, f * P:(f + 1) * P] for f in range(2)], bank)
                    else:
                        for f in range(2):
                            nc.tensor.matmul(bank[:, 0:D], mine[:, f, :], wd[:, f, 0:D], start=(f == 0), stop=False)
                        pe.wait_ge(misc_free, C_END + c * PER_D + D_USES.index(("wT", j)) + 1)
                        for f in range(2):
                            last = nc.tensor.matmul(bank[:, 0:D], wxaT[j % 2][:, f, :], wb[:, f, :],
                                                    start=False, stop=(f == 1))
                        last.then_inc(misc_full, 1)

        @block.scalar
        def _(act):
            def exps(b, k):
                act.wait_ge(st_full, b * PAIRS + k + 1)
                nc.scalar.activation(prob[k % 2][:], exp_buf(k).rearrange("p a n -> p (a n)"), ACT.Exp,
                                     scale=SCALE).then_inc(exp_done, 1)

            def first_parts(b, par, gone):
                act.wait_ge(qk_ready, b + 2)
                if gone is not None:
                    act.wait_ge(parts_out[par], gone * 192)
                nc.scalar.copy(parts[par][:, :, 0, :], qk[:]).then_inc(hi_done, 1)

            def second_parts(b, par):
                act.wait_ge(rest_done, b + 1)
                nc.scalar.copy(parts[par][:, :, 1, :], qk_rest[:]).then_inc(mid_done, 1)

            act.dma_start(eye[:], t["eye"]).then_inc(w_in, 16)
            act.drain().then_inc(exp_done, 1)
            for b in range(2):
                first_parts(b, b, None)
                second_parts(b, b)

            for dst, name in ((wr[:], "wr"), (rows[:], "rows"), (sel[:], "sel"), (wup[:], "wup"), (wdn[:], "wdn"),
                              (wc[:], "wc"), (wd[:], "wd"), (wb[:], "wb"), (w1[:], "w1"), (w2[:], "w2"),
                              (nrb1[:, 0:1], "rb1")):
                act.dma_start(dst, t[name]).then_inc(w2_in, 16)

            def slot(i, par, pqk):
                b = 2 * i + par
                for k in range(PAIRS):
                    exps(b, k)
                    if pqk and k == 3:
                        first_parts(b + 2, par, i + 1)
                    if pqk and k == 4:
                        second_parts(b + 2, par)

            with act.Fori(0, 3) as i:
                for par in range(2):
                    slot(i, par, True)
            slot(3, 0, False)
            slot(3, 1, False)
            if phases < 2:
                return

            act.wait_ge(misc_full, A_END + B_USES.index(("lg",)) + 1)
            nc.scalar.activation(sc[:].rearrange("p b e -> p (b e)"), misc(A_END + B_USES.index(("lg",)))[:, 0:NB * NE],
                                 ACT.Exp, scale=-1.0).then_inc(sig_ready, 1)
            with act.Fori(0, 2) as c:
                for e in range(NCH):
                    act.wait_ge(h_full, c * NCH + e + 1)
                    nc.scalar.activation(rel[e % 2][:], psum[:, e % 2, :], ACT.Relu).then_inc(relu_done, 1)
            if phases < 3:
                return

            def squares(b, u, bank):
                act.wait_ge(misc_full, u + 1)
                nc.scalar.activation(sq[:], bank, ACT.Square).then_inc(sq_done, 1)

            def first_parts_c(u, bank, par, gone):
                act.wait_ge(misc_full, u + 1)
                act.wait_ge(parts_out[par], gone * 192)
                nc.scalar.copy(parts[par][:, :, 0, :], bank.rearrange("p (t n) -> p t n", t=2)).then_inc(hi_done, 1)

            def second_parts_c(u, par):
                act.wait_ge(misc_free, u + 1)
                nc.scalar.copy(parts[par][:, :, 1, :], qk_rest[:]).then_inc(mid_done, 1)

            for b in range(2):
                u = B_END + 4 * b + 2
                squares(b, u, misc(u))
                first_parts_c(u + 1, misc(u + 1), b, 4)
                second_parts_c(u + 1, b)

            def slot_c(i, par, pqk):
                b = 2 * i + par
                for k in range(C_STEPS):
                    act.wait_ge(st_full, NB * PAIRS + b * C_STEPS + k + 1)
                    nc.scalar.activation(prob[k % 2][:], exp_buf(k).rearrange("p a n -> p (a n)"), ACT.Exp,
                                         scale=SCALE).then_inc(exp_done, 1)
                    if pqk and k == 1:
                        n = c_index(True, True, ("qk",))
                        squares(b + 2, c_base(b) + n, misc(C_FIRST + n))
                    if pqk and k == 3:
                        n = c_index(True, True, ("qkT",))
                        first_parts_c(c_base(b) + n, misc(C_FIRST + n), par, i + 5)
                        second_parts_c(c_base(b) + n, par)

            with act.Fori(0, 3) as i:
                for par in range(2):
                    slot_c(i, par, True)
            slot_c(3, 0, False)
            slot_c(3, 1, False)
            if phases < 4:
                return

            with act.Fori(0, 2) as c:
                n = D_USES.index(("h", 0))
                act.wait_ge(misc_full, C_END + c * PER_D + n + 1)
                nc.scalar.activation(eh[:], psum[0:RH, n % D_RING, :], ACT.Exp, bias=nrb1[:, 1:2], scale=-1.0
                                     ).then_inc(eh_done, 1)
                act.wait_ge(gap_done, c + 1)
                nc.scalar.activation(top_i[:, 0:4], top_i[:, 0:4], ACT.Exp).then_inc(egap_done, 1)

        @block.gpsimd
        def _(pool):
            steps = Steps(pool, pool_step)
            for i in range(2):
                nc.gpsimd.memset(kstk[i][:].bitcast(F32), 0.0).then_inc(init, 1)

            def rotate(ready):
                pool.wait_ge(misc_free, ready)
                nc.gpsimd.tensor_tensor(qk[:], rope_ab[:, 0], rope_ab[:, 1], ALU.add).then_inc(qk_ready, 1)

            def rest(b, par):
                pool.wait_ge(hi_done, b + 1)
                nc.gpsimd.tensor_tensor(qk_rest[:], qk[:], parts[par][:, :, 0, :], ALU.subtract
                                        ).then_inc(rest_done, 1)

            def third(b, par):
                pool.wait_ge(mid_done, b + 1)
                nc.gpsimd.tensor_tensor(parts[par][:, :, 2, :], qk_rest[:], parts[par][:, :, 1, :],
                                        ALU.subtract).then_inc(lo_done, 1)

            def negate(ready, half):
                pool.wait_ge(misc_free, ready)
                part = mpart[:, half].rearrange("n b (s q p) -> n b s q p", s=2, q=3)
                m = mneg[:, half].rearrange("n b (s p) -> n b s p", s=2)
                zero = zeros[:, 0].rearrange("n (s p) -> n s p", s=2)
                steps.then(nc.gpsimd.tensor_tensor(mneg[:, half], zeros[:], mx[:, half], ALU.subtract))
                for q in range(2):
                    for nb in range(2):
                        last = nc.gpsimd.tensor_tensor(part[:, nb, :, q, :], m[:, nb], zero, ALU.add)
                        if nb:
                            steps.then(last)
                    for nb in range(2):
                        last = nc.gpsimd.tensor_tensor(m[:, nb], m[:, nb], part[:, nb, :, q, :], ALU.subtract)
                        if nb:
                            steps.then(last)
                for nb in range(2):
                    last = nc.gpsimd.tensor_tensor(part[:, nb, :, 2, :], m[:, nb], zero, ALU.add)
                last.then_inc(neg_done, 1)

            nc.gpsimd.memset(zeros[:], 0.0).then_inc(init, 1)
            pool.wait_ge(init, 3)
            nc.gpsimd.drain().then_inc(qk_ready, 1)
            for b in range(2):
                rotate(3 if b == 0 else 6)
                rest(b, b)
                third(b, b)
            for half in range(2):
                negate(len(PROLOGUE) + 8 * (half + 1), half)

            def slot(i, par, m, pqk):
                b = 2 * i + par
                if pqk:
                    rotate(a_base(b) + a_index(m, pqk, ("k",)) + 1)
                if m:
                    negate(a_base(b) + a_index(m, pqk, ("max", 3, 1)) + 1, 0)
                if pqk:
                    rest(b + 2, par)
                    third(b + 2, par)
                if m:
                    negate(a_base(b) + a_index(m, pqk, ("max", 7, 1)) + 1, 1)

            PER_POOL = 2 * 2 * 5
            with pool.Fori(0, 3) as i:
                steps.enter(i, PER_POOL)
                for par in range(2):
                    slot(i, par, True, True)
            steps.leave(3)
            slot(3, 0, True, False)
            if phases < 3:
                return

            for b in range(2):
                third(NB + b, b)
            with pool.Fori(0, 3) as i:
                for par in range(2):
                    third(NB + 2 * i + par + 2, par)

        @block.vector
        def _(dve):
            steps = Steps(dve, dve_step)

            def rsqrt(o, var, scale, eps, n):
                v, a = rs_v[:, 0:n], rs_a[:, 0:n]
                steps.then(nc.vector.tensor_scalar(v, var, scale, eps, ALU.mult, ALU.add))
                steps.then(nc.vector.tensor_scalar(a.bitcast(I32), v.bitcast(I32), 1, None,
                                                   ALU.logical_shift_right))
                steps.then(nc.vector.tensor_scalar(o.bitcast(I32), a.bitcast(I32), -1.0, float(RSQRT_GUESS),
                                                   ALU.mult, ALU.add))
                for _ in range(3):
                    steps.then(nc.vector.tensor_tensor(a, o, v, ALU.mult))
                    steps.then(nc.vector.scalar_tensor_tensor(out=a, in0=a, scalar=-0.5, in1=o,
                                                              op0=ALU.mult, op1=ALU.mult))
                    steps.then(nc.vector.scalar_tensor_tensor(out=o, in0=a, scalar=1.5, in1=o,
                                                              op0=ALU.add, op1=ALU.mult))

            def norm_stats():
                for b in range(NB):
                    last = nc.vector.bn_stats(stats[:, b, :], xall[:, b, :])
                steps.then(last)
                for b in range(NB):
                    last = nc.vector.bn_aggr(mv[:, b, :], stats[:, b, :])
                steps.then(last)
                rsqrt(rstd[:], mv[:, :, 1], 1.0, LN_EPS, NB)

            def normalize(b, par):
                nc.vector.tensor_scalar(xn[par][:], xall[:, b, :], mv[:, b, 0:1], rstd[:, b:b + 1] if isinstance(b, int)
                                        else rstd[:, bass.ds(b, 1)], ALU.subtract, ALU.mult).then_inc(xn_ready, 1)

            def factors(ten, bank):
                for r in range(2):
                    last = nc.vector.scalar_tensor_tensor(
                        out=rope_ab[:, r, ten, :], in0=bank[:, r * D:(r + 1) * D],
                        scalar=cols[:, 2 * ten + r:2 * ten + r + 1], in1=rope[:, r, :], op0=ALU.add, op1=ALU.mult)
                last.then_inc(misc_free, 1)

            def take_values(par, bank):
                nc.vector.tensor_copy(vt[par][:, :, :, 0:HD],
                                      bank[:, 0:D].rearrange("m (a h d) -> m a h d", a=2, d=HD)).then_inc(misc_free, 1)

            def row_max(pair, s, bank):
                half, p4 = pair // 4, pair % 4
                nc.vector.tensor_reduce(mx[:, half, :, 4 * s + p4:4 * s + p4 + 1],
                                        bank.rearrange("n (b m) -> n b m", b=2), AX_X, ALU.max).then_inc(misc_free, 1)

            def take_maxT(half, bank):
                nc.vector.tensor_copy(mT[:, half, :], bank.bitcast(BF16)[0:24, 0:D]).then_inc(misc_free, 1)

            def divide(b, i):
                dve.wait_ge(pv_done, b * PAIRS + 4 * (i + 1))
                ins = nc.vector.transpose(pvT[i][:], pv_bank(i))
                ins.then_inc(pv_free, 1)
                dve.wait_ge(pv_free, 2 * b + i + 3)
                cells = pvT[i][:].rearrange("p (x r) -> p x r", r=32)
                steps.then(nc.vector.reciprocal(den[i][:], cells[:, :, HD]))
                o = o2[:].rearrange("p (n g d) -> p g n d", g=4, d=HD)
                for g in range(2):
                    last = nc.vector.tensor_tensor(
                        o[:, 2 * i + g], cells[:, 8 * g:8 * g + 8, 0:HD],
                        den[i][:, 8 * g:8 * g + 8].unsqueeze(2).broadcast_to((P, 8, HD)), ALU.mult)
                steps.then(last)
                if i == 1:
                    nc.vector.transpose(o3[:], o2[:]).then_inc(o3_ready, 1)

            steps.then(nc.vector.memset(fill[:], 0.0))
            for j in range(4):
                nc.vector.memset(fill[32 * j:32 * j + 12, 1, 0, :], 1.0).then_inc(fill_set, 1)
            for i in range(2):
                steps.then(nc.vector.memset(vt[i][:], 0.0))
                last = nc.vector.memset(vt[i][:, :, :, HD:HD + 1], 1.0)
                last.then_inc(pv_free, 1)
            dve.wait_ge(x_in, 16)
            norm_stats()
            dve.wait_ge(w_in, 16 * 6)
            steps.then(nc.vector.tensor_scalar(rope[:, 1, :], rope_in[:], cols[:, 6:7], None, ALU.mult))
            for b in range(2):
                normalize(b, b)
            for u, (kind, b) in enumerate(PROLOGUE):
                dve.wait_ge(misc_full, u + 1)
                if kind == "cb":
                    nc.vector.tensor_scalar(cb[:], misc(u)[:, 0:1], cols[:, 5:6], None, ALU.add).then_inc(misc_free, 1)
                elif kind == "v":
                    take_values(0, misc(u))
                else:
                    if b and kind == "q":
                        dve.wait_ge(qk_ready, b + 1)
                    factors(int(kind == "k"), misc(u))
            u = len(PROLOGUE)
            for n in range(2 * PAIRS):
                dve.wait_ge(misc_full, u + 1)
                row_max(n // 2, n % 2, misc(u))
                u += 1
            for half in range(2):
                dve.wait_ge(misc_full, u + 1)
                take_maxT(half, misc(u))
                u += 1

            def slot(i, par, m, pqk):
                b = 2 * i + par
                if pqk:
                    normalize(b + 2, par)
                n = 0
                for step in range(PAIRS + 1):
                    for use in a_uses(step, m, pqk):
                        dve.wait_ge(misc_full, a_base(b) + n + 1)
                        bank = misc(n)
                        if use[0] == "max":
                            if use[1] % 4 == 0 and use[2] == 0:
                                dve.wait_ge(neg_done, 2 * b + use[1] // 4 + 1)
                            row_max(use[1], use[2], bank)
                        elif use[0] == "q":
                            dve.wait_ge(qk_ready, b + 3)
                            factors(0, bank)
                        elif use[0] == "k":
                            factors(1, bank)
                        elif use[0] == "v":
                            take_values(1 - par, bank)
                        elif use[0] == "maxT":
                            dve.wait_ge(mrow_in[use[1]], 32 * (b + 1))
                            take_maxT(use[1], bank)
                        else:
                            xb = xall[:, b, :]
                            nc.vector.scalar_tensor_tensor(out=xb, in0=bank[:, 0:D], scalar=cb[:], in1=xb,
                                                           op0=ALU.add, op1=ALU.add).then_inc(misc_free, 1)
                        n += 1
                    if step == 4 or step == 7:
                        divide(b, step // 7)

            with dve.Fori(0, 3) as i:
                steps.enter(i, 8)
                for par in range(2):
                    slot(i, par, True, True)
            steps.leave(3)
            slot(3, 0, True, False)
            slot(3, 1, False, False)
            if phases < 2:
                return

            def spread(small, big, n):
                return small.unsqueeze(2).broadcast_to((P, big, n))

            def pick(hot_o, peak, v, groups, n):
                num = rows[:, 3 * NE:3 * NE + n] if n == NE else rows[:, 4 * NE - n:4 * NE]
                num = num.unsqueeze(1).broadcast_to((P, groups, n))
                th = hot_t[:].rearrange("p b e -> p (b e)")[:, 0:groups * n].rearrange("p (b e) -> p b e", e=n)
                low = top_i[:, 0:groups]
                steps.then(nc.vector.tensor_reduce(peak.unsqueeze(2), v, AX_X, ALU.max))
                steps.then(nc.vector.tensor_tensor(th, v, spread(peak, groups, n), ALU.is_equal))
                steps.then(nc.vector.tensor_tensor(th, th, num, ALU.mult))
                steps.then(nc.vector.tensor_reduce(low.unsqueeze(2), th, AX_X, ALU.min))
                steps.then(nc.vector.tensor_tensor(hot_o, num, spread(low, groups, n), ALU.is_equal))

            def drop(v, hot_i):
                steps.then(nc.vector.scalar_tensor_tensor(out=v, in0=hot_i, scalar=-3.0e38, in1=v,
                                                          op0=ALU.mult, op1=ALU.add))

            dve.wait_ge(misc_free, A_END)
            norm_stats()
            dve.wait_ge(w2_in, 16 * 11)
            lg_u = A_END + B_USES.index(("lg",))
            for b in range(2):
                normalize(b, b)
            for n, use in enumerate(B_USES):
                u = A_END + n
                dve.wait_ge(misc_full, u + 1)
                bank = misc(u)
                if use[0] == "xT":
                    b = use[1]
                    nc.vector.tensor_copy(xnT[:, :, b * P:(b + 1) * P], bank[:, 0:D].rearrange("p (f n) -> p f n", f=2)
                                          ).then_inc(misc_free, 1)
                    if b + 2 < NB:
                        normalize(b + 2, b % 2)
                elif use[0] == "lgT":
                    nc.vector.tensor_copy(lgT[:, use[1] * HALF:(use[1] + 1) * HALF], bank[0:NE, :]
                                          ).then_inc(misc_free, 1)
                elif use[0] == "lg":
                    dve.wait_ge(sig_ready, 1)
                    steps.then(nc.vector.tensor_scalar(sc[:], sc[:], 1.0, None, ALU.add))
                    steps.then(nc.vector.reciprocal(sc[:], sc[:]))
                    steps.then(nc.vector.tensor_tensor(sel_s[:], sc[:], rows[:, 0:NE].unsqueeze(1).broadcast_to(
                        (P, NB, NE)), ALU.add))
                    s4 = sel_s[:].rearrange("p b (g e) -> p (b g) e", g=4)
                    nc.vector.tensor_tensor(pair_sum[:, :, 0:3], s4[:, :, 0:3], s4[:, :, 1:4], ALU.add)
                    nc.vector.tensor_tensor(pair_sum[:, :, 3:5], s4[:, :, 0:2], s4[:, :, 2:4], ALU.add)
                    steps.then(nc.vector.tensor_tensor(pair_sum[:, :, 5:6], s4[:, :, 0:1], s4[:, :, 3:4], ALU.add))
                    steps.then(nc.vector.tensor_reduce(gsum[:].rearrange("p b g -> p (b g)").unsqueeze(2),
                                                       pair_sum[:], AX_X, ALU.max))
                    g4 = [h[:].rearrange("p b e -> p (b e)")[:, 0:NB * 4].rearrange("p (b g) -> p b g", g=4)
                          for h in hot]
                    pick(g4[0], top[0][:], gsum[:], NB, 4)
                    drop(gsum[:], g4[0])
                    pick(g4[1], top[0][:], gsum[:], NB, 4)
                    steps.then(nc.vector.tensor_tensor(gsum[:], g4[0], g4[1], ALU.add))
                    steps.then(nc.vector.tensor_tensor(
                        s4, s4, spread(gsum[:].rearrange("p b g -> p (b g)"), NB * 4, 4), ALU.mult))
                    pick(hot[0][:], top[0][:], sel_s[:], NB, NE)
                    drop(sel_s[:], hot[0][:])
                    pick(hot[1][:], top[0][:], sel_s[:], NB, NE)
                    steps.then(nc.vector.tensor_tensor(comb[:], hot[0][:], hot[1][:], ALU.add))
                    steps.then(nc.vector.tensor_tensor(comb[:], comb[:], sc[:], ALU.mult))
                    steps.then(nc.vector.tensor_reduce(top[0][:].unsqueeze(2), comb[:], AX_X, ALU.add))
                    steps.then(nc.vector.tensor_scalar(top[0][:], top[0][:], 1e-20, None, ALU.add))
                    steps.then(nc.vector.reciprocal(top[1][:], top[0][:]))
                    steps.then(nc.vector.tensor_tensor(comb[:], comb[:], spread(top[1][:], NB, NE), ALU.mult))
                    for q in range(2):
                        steps.then(nc.vector.tensor_copy(comb16[:, :, q, :], comb[:]))
                        steps.then(nc.vector.tensor_tensor(comb[:], comb[:], comb16[:, :, q, :], ALU.subtract))
                    nc.vector.tensor_copy(comb16[:, :, 2, :], comb[:]).then_inc(misc_free, 1)
                else:
                    nc.vector.tensor_copy(combT[:], bank.bitcast(BF16)[0:3 * NE, :]).then_inc(misc_free, 1)

            dve.drain().then_inc(acc_free, 1)
            with dve.Fori(0, 2) as c:
                steps.enter(c, NE)
                for e in range(NCH):
                    dve.wait_ge(relu_done, c * NCH + e + 1)
                    r = rel[e % 2][:]
                    if e:
                        dve.wait_ge(a_done, c * NCH + e)
                    if e < NE:
                        steps.then(nc.vector.tensor_tensor(wrel[:], psum[:, 2 + e % 2, :], r, ALU.mult))
                    nc.vector.tensor_tensor(act2[e % 2][:], wrel[:] if e < NE else r, r, ALU.mult).then_inc(a_done, 1)
                dve.wait_ge(acc_full, c + 1)
                for j in range(4):
                    xb = xall[:, bass.ds(4 * c + j, 1), :].rearrange("p o n -> p (o n)")
                    last = nc.vector.tensor_tensor(xb, psum[:, 6 + j // 2, (j % 2) * D:(j % 2 + 1) * D], xb, ALU.add)
                last.then_inc(acc_free, 1)
            steps.leave(2)
            if phases < 3:
                return

            dve.wait_ge(acc_free, 3)
            norm_stats()
            for b in range(2):
                normalize(b, b)

            def c_use(kind, par, bank, b=None):
                if kind == "xT":
                    nc.vector.tensor_copy(xT1[:], bank[:, 0:D].rearrange("p (f n) -> p f n", f=2)
                                          ).then_inc(misc_free, 1)
                elif kind == "cT":
                    nc.vector.tensor_copy(ctxT[par][:], bank[:, 0:D].rearrange("p (f n) -> p f n", f=2)
                                          ).then_inc(misc_free, 1)
                elif kind == "qk":
                    dve.wait_ge(sq_done, b + 1)
                    steps.then(nc.vector.tensor_reduce(
                        ss[:].rearrange("n (x p) -> n x p", p=4).unsqueeze(3),
                        sq[:].rearrange("n (x d p) -> n x p d", d=HD, p=4), AX_X, ALU.add))
                    rsqrt(rs[:], ss[:], 1.0 / HD, RMS_EPS, 64)
                    for ten in range(2):
                        last = nc.vector.tensor_tensor(
                            qkn[:, ten].rearrange("n (x d p) -> n x d p", d=HD, p=4),
                            bank[:, ten * D:(ten + 1) * D].rearrange("n (x d p) -> n x d p", d=HD, p=4),
                            rs[:, 32 * ten:32 * ten + 32].rearrange("n (x p) -> n x p", p=4).unsqueeze(2
                                ).broadcast_to((P, 8, HD, 4)), ALU.mult)
                    last.then_inc(misc_free, 1)
                elif kind == "qkT":
                    dve.wait_ge(hi_done, NB + b + 1)
                    dve.wait_ge(lo_done, NB + b)
                    nc.vector.tensor_tensor(qk_rest[:], bank.rearrange("p (t n) -> p t n", t=2),
                                            parts[par][:, :, 0, :], ALU.subtract).then_inc(misc_free, 1)
                elif kind == "v":
                    nc.vector.tensor_copy(vt[par][:].rearrange("m a h r -> m (a h) r")[:, :, 0:HD],
                                          bank[:, 0:D].rearrange("m (h d) -> m h d", d=HD)).then_inc(misc_free, 1)
                else:
                    nc.vector.tensor_tensor(xall[:, b, :], bank[:, 0:D], xall[:, b, :], ALU.add
                                            ).then_inc(misc_free, 1)

            def divide_c(b, i):
                dve.wait_ge(pv_done, NB * PAIRS + b * C_STEPS + 2 * (i + 1))
                nc.vector.transpose(pvT[i][:], pv_bank(i)).then_inc(pv_free, 1)
                dve.wait_ge(pv_free, 2 * NB + 2 * b + i + 3)
                cells = pvT[i][:].rearrange("p (x r) -> p x r", r=32)
                steps.then(nc.vector.reciprocal(den[i][:], cells[:, :, HD]))
                steps.then(nc.vector.tensor_tensor(
                    o2[:, i * P:(i + 1) * P].rearrange("p (n g d) -> p g n d", n=4, d=HD),
                    cells[:, :, 0:HD].rearrange("p (g n) d -> p g n d", g=4),
                    den[i][:].rearrange("p (g n) -> p g n", g=4).unsqueeze(3).broadcast_to((P, 4, 4, HD)), ALU.mult))
                if i == 1:
                    nc.vector.transpose(o3[:], o2[:]).then_inc(o3_ready, 1)

            for n, (kind, b) in enumerate(C_PRO):
                dve.wait_ge(misc_full, B_END + n + 1)
                c_use(kind, b, misc(B_END + n), b)

            def slot_c(i, par, m, pqk):
                b = 2 * i + par
                if pqk:
                    normalize(b + 2, par)
                n = 0
                for step in range(C_STEPS + 1):
                    for (kind,) in c_uses(step, m, pqk):
                        dve.wait_ge(misc_full, c_base(b) + n + 1)
                        ahead = {"v": 1, "o": 0}.get(kind, 2)
                        c_use(kind, (par + ahead) % 2, misc(C_FIRST + n), b + ahead)
                        n += 1
                    if step == 2 or step == 3:
                        divide_c(b, step - 2)

            with dve.Fori(0, 3) as i:
                steps.enter(i, 2 * (1 + 12 + 4))
                for par in range(2):
                    slot_c(i, par, True, True)
            steps.leave(3)
            slot_c(3, 0, True, False)
            slot_c(3, 1, False, False)
            if phases < 4:
                return

            dve.wait_ge(misc_free, C_END)
            norm_stats()
            steps.then(nc.vector.tensor_scalar(nrb1[:, 1:2], nrb1[:, 0:1], -1.0, None, ALU.mult))
            with dve.Fori(0, 2) as c:
                steps.enter(c, 24)
                for j in range(2):
                    normalize(4 * c + j, j)
                for n, (kind, j) in enumerate(D_USES):
                    dve.wait_ge(misc_full, C_END + c * PER_D + n + 1)
                    bank = psum[:, n % D_RING, :]
                    if kind == "xT":
                        nc.vector.tensor_copy(xnT[:, :, j * P:(j + 1) * P],
                                              bank[:, 0:D].rearrange("p (f n) -> p f n", f=2)).then_inc(misc_free, 1)
                        if j < 2:
                            normalize(4 * c + j + 2, j)
                    elif kind == "h":
                        dve.wait_ge(eh_done, c + 1)
                        nc.vector.tensor_scalar(zh[:], bank[0:RH, :], nrb1[:, 0:1], None, ALU.add)
                        steps.then(nc.vector.tensor_scalar(eh[:], eh[:], 1.0, None, ALU.add))
                        steps.then(nc.vector.reciprocal(eh[:], eh[:]))
                        nc.vector.tensor_tensor(eh[:], eh[:], zh[:], ALU.mult).then_inc(misc_free, 1)
                    elif kind == "lg":
                        lg = sel_s[:, 0:4, :]
                        h0, h1 = hot[0][:, 0:4, :], hot[1][:, 0:4, :]
                        for q in range(2):
                            row = rows[:, (q + 1) * NE:(q + 2) * NE].unsqueeze(1).broadcast_to((P, 4, NE))
                            src = bank[:, 0:4 * NE].rearrange("p (b e) -> p b e", e=NE) if q == 0 else lg
                            steps.then(nc.vector.tensor_tensor(lg, src, row, ALU.add))
                        pick(h0, top[0][:, 0:4], lg, 4, NE)
                        drop(lg, h0)
                        pick(h1, top[1][:, 0:4], lg, 4, NE)
                        nc.vector.tensor_tensor(top_i[:, 0:4], top[1][:, 0:4], top[0][:, 0:4], ALU.subtract
                                                ).then_inc(gap_done, 1)
                        dve.wait_ge(egap_done, c + 1)
                        steps.then(nc.vector.tensor_scalar(top[0][:, 0:4], top_i[:, 0:4], 1.0, None, ALU.add))
                        steps.then(nc.vector.reciprocal(top[0][:, 0:4], top[0][:, 0:4]))
                        steps.then(nc.vector.tensor_tensor(top[1][:, 0:4], top_i[:, 0:4], top[0][:, 0:4], ALU.mult))
                        steps.then(nc.vector.tensor_tensor(h0, h0, spread(top[0][:, 0:4], 4, NE), ALU.mult))
                        steps.then(nc.vector.tensor_tensor(h1, h1, spread(top[1][:, 0:4], 4, NE), ALU.mult))
                        nc.vector.tensor_tensor(comb[:, 0:4, :], h0, h1, ALU.add).then_inc(misc_free, 1)
                        dve.wait_ge(misc_free, C_END + c * PER_D + n + 1)
                    elif kind == "xa":
                        nc.vector.tensor_tensor(wxa[j][:].rearrange("p (e r) -> p e r", e=NE),
                                                bank[:, 0:D].rearrange("p (e r) -> p e r", e=NE),
                                                spread(comb[:, j, :], NE, D // NE), ALU.mult).then_inc(misc_free, 1)
                    elif kind == "wT":
                        nc.vector.tensor_copy(wxaT[j % 2][:], bank[:, 0:D].rearrange("p (f n) -> p f n", f=2)
                                              ).then_inc(misc_free, 1)
                    else:
                        xb = xall[:, bass.ds(4 * c + j, 1), :].rearrange("p o n -> p (o n)")
                        steps.then(nc.vector.tensor_tensor(xb, xb, rows[:, 4 * NE:4 * NE + D], ALU.add))
                        nc.vector.tensor_tensor(xb, bank[:, 0:D], xb, ALU.add).then_inc(misc_free, 1)
            steps.leave(2)


def layouts(inp):
    a = {k: np.asarray(v) for k, v in inp.items()}
    half, s, d, p4 = np.meshgrid(np.arange(2), np.arange(2), np.arange(HD), np.arange(4), indexing="ij")
    c0 = (16 * d + 8 * half + 4 * s + p4).ravel()
    c0_rot = (16 * (d ^ 1) + 8 * half + 4 * s + p4).ravel()
    dd = d.ravel()
    k_, s_, d_ = np.meshgrid(np.arange(PAIRS), np.arange(2), np.arange(HD), indexing="ij")
    v0 = (16 * d_ + 8 * (k_ // 4) + 4 * s_ + k_ % 4).ravel()
    j_, g_, e_ = np.meshgrid(np.arange(4), np.arange(4), np.arange(HD), indexing="ij")
    kk = 2 * g_ + j_ // 2
    o0 = (16 * e_ + 8 * (kk // 4) + 4 * (j_ % 2) + kk % 4).ravel()
    wq, wk, wv, wm = (a[f"L0_xattn_W{x}"] for x in "qkvm")
    bq, bk, bv, bm = (a[f"L0_xattn_b{x}"] for x in "qkvm")
    wa = np.concatenate([wq[c0].T, wq[c0_rot].T, wk[c0].T, wk[c0_rot].T, wv[v0].T, wm[:, o0].T], axis=1)
    sign = np.where(dd % 2, 1.0, -1.0).astype(np.float32)
    zero = np.zeros(P, np.float32)
    cols = np.stack([bq[c0], bq[c0_rot], bk[c0], bk[c0_rot], bv[o0], bm, sign, zero], axis=1)
    enc = a["L0_xattn_encoding"].reshape(2, D, HD)
    rope = np.concatenate([enc[0].T[dd], enc[1].T[dd]], axis=1)
    bf16 = mybir.dt.np(BF16)
    def blocks(w):
        return w.reshape(2, P, -1).transpose(1, 0, 2)

    up = a["L0_ffn_w_up"].reshape(NE, 2, P, INTER).transpose(2, 1, 0, 3)
    s_up = a["L0_ffn_shared_up"].reshape(2, P, NCH - NE, INTER).transpose(1, 0, 2, 3)
    dn = a["L0_ffn_w_down"].transpose(1, 0, 2)
    s_dn = a["L0_ffn_shared_down"].reshape(NCH - NE, INTER, D).transpose(1, 0, 2)
    row = np.concatenate([a["L0_ffn_e_bias"], a["L1_ffn_rb2"][:NE], a["L1_ffn_gates"],
                          np.arange(-NE, 0, dtype=np.float32), a["L1_ffn_bias"]])
    sel = np.zeros((3, NE, NE, P), np.float32)
    for e in range(NE):
        sel[:, e, e] = 1.0
    ch, hf, sm, dm, pm = np.meshgrid(np.arange(2), np.arange(2), np.arange(2), np.arange(HD), np.arange(4), indexing="ij")
    hd = 16 * hf + 4 * (2 * ch + sm) + pm
    q1, kv1 = (HD * hd + dm).ravel(), (2 * (HD * hd + dm)).ravel()
    pr, cv, sv, dv = np.meshgrid(np.arange(PAIRS), np.arange(2), np.arange(2), np.arange(HD), indexing="ij")
    v1 = (2 * (HD * (16 * (pr // 4) + 4 * (2 * cv + sv) + pr % 4) + dv) + 1).ravel()
    wkv = np.concatenate([a["L1_xattn_Wk"], a["L1_xattn_Wv"]], axis=0)
    wc = blocks(np.concatenate([a["L1_xattn_Wq"][q1].T, wkv[kv1].T, wkv[v1].T], axis=1))
    wA = a["L1_ffn_A"].reshape(D, D).T
    wB = a["L1_ffn_B"].transpose(0, 2, 1).reshape(D, D)
    t = {"wr": blocks(a["L0_ffn_router_weight"].T), "rows": np.broadcast_to(row, (P, row.size)),
         "sel": sel.reshape(3 * NE, NE, P).astype(bf16),
         "wup": np.concatenate([up, s_up], axis=2), "wdn": np.concatenate([dn, s_dn], axis=1),
         "wc": wc, "wd": blocks(np.concatenate([a["L1_ffn_W"].T, wA], axis=1)), "wb": blocks(wB),
         "w1": blocks(a["L1_ffn_rw1"].T), "w2": a["L1_ffn_rw2"][:NE].T, "rb1": a["L1_ffn_rb1"].reshape(RH, 1),
         "x": a["x"], "ctx": a["ctx_2048"], "wa": wa, "cols": cols, "rope": rope,
         "eye": np.eye(P, dtype=np.float32), "eye16": np.eye(P).astype(bf16)}
    return {k: np.ascontiguousarray(v) for k, v in t.items()}


def kernel(**inputs):
    import concourse.bacc as bacc
    from concourse.bass_utils import run_bass_kernel_spmd

    nc = bacc.Bacc("TRN2", target_bir_lowering=False, num_devices=1)
    arrays = {f"in_{k}": v for k, v in layouts(inputs).items()}
    t = {k[3:]: nc.dram_tensor(k, v.shape, mybir.dt.from_np(v.dtype), kind="ExternalInput").ap()
         for k, v in arrays.items()}
    out = nc.dram_tensor("out_0", (NB, P, D), F32, kind="ExternalOutput").ap()
    build(nc, t, out)
    return run_bass_kernel_spmd(nc, [arrays], core_ids=[0]).results[0]["out_0"]
```

```python
from contextlib import ExitStack

import numpy as np

import concourse.bass as bass
from concourse import mybir

F32 = mybir.dt.float32
BF16 = mybir.dt.bfloat16
I32 = mybir.dt.int32
ALU = mybir.AluOpType
ACT = mybir.ActivationFunctionType
AX_X = mybir.AxisListType.X

P = 128
NB = 8
D = 256
HD = 8
LN_EPS = 1e-5
RMS_EPS = 1e-6
SCALE = HD ** -0.5
TERMS = 6
ROWS = 64
MAX_ROW = 46
TERM_PARTS = ((0, 0, 0, 1, 1, 2), (0, 1, 2, 0, 1, 0))
PAIRS = 8
NE = 16
INTER = 128
SHARED = 512
NCH = NE + SHARED // INTER
TOK = NB * P
HALF = TOK // 2
RH = 64
RSQRT_GUESS = 0x5F3759DF


class Steps:

    def __init__(self, eng, sem):
        self.eng, self.sem, self.base, self.n = eng, sem, 0, 0

    def then(self, ins):
        self.n += 1
        ins.then_inc(self.sem, 1)
        self.eng.wait_ge(self.sem, self.base + self.n)

    def enter(self, i, per):
        self.start, self.per, self.base, self.n = self.base + self.n, per, self.base + self.n + i * per, 0

    def leave(self, times):
        assert self.n == self.per, self.n
        self.base, self.n = self.start + times * self.per, 0


def build(nc, t, out, phases=4):
    with ExitStack() as ctx:
        def sb(name, shape, dt=F32):
            return ctx.enter_context(nc.sbuf_tensor(name, shape, dt))

        def sem(name):
            return ctx.enter_context(nc.semaphore(name))

        psum = ctx.enter_context(nc.psum_tensor("psum", [P, 8, 512], F32))

        xall = sb("xall", [P, NB, D])
        wa = sb("wa", [P, 6, P])
        cols = sb("cols", [P, 8])
        rope = sb("rope", [P, 2, D])
        rope_in = sb("rope_in", [P, D])
        eye = sb("eye", [P, P])
        eye16 = sb("eye16", [P, P], BF16)
        ctxb = [sb(f"ctx{i}", [P, D]) for i in range(2)]
        xn = [sb(f"xn{i}", [P, D]) for i in range(2)]
        stats = sb("stats", [P, NB, 6])
        mv = sb("mv", [P, NB, 2])
        rstd = sb("rstd", [P, NB])
        rs_v = sb("rs_v", [P, 64])
        rs_a = sb("rs_a", [P, 64])
        rope_ab = sb("rope_ab", [P, 2, 2, D])
        qk = sb("qk", [P, 2, D])
        qk_rest = sb("qk_rest", [P, 2, D])
        parts = [sb(f"parts{i}", [P, 2, 3, D], BF16) for i in range(2)]
        qstk = [sb(f"qstk{i}", [P, PAIRS, D], BF16) for i in range(2)]
        kstk = [sb(f"kstk{i}", [P, 2, PAIRS, D], BF16) for i in range(2)]
        fill = sb("fill", [P, 2, 2, D], BF16)
        mx = sb("mx", [P, 2, 2, 8])
        mneg = sb("mneg", [P, 2, 2, 8])
        zeros = sb("zeros", [P, 2, 8])
        mpart = sb("mpart", [P, 2, 2, 24], BF16)
        mT = sb("mT", [24, 2, D], BF16)
        prob = [sb(f"prob{i}", [P, 2 * 512]) for i in range(2)]
        vt = [sb(f"vt{i}", [P, 2, 16, 32]) for i in range(2)]
        pvT = [sb(f"pvT{i}", [P, 512]) for i in range(2)]
        den = [sb(f"den{i}", [P, 16]) for i in range(2)]
        o2 = sb("o2", [P, 2 * P])
        o3 = sb("o3", [P, 2 * P])
        cb = sb("cb", [P, 1])
        wup = sb("wup", [P, 2, NCH, INTER])
        wdn = sb("wdn", [P, NCH, D])
        wr = sb("wr", [P, 2, NE])
        rows = sb("rows", [P, 4 * NE + D])
        sel = sb("sel", [3 * NE, NE, P], BF16)
        xnT = sb("xnT", [P, 2, TOK])
        lgT = sb("lgT", [NE, TOK])
        sc = sb("sc", [P, NB, NE])
        sel_s = sb("sel_s", [P, NB, NE])
        pair_sum = sb("pair_sum", [P, NB * 4, 6])
        gsum = sb("gsum", [P, NB, 4])
        hot = [sb(f"hot{i}", [P, NB, NE]) for i in range(2)]
        hot_t = sb("hot_t", [P, NB, NE])
        top = [sb(f"top{i}", [P, NB]) for i in range(2)]
        top_i = sb("top_i", [P, NB])
        comb = sb("comb", [P, NB, NE])
        comb16 = sb("comb16", [P, NB, 3, NE], BF16)
        combT = sb("combT", [3 * NE, TOK], BF16)
        rel = [sb(f"rel{i}", [P, HALF]) for i in range(2)]
        wrel = sb("wrel", [P, HALF])
        act2 = [sb(f"act2{i}", [P, HALF]) for i in range(2)]
        wc = sb("wc", [P, 2, 3 * D])
        ctxT = [sb(f"ctxT{i}", [P, 2, P]) for i in range(2)]
        xT1 = sb("xT1", [P, 2, P])
        sq = sb("sq", [P, 2 * D])
        ss = sb("ss", [P, 64])
        rs = sb("rs", [P, 64])
        qkn = sb("qkn", [P, 2, D])
        wd = sb("wd", [P, 2, 2 * D])
        wb = sb("wb", [P, 2, D])
        w1 = sb("w1", [P, 2, RH])
        w2 = sb("w2", [RH, NE])
        nrb1 = sb("nrb1", [RH, 2])
        eh = sb("eh", [RH, HALF])
        zh = sb("zh", [RH, HALF])
        wxa = [sb(f"wxa{i}", [P, D]) for i in range(4)]
        wxaT = [sb(f"wxaT{i}", [P, 2, P]) for i in range(2)]
        scr = nc.dram_tensor("stack_scratch", (2, 2, P * 8, D), BF16, kind="Internal").ap()

        x_in = sem("x_in")
        w_in = sem("w_in")
        ctx_in = [sem(f"ctx_in{i}") for i in range(2)]
        xn_ready = sem("xn_ready")
        misc_full = sem("misc_full")
        misc_free = sem("misc_free")
        st_full = sem("st_full")
        exp_done = sem("exp_done")
        pv_done = sem("pv_done")
        pv_free = sem("pv_free")
        qk_ready = sem("qk_ready")
        hi_done = sem("hi_done")
        rest_done = sem("rest_done")
        mid_done = sem("mid_done")
        lo_done = sem("lo_done")
        parts_out = [sem(f"parts_out{i}") for i in range(2)]
        stack_in = [[sem(f"stack_in{i}{h}") for h in range(2)] for i in range(2)]
        neg_done = sem("neg_done")
        mrow_in = [sem(f"mrow_in{h}") for h in range(2)]
        o3_ready = sem("o3_ready")
        init = sem("init")
        fill_set = sem("fill_set")
        fill_out = sem("fill_out")
        out_done = sem("out_done")
        w2_in = sem("w2_in")
        sig_ready = sem("sig_ready")
        h_full = sem("h_full")
        relu_done = sem("relu_done")
        a_done = sem("a_done")
        acc_full = sem("acc_full")
        acc_free = sem("acc_free")
        sq_done = sem("sq_done")
        eh_done = sem("eh_done")
        gap_done = sem("gap_done")
        egap_done = sem("egap_done")
        dve_step = sem("dve_step")
        pool_step = sem("pool_step")

        def misc(u):
            return psum[:, 4 + u % 2, :]

        def exp_buf(k):
            return psum[:, 2 * (k % 2):2 * (k % 2) + 2, :]

        def pv_bank(i):
            return psum[:, 6 + i, :]

        def a_uses(step, wm, m, pqk):
            u = [("v",)] if m and step == 0 else []
            u += [("maxT", 1)] if step == 1 else []
            u += [("max", step, 0), ("max", step, 1)] if m else []
            u += [("q",)] if pqk and step == 2 else []
            u += [("wm",)] if wm and step == 3 else []
            u += [("k",)] if pqk and step == 4 else []
            u += [("maxT", 0)] if m and step == 5 else []
            return u

        def a_index(flags, use):
            return [x for step in range(PAIRS) for x in a_uses(step, *flags)].index(use)

        def a_flags(b):
            return b > 0, b < NB - 1, b < NB - 3

        def count(uses, steps, flags, b):
            return sum(len(uses(step, *flags(b))) for step in range(steps))

        PROLOGUE = [("cb", 0), ("k", 0), ("q", 0), ("v", 0), ("k", 1), ("q", 1), ("k", 2), ("q", 2)]
        N_PRO = len(PROLOGUE) + 2 * PAIRS + 1
        PER_A = count(a_uses, PAIRS, a_flags, 1)
        assert PER_A % 2 == 0 and all(a_flags(b) == a_flags(1) for b in range(1, 5))

        def first_use(start, uses, steps, flags, b):
            if isinstance(b, int):
                return start + sum(count(uses, steps, flags, x) for x in range(b))
            per = count(uses, steps, flags, 1)
            return start + count(uses, steps, flags, 0) - per + per * b

        def a_base(b):
            return first_use(N_PRO, a_uses, PAIRS, a_flags, b)

        A_END = a_base(NB) + 1

        W2_IN = 16 * 17
        B_USES = [("xT", b) for b in range(NB)] + [("lgT", 0), ("lgT", 1), ("lg",), ("combT",)]
        B_END = A_END + len(B_USES)
        C_PRO = [("xT", 0), ("cT", 0), ("qk", 0), ("qkT", 0), ("v", 0), ("xT", 1), ("cT", 1), ("qk", 1), ("qkT", 1),
                 ("xT", 2), ("cT", 2), ("qk", 2)]
        C_STEPS = 4
        AHEAD = {"v": 1, "o": -1, "xT": 3, "cT": 3, "qk": 3, "qkT": 2}

        def c_uses(step, o, m, t, pqk):
            u = [("v",)] if m and step == 0 else []
            u += [("qkT",)] if t and step == 1 else []
            u += [("o",)] if o and step == 1 else []
            u += [("xT",), ("cT",)] if pqk and step == 2 else []
            u += [("qk",)] if pqk and step == 3 else []
            return u

        def c_flags(b):
            return b > 0, b < NB - 1, b < NB - 2, b < NB - 3

        def c_index(flags, use):
            return [x for step in range(C_STEPS) for x in c_uses(step, *flags)].index(use)

        PER_C = count(c_uses, C_STEPS, c_flags, 1)
        C_FIRST = B_END + len(C_PRO)

        def c_base(b):
            return first_use(C_FIRST, c_uses, C_STEPS, c_flags, b)

        C_END = c_base(NB) + 1

        D_USES = [("xT", 0), ("xT", 1), ("xT", 2), ("xT", 3), ("h", 0), ("lg", 0), ("xa", 0), ("xa", 1),
                  ("wT", 0), ("xa", 2), ("wT", 1), ("o", 0), ("xa", 3), ("wT", 2), ("o", 1), ("wT", 3),
                  ("o", 2), ("o", 3)]
        D_RING = 6
        PER_D = len(D_USES)
        assert PER_D % D_RING == 0 and PER_C % 2 == 0

        block = ctx.enter_context(nc.Block())

        @block.sync
        def _(sp):
            def by_channel(par, ten, first, n):
                return scr[par, ten].rearrange("(c t) n -> c t n", t=8)[:, first:first + n, :]

            sp.dma_start(xall[:], t["x"].rearrange("b p d -> p b d")).then_inc(x_in, 16)
            sp.dma_start(ctxb[0][:], t["ctx"][0]).then_inc(ctx_in[0], 16)
            sp.dma_start(wa[:], t["wa"].rearrange("p (w c) -> p w c", w=6)).then_inc(w_in, 16)
            sp.dma_start(cols[:], t["cols"]).then_inc(w_in, 16)
            sp.dma_start(rope[:, 0, :], t["rope"][:, 0:D]).then_inc(w_in, 16)
            sp.dma_start(rope_in[:], t["rope"][:, D:2 * D]).then_inc(w_in, 16)
            sp.dma_start(eye16[:], t["eye16"]).then_inc(w_in, 16)
            sp.dma_start(ctxb[1][:], t["ctx"][1]).then_inc(ctx_in[1], 16)
            sp.wait_ge(fill_set, 1)
            for ten in range(2):
                for par in range(2):
                    sp.dma_start(by_channel(par, ten, TERMS, 2), fill[:, ten]).then_inc(fill_out, 16)

            def parts_to_dram(b0, i):
                par, nth = b0 % 2, b0 // 2 + i
                sp.wait_ge(lo_done, b0 + 2 * i + 1)
                if b0 >= 2:
                    for half in range(2):
                        sp.wait_ge(stack_in[par][half], nth * 48)
                src = parts[par]
                for part, (first, n) in enumerate(((0, 3), (3, 2), (5, 1))):
                    sp.dma_start(by_channel(par, 0, first, n), src[:, 0, part:part + 1, :].broadcast_to((P, n, D))
                                 ).then_inc(parts_out[par], 16)
                for first, n in ((0, 3), (3, 2), (5, 1)):
                    sp.dma_start(by_channel(par, 1, first, n), src[:, 1, 0:n, :]).then_inc(parts_out[par], 16)

            def stack_from_dram(b0, i, half):
                par, nth = b0 % 2, b0 // 2 + i
                sp.wait_ge(parts_out[par], nth * 96 + 96)
                src = [scr[par, ten].rearrange("(k r) n -> r k n", r=P)[:, 4 * half:4 * half + 4, :] for ten in range(2)]
                sp.dma_start(qstk[par][:, 4 * half:4 * half + 4, :], src[0]).then_inc(stack_in[par][half], 16)
                for s in range(2):
                    rows = slice(ROWS * s, ROWS * s + ROWS)
                    sp.dma_start(kstk[par][rows, s, 4 * half:4 * half + 4, :], src[1][rows]
                                 ).then_inc(stack_in[par][half], 16)

            def max_rows(ready, par, half):
                sp.wait_ge(misc_free, ready)
                sp.dma_start(qstk[par][MAX_ROW:MAX_ROW + 41:8, 4 * half:4 * half + 4, :],
                             mT[:, half, :]).then_inc(mrow_in[half], 16)

            def weights(names):
                for name in names:
                    dst = {"wr": wr, "rows": rows, "sel": sel, "wc": wc, "wd": wd, "wb": wb, "w1": w1, "w2": w2}
                    if name in dst:
                        sp.dma_start(dst[name][:], t[name]).then_inc(w2_in, 16)
                    elif name == "rb1":
                        sp.dma_start(nrb1[:, 0:1], t[name]).then_inc(w2_in, 16)
                    else:
                        kind, c = name
                        e = slice(5 * c, 5 * c + 5)
                        if kind == "wup":
                            sp.dma_start(wup[:, :, e, :], t["wup"][:, :, e, :]).then_inc(w2_in, 16)
                        else:
                            sp.dma_start(wdn[:, e, :], t["wdn"][:, e, :]).then_inc(w2_in, 16)

            sp.wait_ge(fill_out, 64)
            sp.wait_ge(init, 2)
            sp.wait_ge(misc_free, PROLOGUE.index(("v", 0)) + 1)
            sp.dma_start(ctxb[0][:], t["ctx"][2]).then_inc(ctx_in[0], 16)
            for b in range(2):
                parts_to_dram(b, 0)
                for half in range(2):
                    stack_from_dram(b, 0, half)
            max_rows(N_PRO, 0, 0)
            parts_to_dram(2, 0)

            def slot(b0, i, shape):
                b = b0 + 2 * i
                wm, m, pqk = flags = a_flags(shape)
                if pqk:
                    sp.wait_ge(misc_free, a_base(b) + a_index(flags, ("v",)) + 1)
                    sp.dma_start(ctxb[(b0 + 1) % 2][:], t["ctx"][b + 3]).then_inc(ctx_in[(b0 + 1) % 2], 16)
                max_rows(a_base(b) + a_index(flags, ("maxT", 1)) + 1, b0 % 2, 1)
                if shape < NB - 2:
                    sp.wait_ge(st_full, b * PAIRS + 4)
                    stack_from_dram(b0 + 2, i, 0)
                if m:
                    max_rows(a_base(b) + a_index(flags, ("maxT", 0)) + 1, (b0 + 1) % 2, 0)
                if pqk:
                    parts_to_dram(b0 + 3, i)
                if shape < NB - 2:
                    sp.wait_ge(st_full, b * PAIRS + 8)
                    stack_from_dram(b0 + 2, i, 1)

            slot(0, 0, 0)
            with sp.Fori(0, 2) as i:
                for b0 in (1, 2):
                    slot(b0, i, 1)
            slot(5, 0, 5)
            weights(["wr", "rows", "sel"] + [("wup", c) for c in range(4)])
            slot(6, 0, 6)
            weights([("wdn", c) for c in range(4)] + ["wc", "wd", "wb", "w1", "w2", "rb1"])
            slot(7, 0, 7)
            if phases <= 2:
                sp.wait_ge(misc_free, A_END)
                if phases == 2:
                    sp.wait_ge(acc_free, 3)
                sp.dma_start(out.rearrange("b p d -> p b d"), xall[:]).then_inc(out_done, 16)
                sp.wait_ge(out_done, 16)
                return

            for b in range(2):
                sp.wait_ge(misc_free, a_base(5 + b) + 1)
                sp.dma_start(ctxb[b][:], t["ctx"][b]).then_inc(ctx_in[b], 16)
            sp.wait_ge(misc_free, B_END + C_PRO.index(("cT", 0)) + 1)
            sp.dma_start(ctxb[0][:], t["ctx"][2]).then_inc(ctx_in[0], 16)
            for b in range(2):
                parts_to_dram(NB + b, 0)
                for half in range(2):
                    stack_from_dram(NB + b, 0, half)

            def slot_c(b0, i, shape):
                b = b0 + 2 * i
                o, m, t2, pqk = c_flags(shape)
                if pqk:
                    sp.wait_ge(misc_free, B_END + C_PRO.index(("cT", 1)) + 1 if shape == 0 else c_base(b))
                    sp.dma_start(ctxb[(b0 + 1) % 2][:], t["ctx"][b + 3]).then_inc(ctx_in[(b0 + 1) % 2], 16)
                if t2:
                    parts_to_dram(NB + b0 + 2, i)
                    sp.wait_ge(st_full, NB * PAIRS + b * C_STEPS + 4)
                    for half in range(2):
                        stack_from_dram(NB + b0 + 2, i, half)

            slot_c(0, 0, 0)
            with sp.Fori(0, 2) as i:
                for b0 in (1, 2):
                    slot_c(b0, i, 1)
            slot_c(5, 0, 5)

            if phases == 3:
                sp.wait_ge(misc_free, C_END)
                sp.dma_start(out.rearrange("b p d -> p b d"), xall[:]).then_inc(out_done, 16)
                sp.wait_ge(out_done, 16)
                return

            for b in range(NB):
                sp.wait_ge(misc_free, C_END + PER_D * (b // 4) + D_USES.index(("o", b % 4)) + 1)
                sp.dma_start(out[b], xall[:, b, :]).then_inc(out_done, 16)
            sp.wait_ge(out_done, 16 * NB)

        @block.tensor
        def _(pe):
            def project(par, w, bank):
                src = xn[par] if w == 0 else ctxb[par]
                for r in range(2):
                    last = nc.tensor.matmul(bank[:, r * D:(r + 1) * D], wa[:, w + r, :], src[:],
                                            start=True, stop=True)
                last.then_inc(misc_full, 1)

            def values(par, bank):
                for mb in range(2):
                    last = nc.tensor.matmul(bank[:, mb * P:(mb + 1) * P], ctxb[par][:, mb * P:(mb + 1) * P],
                                            wa[:, 4, :], start=True, stop=True)
                last.then_inc(misc_full, 1)

            def max_scores(par, pair, s, bank):
                for nb in range(2):
                    last = nc.tensor.matmul(bank[:, nb * D:(nb + 1) * D],
                                            qstk[par][:, pair, nb * P:(nb + 1) * P], kstk[par][:, s, pair, :],
                                            start=True, stop=True)
                last.then_inc(misc_full, 1)

            def max_transpose(half, bank):
                o = bank.bitcast(BF16)
                for nb in range(2):
                    last = nc.tensor.transpose(o[0:24, nb * P:(nb + 1) * P], mpart[:, half, nb, :], eye16[:])
                last.then_inc(misc_full, 1)

            def scores(b, par, k, first=False):
                if not first:
                    pe.wait_ge(exp_done, b * PAIRS + k)
                if k % 4 == 0:
                    pe.wait_ge(mrow_in[k // 4], 16 * (b + 1))
                for s in range(2):
                    for mb in range(2):
                        last = nc.tensor.matmul(exp_buf(k)[:, s, mb * D:(mb + 1) * D],
                                                kstk[par][:, s, k, mb * P:(mb + 1) * P], qstk[par][:, k, :],
                                                start=True, stop=True)
                last.then_inc(st_full, 1)

            def pv(b, par, k):
                pe.wait_ge(exp_done, b * PAIRS + k + 2)
                if k % 4 == 0:
                    pe.wait_ge(pv_free, 2 * b + 1 + k // 4)
                for s in range(2):
                    j, g = 2 * (k % 2) + s, k // 2
                    for mb in range(2):
                        last = nc.tensor.matmul(
                            pv_bank(g // 2)[32 * j:32 * j + 32, (g % 2) * D:(g % 2 + 1) * D],
                            vt[par][:, mb, 2 * k + s, :],
                            prob[k % 2][:, (2 * s + mb) * D:(2 * s + mb + 1) * D],
                            start=(mb == 0), stop=(mb == 1))
                last.then_inc(pv_done, 1)

            def output(bank):
                nc.tensor.matmul(bank[:, 0:D], wa[:, 5, :], o3[:], start=True, stop=True).then_inc(misc_full, 1)

            pe.wait_ge(w_in, 16 * 6)
            nc.tensor.matmul(misc(0)[:, 0:1], wa[:, 5, :], cols[:, 4:5], start=True, stop=True).then_inc(misc_full, 1)
            for u, (kind, b) in list(enumerate(PROLOGUE))[1:]:
                if u > 1:
                    pe.wait_ge(misc_free, u - 1)
                if kind == "q":
                    pe.wait_ge(xn_ready, b + 1)
                    project(b % 2, 0, misc(u))
                elif kind == "k":
                    pe.wait_ge(ctx_in[b % 2], 16 + 16 * (b // 2))
                    project(b % 2, 2, misc(u))
                else:
                    values(0, misc(u))
            u = len(PROLOGUE)
            pe.wait_ge(init, 2)
            for half in range(2):
                pe.wait_ge(stack_in[0][half], 48)
                for n in range(8):
                    pe.wait_ge(misc_free, u - 1)
                    max_scores(0, 4 * half + n // 2, n % 2, misc(u))
                    u += 1
            pe.wait_ge(misc_free, u - 1)
            pe.wait_ge(neg_done, 1)
            max_transpose(0, misc(u))
            scores(0, 0, 0, first=True)

            def slot(b0, i, shape):
                b = b0 + 2 * i
                wm, m, pqk = flags = a_flags(shape)
                par, other = b0 % 2, (b0 + 1) % 2
                n = 0
                for step in range(PAIRS):
                    if step < PAIRS - 1:
                        scores(b, par, step + 1)
                    elif m:
                        scores(b + 1, other, 0)
                    for use in a_uses(step, *flags):
                        pe.wait_ge(misc_free, a_base(b) + n - 1)
                        bank = misc(a_base(b0) + n)
                        if use[0] == "max":
                            if use[1] % 4 == 0 and use[2] == 0:
                                pe.wait_ge(stack_in[other][use[1] // 4], 48 * ((b0 + 1) // 2 + i + 1))
                            max_scores(other, use[1], use[2], bank)
                        elif use[0] == "q":
                            pe.wait_ge(xn_ready, b + 4)
                            project(other, 0, bank)
                        elif use[0] == "k":
                            pe.wait_ge(ctx_in[other], 16 * ((b0 + 3) // 2 + i + 1))
                            project(other, 2, bank)
                        elif use[0] == "v":
                            values(other, bank)
                        elif use[0] == "maxT":
                            pe.wait_ge(neg_done, 2 * b + (2 if use[1] else 3))
                            max_transpose(use[1], bank)
                        else:
                            pe.wait_ge(o3_ready, b)
                            output(bank)
                        n += 1
                    pv(b, par, step)

            slot(0, 0, 0)
            with pe.Fori(0, 2) as i:
                for b0 in (1, 2):
                    slot(b0, i, 1)
            for b in (5, 6, 7):
                slot(b, 0, b)
            pe.wait_ge(misc_free, A_END - 2)
            pe.wait_ge(o3_ready, NB)
            output(misc(A_END - 1))
            if phases < 2:
                return

            def transposes(blocks, bank):
                for n, blk in enumerate(blocks):
                    last = nc.tensor.transpose(bank[:, n * P:(n + 1) * P], blk, eye[:])
                last.then_inc(misc_full, 1)

            pe.wait_ge(misc_free, A_END)
            pe.wait_ge(w2_in, W2_IN)
            for n, use in enumerate(B_USES):
                u = A_END + n
                pe.wait_ge(misc_free, u - 1)
                bank = misc(u)
                if use[0] == "xT":
                    pe.wait_ge(xn_ready, NB + use[1] + 1)
                    transposes([xn[use[1] % 2][:, f * P:(f + 1) * P] for f in range(2)], bank)
                elif use[0] == "lgT":
                    if use[1] == 0:
                        pe.wait_ge(misc_free, u)
                    for f in range(2):
                        last = nc.tensor.matmul(bank[0:NE, :], wr[:, f, :],
                                                xnT[:, f, use[1] * HALF:(use[1] + 1) * HALF],
                                                start=(f == 0), stop=(f == 1))
                    last.then_inc(misc_full, 1)
                elif use[0] == "lg":
                    pe.wait_ge(misc_free, u)
                    for b in range(NB):
                        last = nc.tensor.transpose(bank[:, b * NE:(b + 1) * NE], lgT[:, b * P:(b + 1) * P],
                                                   eye[0:NE, 0:NE])
                    last.then_inc(misc_full, 1)
                else:
                    pe.wait_ge(misc_free, u)
                    for b in range(NB):
                        last = nc.tensor.transpose(bank.bitcast(BF16)[0:3 * NE, b * P:(b + 1) * P],
                                                   comb16[:, b].rearrange("p q e -> p (q e)"), eye16[:])
                    last.then_inc(misc_full, 1)
            pe.wait_ge(misc_free, B_END)

            def up(c, e):
                for f in range(2):
                    last = nc.tensor.matmul(psum[:, e % 2, :], wup[:, f, e, :],
                                            xnT[:, f, bass.ds(c * HALF, HALF)], start=(f == 0), stop=(f == 1))
                if e < NE:
                    last = nc.tensor.matmul(psum[:, 2 + e % 2, :], sel[:, e, :], combT[:, bass.ds(c * HALF, HALF)],
                                            start=True, stop=True)
                last.then_inc(h_full, 1)

            def down(c, e):
                pe.wait_ge(a_done, c * NCH + e + 1)
                if e == 0:
                    pe.wait_ge(acc_free, c + 1)
                for j in range(4):
                    last = nc.tensor.matmul(psum[:, 6 + j // 2, (j % 2) * D:(j % 2 + 1) * D],
                                            act2[e % 2][:, j * P:(j + 1) * P], wdn[:, e, :],
                                            start=(e == 0 and j % 2 == 0), stop=(e == NCH - 1),
                                            skip_group_check=True)
                if e == NCH - 1:
                    last.then_inc(acc_full, 1)

            with pe.Fori(0, 2) as c:
                up(c, 0)
                for e in range(NCH):
                    if e + 1 < NCH:
                        up(c, e + 1)
                    down(c, e)
            if phases < 3:
                return

            def c_use(kind, b, par, bank, u):
                if kind == "xT":
                    pe.wait_ge(xn_ready, 2 * NB + b + 1)
                    transposes([xn[par][:, f * P:(f + 1) * P] for f in range(2)], bank)
                elif kind == "cT":
                    transposes([ctxb[par][:, f * P:(f + 1) * P] for f in range(2)], bank)
                elif kind == "qk":
                    pe.wait_ge(misc_free, u)
                    for ten, src in enumerate((xT1, ctxT[par])):
                        for f in range(2):
                            last = nc.tensor.matmul(bank[:, ten * D:(ten + 1) * D], src[:, f, :],
                                                    wc[:, f, ten * D:(ten + 1) * D], start=(f == 0), stop=(f == 1))
                    last.then_inc(misc_full, 1)
                elif kind == "qkT":
                    transposes([qkn[:, ten, f * P:(f + 1) * P] for ten in range(2) for f in range(2)], bank)
                elif kind == "v":
                    for f in range(2):
                        last = nc.tensor.matmul(bank[:, 0:D], ctxT[par][:, f, :], wc[:, f, 2 * D:3 * D],
                                                start=(f == 0), stop=(f == 1))
                    last.then_inc(misc_full, 1)
                else:
                    pe.wait_ge(o3_ready, NB + b + 1)
                    transposes([o3[:, f * P:(f + 1) * P] for f in range(2)], bank)

            def scores_c(b, par, k, first=False):
                if not first:
                    pe.wait_ge(exp_done, NB * PAIRS + b * C_STEPS + k)
                buf = exp_buf(k).rearrange("p a n -> p (a n)")
                for pp in range(2):
                    for ch in range(2):
                        for s in range(2):
                            h = 4 * pp + 2 * ch + s
                            last = nc.tensor.matmul(buf[:, h * P:(h + 1) * P],
                                                    kstk[par][:, s, 2 * k + pp, ch * P:(ch + 1) * P],
                                                    qstk[par][:, 2 * k + pp, ch * P:(ch + 1) * P],
                                                    start=True, stop=True)
                last.then_inc(st_full, 1)

            def pv_c(b, par, k):
                pe.wait_ge(exp_done, NB * PAIRS + b * C_STEPS + k + 2)
                if k % 2 == 0:
                    pe.wait_ge(pv_free, 2 * NB + 2 * b + k // 2 + 1)
                v = vt[par][:].rearrange("m a h r -> m (a h) r")
                for pp in range(2):
                    for j in range(4):
                        h = 4 * pp + j
                        g = 2 * (k % 2) + pp
                        last = nc.tensor.matmul(pv_bank(k // 2)[32 * j:32 * j + 32, g * P:(g + 1) * P],
                                                v[:, 8 * k + h, :], prob[k % 2][:, h * P:(h + 1) * P],
                                                start=True, stop=True)
                last.then_inc(pv_done, 1)

            for n, (kind, b) in enumerate(C_PRO):
                u = B_END + n
                pe.wait_ge(misc_free, u if kind == "qkT" else u - 1)
                if kind == "cT":
                    pe.wait_ge(ctx_in[b % 2], 16 * (5 + b // 2))
                c_use(kind, b, b % 2, misc(u), u)
            for half in range(2):
                pe.wait_ge(stack_in[0][half], 48 * 5)
            scores_c(0, 0, 0)

            def slot_c(b0, i, shape):
                b = b0 + 2 * i
                o, m, t2, pqk = flags = c_flags(shape)
                n = 0
                for step in range(C_STEPS):
                    if step < C_STEPS - 1:
                        scores_c(b, b0 % 2, step + 1)
                    elif m:
                        for half in range(2):
                            pe.wait_ge(stack_in[(b0 + 1) % 2][half], 48 * ((b0 + 1) // 2 + i + 5))
                        scores_c(b + 1, (b0 + 1) % 2, 0)
                    for (kind,) in c_uses(step, *flags):
                        u = c_base(b) + n
                        pe.wait_ge(misc_free, u - 1)
                        if kind == "cT":
                            pe.wait_ge(ctx_in[(b0 + 1) % 2], 16 * ((b0 + 3) // 2 + i + 5))
                        c_use(kind, b + AHEAD[kind], (b0 + AHEAD[kind]) % 2, misc(c_base(b0) + n), u)
                        n += 1
                    pv_c(b, b0 % 2, step)

            slot_c(0, 0, 0)
            with pe.Fori(0, 2) as i:
                for b0 in (1, 2):
                    slot_c(b0, i, 1)
            for b in (5, 6, 7):
                slot_c(b, 0, b)
            pe.wait_ge(misc_free, C_END - 2)
            c_use("o", NB - 1, 1, misc(C_END - 1), C_END - 1)
            if phases < 4:
                return

            pe.wait_ge(misc_free, C_END)
            with pe.Fori(0, 2) as c:
                for n, (kind, j) in enumerate(D_USES):
                    u = C_END + c * PER_D + n
                    pe.wait_ge(misc_free, u - D_RING + 1)
                    bank = psum[:, n % D_RING, :]
                    mine = xnT[:, :, j * P:(j + 1) * P]
                    if kind == "xT":
                        pe.wait_ge(xn_ready, 3 * NB + 4 * c + j + 1)
                        transposes([xn[j % 2][:, f * P:(f + 1) * P] for f in range(2)], bank)
                    elif kind == "h":
                        pe.wait_ge(misc_free, u)
                        for f in range(2):
                            last = nc.tensor.matmul(bank[0:RH, :], w1[:, f, :], xnT[:, f, 0:HALF],
                                                    start=(f == 0), stop=(f == 1))
                        last.then_inc(misc_full, 1)
                    elif kind == "lg":
                        pe.wait_ge(misc_free, u)
                        for q in range(4):
                            last = nc.tensor.matmul(bank[:, q * NE:(q + 1) * NE], eh[:, q * P:(q + 1) * P], w2[:],
                                                    start=True, stop=True)
                        last.then_inc(misc_full, 1)
                    elif kind == "xa":
                        for f in range(2):
                            last = nc.tensor.matmul(bank[:, 0:D], mine[:, f, :], wd[:, f, D:2 * D],
                                                    start=(f == 0), stop=(f == 1))
                        last.then_inc(misc_full, 1)
                    elif kind == "wT":
                        pe.wait_ge(misc_free, C_END + c * PER_D + D_USES.index(("xa", j)) + 1)
                        transposes([wxa[j][:, f * P:(f + 1) * P] for f in range(2)], bank)
                    else:
                        for f in range(2):
                            nc.tensor.matmul(bank[:, 0:D], mine[:, f, :], wd[:, f, 0:D], start=(f == 0), stop=False)
                        pe.wait_ge(misc_free, C_END + c * PER_D + D_USES.index(("wT", j)) + 1)
                        for f in range(2):
                            last = nc.tensor.matmul(bank[:, 0:D], wxaT[j % 2][:, f, :], wb[:, f, :],
                                                    start=False, stop=(f == 1))
                        last.then_inc(misc_full, 1)

        @block.scalar
        def _(act):
            def exps(b, k):
                act.wait_ge(st_full, b * PAIRS + k + 1)
                nc.scalar.activation(prob[k % 2][:], exp_buf(k).rearrange("p a n -> p (a n)"), ACT.Exp,
                                     scale=SCALE).then_inc(exp_done, 1)

            def first_parts(b, par, gone):
                act.wait_ge(qk_ready, b + 2)
                if gone is not None:
                    act.wait_ge(parts_out[par], gone * 96)
                nc.scalar.copy(parts[par][:, :, 0, :], qk[:]).then_inc(hi_done, 1)

            def second_parts(b, par):
                act.wait_ge(rest_done, b + 1)
                nc.scalar.copy(parts[par][:, :, 1, :], qk_rest[:]).then_inc(mid_done, 1)

            act.dma_start(eye[:], t["eye"]).then_inc(w_in, 16)
            act.drain().then_inc(exp_done, 1)
            for b in range(3):
                first_parts(b, b % 2, 1 if b == 2 else None)
                second_parts(b, b % 2)

            def slot(b0, i, shape):
                b = b0 + 2 * i
                wm, m, pqk = a_flags(shape)
                for k in range(PAIRS):
                    exps(b, k)
                    if pqk and k == 5:
                        first_parts(b + 3, (b0 + 1) % 2, (b0 + 3) // 2 + i)
                    if pqk and k == 6:
                        second_parts(b + 3, (b0 + 1) % 2)

            slot(0, 0, 0)
            with act.Fori(0, 2) as i:
                for b0 in (1, 2):
                    slot(b0, i, 1)
            for b in (5, 6, 7):
                slot(b, 0, b)
            if phases < 2:
                return

            act.wait_ge(misc_full, A_END + B_USES.index(("lg",)) + 1)
            nc.scalar.activation(sc[:].rearrange("p b e -> p (b e)"), misc(A_END + B_USES.index(("lg",)))[:, 0:NB * NE],
                                 ACT.Exp, scale=-1.0).then_inc(sig_ready, 1)
            with act.Fori(0, 2) as c:
                for e in range(NCH):
                    act.wait_ge(h_full, c * NCH + e + 1)
                    nc.scalar.activation(rel[e % 2][:], psum[:, e % 2, :], ACT.Relu).then_inc(relu_done, 1)
            if phases < 3:
                return

            def squares(b, u, bank):
                act.wait_ge(misc_full, u + 1)
                nc.scalar.activation(sq[:], bank, ACT.Square).then_inc(sq_done, 1)

            def first_parts_c(u, bank, par, gone):
                act.wait_ge(misc_full, u + 1)
                act.wait_ge(parts_out[par], gone * 96)
                nc.scalar.copy(parts[par][:, :, 0, :], bank.rearrange("p (t n) -> p t n", t=2)).then_inc(hi_done, 1)

            def second_parts_c(u, par):
                act.wait_ge(misc_free, u + 1)
                nc.scalar.copy(parts[par][:, :, 1, :], qk_rest[:]).then_inc(mid_done, 1)

            for b in range(3):
                u = B_END + C_PRO.index(("qk", b))
                squares(b, u, misc(u))
                if b < 2:
                    first_parts_c(u + 1, misc(u + 1), b % 2, 4 + b // 2)
                    second_parts_c(u + 1, b % 2)

            def slot_c(b0, i, shape):
                b = b0 + 2 * i
                o, m, t2, pqk = flags = c_flags(shape)
                for k in range(C_STEPS):
                    act.wait_ge(st_full, NB * PAIRS + b * C_STEPS + k + 1)
                    nc.scalar.activation(prob[k % 2][:], exp_buf(k).rearrange("p a n -> p (a n)"), ACT.Exp,
                                         scale=SCALE).then_inc(exp_done, 1)
                    if t2 and k == 1:
                        n = c_index(flags, ("qkT",))
                        first_parts_c(c_base(b) + n, misc(c_base(b0) + n), b0 % 2, (b0 + 2) // 2 + i + 4)
                    if t2 and k == 2:
                        second_parts_c(c_base(b) + c_index(flags, ("qkT",)), b0 % 2)
                    if pqk and k == 3:
                        n = c_index(flags, ("qk",))
                        squares(b + 3, c_base(b) + n, misc(c_base(b0) + n))

            slot_c(0, 0, 0)
            with act.Fori(0, 2) as i:
                for b0 in (1, 2):
                    slot_c(b0, i, 1)
            for b in (5, 6, 7):
                slot_c(b, 0, b)
            if phases < 4:
                return

            with act.Fori(0, 2) as c:
                n = D_USES.index(("h", 0))
                act.wait_ge(misc_full, C_END + c * PER_D + n + 1)
                nc.scalar.activation(eh[:], psum[0:RH, n % D_RING, :], ACT.Exp, bias=nrb1[:, 1:2], scale=-1.0
                                     ).then_inc(eh_done, 1)
                act.wait_ge(gap_done, c + 1)
                nc.scalar.activation(top_i[:, 0:4], top_i[:, 0:4], ACT.Exp).then_inc(egap_done, 1)

        @block.gpsimd
        def _(pool):
            steps = Steps(pool, pool_step)
            for i in range(2):
                nc.gpsimd.memset(kstk[i][:].bitcast(F32), 0.0).then_inc(init, 1)

            def rotate(ready):
                pool.wait_ge(misc_free, ready)
                nc.gpsimd.tensor_tensor(qk[:], rope_ab[:, 0], rope_ab[:, 1], ALU.add).then_inc(qk_ready, 1)

            def rest(b, par):
                pool.wait_ge(hi_done, b + 1)
                nc.gpsimd.tensor_tensor(qk_rest[:], qk[:], parts[par][:, :, 0, :], ALU.subtract
                                        ).then_inc(rest_done, 1)

            def third(b, par):
                pool.wait_ge(mid_done, b + 1)
                nc.gpsimd.tensor_tensor(parts[par][:, :, 2, :], qk_rest[:], parts[par][:, :, 1, :],
                                        ALU.subtract).then_inc(lo_done, 1)

            def negate(ready, half):
                pool.wait_ge(misc_free, ready)
                part = mpart[:, half].rearrange("n b (s q p) -> n b s q p", s=2, q=3)
                m = mneg[:, half].rearrange("n b (s p) -> n b s p", s=2)
                zero = zeros[:, 0].rearrange("n (s p) -> n s p", s=2)
                steps.then(nc.gpsimd.tensor_tensor(mneg[:, half], zeros[:], mx[:, half], ALU.subtract))
                for q in range(2):
                    for nb in range(2):
                        last = nc.gpsimd.tensor_tensor(part[:, nb, :, q, :], m[:, nb], zero, ALU.add)
                        if nb:
                            steps.then(last)
                    for nb in range(2):
                        last = nc.gpsimd.tensor_tensor(m[:, nb], m[:, nb], part[:, nb, :, q, :], ALU.subtract)
                        if nb:
                            steps.then(last)
                for nb in range(2):
                    last = nc.gpsimd.tensor_tensor(part[:, nb, :, 2, :], m[:, nb], zero, ALU.add)
                last.then_inc(neg_done, 1)

            nc.gpsimd.memset(zeros[:], 0.0).then_inc(init, 1)
            pool.wait_ge(init, 3)
            nc.gpsimd.drain().then_inc(qk_ready, 1)
            for b in range(3):
                rotate(PROLOGUE.index(("q", b)) + 1)
                rest(b, b % 2)
                third(b, b % 2)
            for half in range(2):
                negate(len(PROLOGUE) + 8 * (half + 1), half)

            def slot(b0, i, shape):
                b = b0 + 2 * i
                wm, m, pqk = flags = a_flags(shape)
                if m:
                    negate(a_base(b) + a_index(flags, ("max", 3, 1)) + 1, 0)
                if pqk:
                    rotate(a_base(b) + a_index(flags, ("k",)) + 1)
                    rest(b + 3, (b0 + 1) % 2)
                    third(b + 3, (b0 + 1) % 2)
                if m:
                    negate(a_base(b) + a_index(flags, ("max", 7, 1)) + 1, 1)

            slot(0, 0, 0)
            with pool.Fori(0, 2) as i:
                steps.enter(i, 2 * 2 * 5)
                for b0 in (1, 2):
                    slot(b0, i, 1)
            steps.leave(2)
            for b in (5, 6):
                slot(b, 0, b)
            if phases < 3:
                return

            with pool.Fori(0, 4) as i:
                for par in range(2):
                    third(NB + 2 * i + par, par)

        @block.vector
        def _(dve):
            steps = Steps(dve, dve_step)

            def rsqrt(o, var, scale, eps, n):
                v, a = rs_v[:, 0:n], rs_a[:, 0:n]
                steps.then(nc.vector.tensor_scalar(v, var, scale, eps, ALU.mult, ALU.add))
                steps.then(nc.vector.tensor_scalar(a.bitcast(I32), v.bitcast(I32), 1, None,
                                                   ALU.logical_shift_right))
                steps.then(nc.vector.tensor_scalar(o.bitcast(I32), a.bitcast(I32), -1.0, float(RSQRT_GUESS),
                                                   ALU.mult, ALU.add))
                for _ in range(3):
                    steps.then(nc.vector.tensor_tensor(a, o, v, ALU.mult))
                    steps.then(nc.vector.scalar_tensor_tensor(out=a, in0=a, scalar=-0.5, in1=o,
                                                              op0=ALU.mult, op1=ALU.mult))
                    steps.then(nc.vector.scalar_tensor_tensor(out=o, in0=a, scalar=1.5, in1=o,
                                                              op0=ALU.add, op1=ALU.mult))

            def rows_of(b):
                return xall[:, b, :] if isinstance(b, int) else xall[:, bass.ds(b, 1), :].rearrange("p o n -> p (o n)")

            def norm_stats():
                for b in range(NB):
                    last = nc.vector.bn_stats(stats[:, b, :], xall[:, b, :])
                steps.then(last)
                for b in range(NB):
                    last = nc.vector.bn_aggr(mv[:, b, :], stats[:, b, :])
                steps.then(last)
                rsqrt(rstd[:], mv[:, :, 1], 1.0, LN_EPS, NB)

            def normalize(b, par):
                nc.vector.tensor_scalar(xn[par][:], xall[:, b, :], mv[:, b, 0:1], rstd[:, b:b + 1] if isinstance(b, int)
                                        else rstd[:, bass.ds(b, 1)], ALU.subtract, ALU.mult).then_inc(xn_ready, 1)

            def factors(ten, bank):
                for r in range(2):
                    last = nc.vector.scalar_tensor_tensor(
                        out=rope_ab[:, r, ten, :], in0=bank[:, r * D:(r + 1) * D],
                        scalar=cols[:, 2 * ten + r:2 * ten + r + 1], in1=rope[:, r, :], op0=ALU.add, op1=ALU.mult)
                last.then_inc(misc_free, 1)

            def take_values(par, bank):
                nc.vector.tensor_copy(vt[par][:, :, :, 0:HD],
                                      bank[:, 0:D].rearrange("m (a h d) -> m a h d", a=2, d=HD)).then_inc(misc_free, 1)

            def row_max(pair, s, bank):
                half, p4 = pair // 4, pair % 4
                nc.vector.tensor_reduce(mx[:, half, :, 4 * s + p4:4 * s + p4 + 1],
                                        bank.rearrange("n (b m) -> n b m", b=2), AX_X, ALU.max).then_inc(misc_free, 1)

            def take_maxT(half, bank):
                nc.vector.tensor_copy(mT[:, half, :], bank.bitcast(BF16)[0:24, 0:D]).then_inc(misc_free, 1)

            def add_output(b, bank):
                xb = rows_of(b)
                nc.vector.scalar_tensor_tensor(out=xb, in0=bank[:, 0:D], scalar=cb[:], in1=xb,
                                               op0=ALU.add, op1=ALU.add).then_inc(misc_free, 1)

            def divide(b, i):
                dve.wait_ge(pv_done, b * PAIRS + 4 * (i + 1))
                ins = nc.vector.transpose(pvT[i][:], pv_bank(i))
                ins.then_inc(pv_free, 1)
                dve.wait_ge(pv_free, 2 * b + i + 3)
                cells = pvT[i][:].rearrange("p (x r) -> p x r", r=32)
                steps.then(nc.vector.reciprocal(den[i][:], cells[:, :, HD]))
                o = o2[:].rearrange("p (n g d) -> p g n d", g=4, d=HD)
                for g in range(2):
                    last = nc.vector.tensor_tensor(
                        o[:, 2 * i + g], cells[:, 8 * g:8 * g + 8, 0:HD],
                        den[i][:, 8 * g:8 * g + 8].unsqueeze(2).broadcast_to((P, 8, HD)), ALU.mult)
                steps.then(last)
                if i == 1:
                    nc.vector.transpose(o3[:], o2[:]).then_inc(o3_ready, 1)

            for i in range(2):
                steps.then(nc.vector.memset(vt[i][:], 0.0))
                last = nc.vector.memset(vt[i][:, :, :, HD:HD + 1], 1.0)
                last.then_inc(pv_free, 1)
            dve.wait_ge(x_in, 16)
            norm_stats()
            dve.wait_ge(w_in, 16 * 6)
            nc.vector.memset(fill[:, 0], 0.0)
            nc.vector.memset(fill[:, 1, 1], 0.0)
            nc.vector.tensor_copy(fill[:, 1, 0], cols[:, 7:8].broadcast_to((P, D))).then_inc(fill_set, 1)
            steps.then(nc.vector.tensor_scalar(rope[:, 1, :], rope_in[:], cols[:, 6:7], None, ALU.mult))
            for b in range(2):
                normalize(b, b)
            for u, (kind, b) in enumerate(PROLOGUE):
                if (kind, b) == ("k", 2):
                    normalize(2, 0)
                dve.wait_ge(misc_full, u + 1)
                if kind == "cb":
                    nc.vector.tensor_scalar(cb[:], misc(u)[:, 0:1], cols[:, 5:6], None, ALU.add).then_inc(misc_free, 1)
                elif kind == "v":
                    take_values(0, misc(u))
                else:
                    if b and kind == "k":
                        dve.wait_ge(qk_ready, b + 1)
                    factors(int(kind == "k"), misc(u))
            u = len(PROLOGUE)
            for n in range(2 * PAIRS):
                dve.wait_ge(misc_full, u + 1)
                row_max(n // 2, n % 2, misc(u))
                u += 1
            dve.wait_ge(misc_full, u + 1)
            take_maxT(0, misc(u))

            def slot(b0, i, shape):
                b = b0 + 2 * i
                wm, m, pqk = flags = a_flags(shape)
                if pqk:
                    normalize(b + 3, (b0 + 1) % 2)
                n = 0
                for step in range(PAIRS):
                    for use in a_uses(step, *flags):
                        dve.wait_ge(misc_full, a_base(b) + n + 1)
                        bank = misc(a_base(b0) + n)
                        if use[0] == "max":
                            if use[1] % 4 == 0 and use[2] == 0:
                                dve.wait_ge(neg_done, 2 * b + use[1] // 4 + 1)
                            row_max(use[1], use[2], bank)
                        elif use[0] == "q":
                            dve.wait_ge(qk_ready, b + 4)
                            factors(0, bank)
                        elif use[0] == "k":
                            factors(1, bank)
                        elif use[0] == "v":
                            if shape:
                                dve.wait_ge(pv_done, b * PAIRS)
                            take_values((b0 + 1) % 2, bank)
                        elif use[0] == "maxT":
                            if use[1] == 0 or shape:
                                dve.wait_ge(mrow_in[use[1]], 16 * b + (0 if use[1] else 16))
                            take_maxT(use[1], bank)
                        else:
                            add_output(b - 1, bank)
                        n += 1
                    if step == 0 and wm:
                        divide(b - 1, 1)
                    if step == 4:
                        divide(b, 0)

            slot(0, 0, 0)
            with dve.Fori(0, 2) as i:
                steps.enter(i, 8)
                for b0 in (1, 2):
                    slot(b0, i, 1)
            steps.leave(2)
            for b in (5, 6, 7):
                slot(b, 0, b)
            divide(NB - 1, 1)
            dve.wait_ge(misc_full, A_END)
            add_output(NB - 1, misc(A_END - 1))
            if phases < 2:
                return

            def spread(small, big, n):
                return small.unsqueeze(2).broadcast_to((P, big, n))

            def pick(hot_o, peak, v, groups, n):
                num = rows[:, 3 * NE:3 * NE + n] if n == NE else rows[:, 4 * NE - n:4 * NE]
                num = num.unsqueeze(1).broadcast_to((P, groups, n))
                th = hot_t[:].rearrange("p b e -> p (b e)")[:, 0:groups * n].rearrange("p (b e) -> p b e", e=n)
                low = top_i[:, 0:groups]
                steps.then(nc.vector.tensor_reduce(peak.unsqueeze(2), v, AX_X, ALU.max))
                steps.then(nc.vector.tensor_tensor(th, v, spread(peak, groups, n), ALU.is_equal))
                steps.then(nc.vector.tensor_tensor(th, th, num, ALU.mult))
                steps.then(nc.vector.tensor_reduce(low.unsqueeze(2), th, AX_X, ALU.min))
                steps.then(nc.vector.tensor_tensor(hot_o, num, spread(low, groups, n), ALU.is_equal))

            def drop(v, hot_i):
                steps.then(nc.vector.scalar_tensor_tensor(out=v, in0=hot_i, scalar=-3.0e38, in1=v,
                                                          op0=ALU.mult, op1=ALU.add))

            dve.wait_ge(misc_free, A_END)
            norm_stats()
            dve.wait_ge(w2_in, W2_IN)
            lg_u = A_END + B_USES.index(("lg",))
            for b in range(2):
                normalize(b, b)
            for n, use in enumerate(B_USES):
                u = A_END + n
                dve.wait_ge(misc_full, u + 1)
                bank = misc(u)
                if use[0] == "xT":
                    b = use[1]
                    nc.vector.tensor_copy(xnT[:, :, b * P:(b + 1) * P], bank[:, 0:D].rearrange("p (f n) -> p f n", f=2)
                                          ).then_inc(misc_free, 1)
                    if b + 2 < NB:
                        normalize(b + 2, b % 2)
                elif use[0] == "lgT":
                    nc.vector.tensor_copy(lgT[:, use[1] * HALF:(use[1] + 1) * HALF], bank[0:NE, :]
                                          ).then_inc(misc_free, 1)
                elif use[0] == "lg":
                    dve.wait_ge(sig_ready, 1)
                    steps.then(nc.vector.tensor_scalar(sc[:], sc[:], 1.0, None, ALU.add))
                    steps.then(nc.vector.reciprocal(sc[:], sc[:]))
                    steps.then(nc.vector.tensor_tensor(sel_s[:], sc[:], rows[:, 0:NE].unsqueeze(1).broadcast_to(
                        (P, NB, NE)), ALU.add))
                    s4 = sel_s[:].rearrange("p b (g e) -> p (b g) e", g=4)
                    nc.vector.tensor_tensor(pair_sum[:, :, 0:3], s4[:, :, 0:3], s4[:, :, 1:4], ALU.add)
                    nc.vector.tensor_tensor(pair_sum[:, :, 3:5], s4[:, :, 0:2], s4[:, :, 2:4], ALU.add)
                    steps.then(nc.vector.tensor_tensor(pair_sum[:, :, 5:6], s4[:, :, 0:1], s4[:, :, 3:4], ALU.add))
                    steps.then(nc.vector.tensor_reduce(gsum[:].rearrange("p b g -> p (b g)").unsqueeze(2),
                                                       pair_sum[:], AX_X, ALU.max))
                    g4 = [h[:].rearrange("p b e -> p (b e)")[:, 0:NB * 4].rearrange("p (b g) -> p b g", g=4)
                          for h in hot]
                    pick(g4[0], top[0][:], gsum[:], NB, 4)
                    drop(gsum[:], g4[0])
                    pick(g4[1], top[0][:], gsum[:], NB, 4)
                    steps.then(nc.vector.tensor_tensor(gsum[:], g4[0], g4[1], ALU.add))
                    steps.then(nc.vector.tensor_tensor(
                        s4, s4, spread(gsum[:].rearrange("p b g -> p (b g)"), NB * 4, 4), ALU.mult))
                    pick(hot[0][:], top[0][:], sel_s[:], NB, NE)
                    drop(sel_s[:], hot[0][:])
                    pick(hot[1][:], top[0][:], sel_s[:], NB, NE)
                    steps.then(nc.vector.tensor_tensor(comb[:], hot[0][:], hot[1][:], ALU.add))
                    steps.then(nc.vector.tensor_tensor(comb[:], comb[:], sc[:], ALU.mult))
                    steps.then(nc.vector.tensor_reduce(top[0][:].unsqueeze(2), comb[:], AX_X, ALU.add))
                    steps.then(nc.vector.tensor_scalar(top[0][:], top[0][:], 1e-20, None, ALU.add))
                    steps.then(nc.vector.reciprocal(top[1][:], top[0][:]))
                    steps.then(nc.vector.tensor_tensor(comb[:], comb[:], spread(top[1][:], NB, NE), ALU.mult))
                    for q in range(2):
                        steps.then(nc.vector.tensor_copy(comb16[:, :, q, :], comb[:]))
                        steps.then(nc.vector.tensor_tensor(comb[:], comb[:], comb16[:, :, q, :], ALU.subtract))
                    nc.vector.tensor_copy(comb16[:, :, 2, :], comb[:]).then_inc(misc_free, 1)
                else:
                    nc.vector.tensor_copy(combT[:], bank.bitcast(BF16)[0:3 * NE, :]).then_inc(misc_free, 1)

            dve.drain().then_inc(acc_free, 1)
            with dve.Fori(0, 2) as c:
                steps.enter(c, NE)
                for e in range(NCH):
                    dve.wait_ge(relu_done, c * NCH + e + 1)
                    r = rel[e % 2][:]
                    if e:
                        dve.wait_ge(a_done, c * NCH + e)
                    if e < NE:
                        steps.then(nc.vector.tensor_tensor(wrel[:], psum[:, 2 + e % 2, :], r, ALU.mult))
                    nc.vector.tensor_tensor(act2[e % 2][:], wrel[:] if e < NE else r, r, ALU.mult).then_inc(a_done, 1)
                dve.wait_ge(acc_full, c + 1)
                for j in range(4):
                    xb = xall[:, bass.ds(4 * c + j, 1), :].rearrange("p o n -> p (o n)")
                    last = nc.vector.tensor_tensor(xb, psum[:, 6 + j // 2, (j % 2) * D:(j % 2 + 1) * D], xb, ALU.add)
                last.then_inc(acc_free, 1)
            steps.leave(2)
            if phases < 3:
                return

            dve.wait_ge(acc_free, 3)
            norm_stats()
            for b in range(2):
                normalize(b, b)

            def c_use(kind, par, bank, b):
                if kind == "xT":
                    nc.vector.tensor_copy(xT1[:], bank[:, 0:D].rearrange("p (f n) -> p f n", f=2)
                                          ).then_inc(misc_free, 1)
                elif kind == "cT":
                    nc.vector.tensor_copy(ctxT[par][:], bank[:, 0:D].rearrange("p (f n) -> p f n", f=2)
                                          ).then_inc(misc_free, 1)
                elif kind == "qk":
                    dve.wait_ge(sq_done, b + 1)
                    steps.then(nc.vector.tensor_reduce(
                        ss[:].unsqueeze(2), sq[:].rearrange("n (h d) -> n h d", d=HD), AX_X, ALU.add))
                    rsqrt(rs[:], ss[:], 1.0 / HD, RMS_EPS, 64)
                    for ten in range(2):
                        last = nc.vector.tensor_tensor(
                            qkn[:, ten].rearrange("n (h d) -> n h d", d=HD),
                            bank[:, ten * D:(ten + 1) * D].rearrange("n (h d) -> n h d", d=HD),
                            rs[:, 32 * ten:32 * ten + 32].unsqueeze(2).broadcast_to((P, 32, HD)), ALU.mult)
                    last.then_inc(misc_free, 1)
                elif kind == "qkT":
                    dve.wait_ge(hi_done, NB + b + 1)
                    dve.wait_ge(lo_done, NB + b)
                    nc.vector.tensor_tensor(qk_rest[:], bank.rearrange("p (t n) -> p t n", t=2),
                                            parts[par][:, :, 0, :], ALU.subtract).then_inc(misc_free, 1)
                elif kind == "v":
                    nc.vector.tensor_copy(vt[par][:].rearrange("m a h r -> m (a h) r")[:, :, 0:HD],
                                          bank[:, 0:D].rearrange("m (h d) -> m h d", d=HD)).then_inc(misc_free, 1)
                else:
                    nc.vector.tensor_tensor(rows_of(b), bank[:, 0:D], rows_of(b), ALU.add).then_inc(misc_free, 1)

            def divide_c(b, i):
                dve.wait_ge(pv_done, NB * PAIRS + b * C_STEPS + 2 * (i + 1))
                nc.vector.transpose(pvT[i][:], pv_bank(i)).then_inc(pv_free, 1)
                dve.wait_ge(pv_free, 2 * NB + 2 * b + i + 3)
                cells = pvT[i][:].rearrange("p (x r) -> p x r", r=32)
                steps.then(nc.vector.reciprocal(den[i][:], cells[:, :, HD]))
                steps.then(nc.vector.tensor_tensor(
                    o2[:, i * P:(i + 1) * P].rearrange("p (n g d) -> p g n d", n=4, d=HD),
                    cells[:, :, 0:HD].rearrange("p (g n) d -> p g n d", g=4),
                    den[i][:].rearrange("p (g n) -> p g n", g=4).unsqueeze(3).broadcast_to((P, 4, 4, HD)), ALU.mult))
                if i == 1:
                    nc.vector.transpose(o3[:], o2[:]).then_inc(o3_ready, 1)

            for n, (kind, b) in enumerate(C_PRO):
                if (kind, b) == ("xT", 2):
                    normalize(2, 0)
                dve.wait_ge(misc_full, B_END + n + 1)
                c_use(kind, b % 2, misc(B_END + n), b)

            def slot_c(b0, i, shape):
                b = b0 + 2 * i
                o, m, t2, pqk = flags = c_flags(shape)
                if pqk:
                    normalize(b + 3, (b0 + 1) % 2)
                n = 0
                for step in range(C_STEPS):
                    for (kind,) in c_uses(step, *flags):
                        dve.wait_ge(misc_full, c_base(b) + n + 1)
                        if kind == "v" and shape:
                            dve.wait_ge(pv_done, NB * PAIRS + b * C_STEPS)
                        c_use(kind, (b0 + AHEAD[kind]) % 2, misc(c_base(b0) + n), b + AHEAD[kind])
                        n += 1
                    if step == 0 and o:
                        divide_c(b - 1, 1)
                    if step == 2:
                        divide_c(b, 0)

            slot_c(0, 0, 0)
            with dve.Fori(0, 2) as i:
                steps.enter(i, 2 * (1 + 12 + 4))
                for b0 in (1, 2):
                    slot_c(b0, i, 1)
            steps.leave(2)
            for b in (5, 6, 7):
                slot_c(b, 0, b)
            divide_c(NB - 1, 1)
            dve.wait_ge(misc_full, C_END)
            c_use("o", 1, misc(C_END - 1), NB - 1)
            if phases < 4:
                return

            dve.wait_ge(misc_free, C_END)
            norm_stats()
            steps.then(nc.vector.tensor_scalar(nrb1[:, 1:2], nrb1[:, 0:1], -1.0, None, ALU.mult))
            with dve.Fori(0, 2) as c:
                steps.enter(c, 24)
                for j in range(2):
                    normalize(4 * c + j, j)
                for n, (kind, j) in enumerate(D_USES):
                    dve.wait_ge(misc_full, C_END + c * PER_D + n + 1)
                    bank = psum[:, n % D_RING, :]
                    if kind == "xT":
                        nc.vector.tensor_copy(xnT[:, :, j * P:(j + 1) * P],
                                              bank[:, 0:D].rearrange("p (f n) -> p f n", f=2)).then_inc(misc_free, 1)
                        if j < 2:
                            normalize(4 * c + j + 2, j)
                    elif kind == "h":
                        dve.wait_ge(eh_done, c + 1)
                        nc.vector.tensor_scalar(zh[:], bank[0:RH, :], nrb1[:, 0:1], None, ALU.add)
                        steps.then(nc.vector.tensor_scalar(eh[:], eh[:], 1.0, None, ALU.add))
                        steps.then(nc.vector.reciprocal(eh[:], eh[:]))
                        nc.vector.tensor_tensor(eh[:], eh[:], zh[:], ALU.mult).then_inc(misc_free, 1)
                    elif kind == "lg":
                        lg = sel_s[:, 0:4, :]
                        h0, h1 = hot[0][:, 0:4, :], hot[1][:, 0:4, :]
                        for q in range(2):
                            row = rows[:, (q + 1) * NE:(q + 2) * NE].unsqueeze(1).broadcast_to((P, 4, NE))
                            src = bank[:, 0:4 * NE].rearrange("p (b e) -> p b e", e=NE) if q == 0 else lg
                            steps.then(nc.vector.tensor_tensor(lg, src, row, ALU.add))
                        pick(h0, top[0][:, 0:4], lg, 4, NE)
                        drop(lg, h0)
                        pick(h1, top[1][:, 0:4], lg, 4, NE)
                        nc.vector.tensor_tensor(top_i[:, 0:4], top[1][:, 0:4], top[0][:, 0:4], ALU.subtract
                                                ).then_inc(gap_done, 1)
                        dve.wait_ge(egap_done, c + 1)
                        steps.then(nc.vector.tensor_scalar(top[0][:, 0:4], top_i[:, 0:4], 1.0, None, ALU.add))
                        steps.then(nc.vector.reciprocal(top[0][:, 0:4], top[0][:, 0:4]))
                        steps.then(nc.vector.tensor_tensor(top[1][:, 0:4], top_i[:, 0:4], top[0][:, 0:4], ALU.mult))
                        steps.then(nc.vector.tensor_tensor(h0, h0, spread(top[0][:, 0:4], 4, NE), ALU.mult))
                        steps.then(nc.vector.tensor_tensor(h1, h1, spread(top[1][:, 0:4], 4, NE), ALU.mult))
                        nc.vector.tensor_tensor(comb[:, 0:4, :], h0, h1, ALU.add).then_inc(misc_free, 1)
                        dve.wait_ge(misc_free, C_END + c * PER_D + n + 1)
                    elif kind == "xa":
                        nc.vector.tensor_tensor(wxa[j][:].rearrange("p (e r) -> p e r", e=NE),
                                                bank[:, 0:D].rearrange("p (e r) -> p e r", e=NE),
                                                spread(comb[:, j, :], NE, D // NE), ALU.mult).then_inc(misc_free, 1)
                    elif kind == "wT":
                        nc.vector.tensor_copy(wxaT[j % 2][:], bank[:, 0:D].rearrange("p (f n) -> p f n", f=2)
                                              ).then_inc(misc_free, 1)
                    else:
                        xb = xall[:, bass.ds(4 * c + j, 1), :].rearrange("p o n -> p (o n)")
                        steps.then(nc.vector.tensor_tensor(xb, xb, rows[:, 4 * NE:4 * NE + D], ALU.add))
                        nc.vector.tensor_tensor(xb, bank[:, 0:D], xb, ALU.add).then_inc(misc_free, 1)
            steps.leave(2)


def layouts(inp):
    a = {k: np.asarray(v) for k, v in inp.items()}
    half, p4, s, d = np.meshgrid(np.arange(2), np.arange(4), np.arange(2), np.arange(HD), indexing="ij")
    c0 = (16 * d + 8 * half + 4 * s + p4).ravel()
    c0_rot = (16 * (d ^ 1) + 8 * half + 4 * s + p4).ravel()
    dd = d.ravel()
    k_, s_, d_ = np.meshgrid(np.arange(PAIRS), np.arange(2), np.arange(HD), indexing="ij")
    v0 = (16 * d_ + 8 * (k_ // 4) + 4 * s_ + k_ % 4).ravel()
    j_, g_, e_ = np.meshgrid(np.arange(4), np.arange(4), np.arange(HD), indexing="ij")
    kk = 2 * g_ + j_ // 2
    o0 = (16 * e_ + 8 * (kk // 4) + 4 * (j_ % 2) + kk % 4).ravel()
    wq, wk, wv, wm = (a[f"L0_xattn_W{x}"] for x in "qkvm")
    bq, bk, bv, bm = (a[f"L0_xattn_b{x}"] for x in "qkvm")
    wa = np.concatenate([wq[c0].T, wq[c0_rot].T, wk[c0].T, wk[c0_rot].T, wv[v0].T, wm[:, o0].T], axis=1)
    sign = np.where(dd % 2, 1.0, -1.0).astype(np.float32)
    one = (((np.arange(P) % 16) >= 5) & ((np.arange(P) % 16) < 11)).astype(np.float32)
    cols = np.stack([bq[c0], bq[c0_rot], bk[c0], bk[c0_rot], bv[o0], bm, sign, one], axis=1)
    enc = a["L0_xattn_encoding"].reshape(2, D, HD)
    rope = np.concatenate([enc[0].T[dd], enc[1].T[dd]], axis=1)
    bf16 = mybir.dt.np(BF16)
    def blocks(w):
        return w.reshape(2, P, -1).transpose(1, 0, 2)

    up = a["L0_ffn_w_up"].reshape(NE, 2, P, INTER).transpose(2, 1, 0, 3)
    s_up = a["L0_ffn_shared_up"].reshape(2, P, NCH - NE, INTER).transpose(1, 0, 2, 3)
    dn = a["L0_ffn_w_down"].transpose(1, 0, 2)
    s_dn = a["L0_ffn_shared_down"].reshape(NCH - NE, INTER, D).transpose(1, 0, 2)
    row = np.concatenate([a["L0_ffn_e_bias"], a["L1_ffn_rb2"][:NE], a["L1_ffn_gates"],
                          np.arange(-NE, 0, dtype=np.float32), a["L1_ffn_bias"]])
    sel = np.zeros((3, NE, NE, P), np.float32)
    for e in range(NE):
        sel[:, e, e] = 1.0
    ch, hf, pm, sm, dm = np.meshgrid(np.arange(2), np.arange(2), np.arange(4), np.arange(2), np.arange(HD), indexing="ij")
    hd = 16 * hf + 4 * (2 * ch + sm) + pm
    q1, kv1 = (HD * hd + dm).ravel(), (2 * (HD * hd + dm)).ravel()
    pr, cv, sv, dv = np.meshgrid(np.arange(PAIRS), np.arange(2), np.arange(2), np.arange(HD), indexing="ij")
    v1 = (2 * (HD * (16 * (pr // 4) + 4 * (2 * cv + sv) + pr % 4) + dv) + 1).ravel()
    wkv = np.concatenate([a["L1_xattn_Wk"], a["L1_xattn_Wv"]], axis=0)
    wc = blocks(np.concatenate([a["L1_xattn_Wq"][q1].T, wkv[kv1].T, wkv[v1].T], axis=1))
    wA = a["L1_ffn_A"].reshape(D, D).T
    wB = a["L1_ffn_B"].transpose(0, 2, 1).reshape(D, D)
    t = {"wr": blocks(a["L0_ffn_router_weight"].T), "rows": np.broadcast_to(row, (P, row.size)),
         "sel": sel.reshape(3 * NE, NE, P).astype(bf16),
         "wup": np.concatenate([up, s_up], axis=2), "wdn": np.concatenate([dn, s_dn], axis=1),
         "wc": wc, "wd": blocks(np.concatenate([a["L1_ffn_W"].T, wA], axis=1)), "wb": blocks(wB),
         "w1": blocks(a["L1_ffn_rw1"].T), "w2": a["L1_ffn_rw2"][:NE].T, "rb1": a["L1_ffn_rb1"].reshape(RH, 1),
         "x": a["x"], "ctx": a["ctx_2048"], "wa": wa, "cols": cols, "rope": rope,
         "eye": np.eye(P, dtype=np.float32), "eye16": np.eye(P).astype(bf16)}
    return {k: np.ascontiguousarray(v) for k, v in t.items()}


def kernel(**inputs):
    import concourse.bacc as bacc
    from concourse.bass_utils import run_bass_kernel_spmd

    nc = bacc.Bacc("TRN2", target_bir_lowering=False, num_devices=1)
    arrays = {f"in_{k}": v for k, v in layouts(inputs).items()}
    t = {k[3:]: nc.dram_tensor(k, v.shape, mybir.dt.from_np(v.dtype), kind="ExternalInput").ap()
         for k, v in arrays.items()}
    out = nc.dram_tensor("out_0", (NB, P, D), F32, kind="ExternalOutput").ap()
    build(nc, t, out)
    return run_bass_kernel_spmd(nc, [arrays], core_ids=[0]).results[0]["out_0"]
```

```python
from contextlib import ExitStack

import numpy as np

import concourse.bass as bass
from concourse import mybir

F32 = mybir.dt.float32
BF16 = mybir.dt.bfloat16
I32 = mybir.dt.int32
ALU = mybir.AluOpType
ACT = mybir.ActivationFunctionType
AX_X = mybir.AxisListType.X

P = 128
NB = 8
D = 256
HD = 8
LN_EPS = 1e-5
RMS_EPS = 1e-6
SCALE = HD ** -0.5
TERMS = 6
ROWS = 64
MAX_ROW = 46
PAIRS = 8
NE = 16
INTER = 128
SHARED = 512
NCH = NE + SHARED // INTER
TOK = NB * P
HALF = TOK // 2
RH = 64
RSQRT_GUESS = 0x5F3759DF


class Steps:

    def __init__(self, eng, sem):
        self.eng, self.sem, self.base, self.n = eng, sem, 0, 0

    def then(self, ins):
        self.n += 1
        ins.then_inc(self.sem, 1)
        self.eng.wait_ge(self.sem, self.base + self.n)

    def enter(self, i, per):
        self.start, self.per, self.base, self.n = self.base + self.n, per, self.base + self.n + i * per, 0

    def leave(self, times):
        assert self.n == self.per, self.n
        self.base, self.n = self.start + times * self.per, 0


def build(nc, t, out):
    with ExitStack() as ctx:
        def sb(name, shape, dt=F32):
            return ctx.enter_context(nc.sbuf_tensor(name, shape, dt))

        def sem(name):
            return ctx.enter_context(nc.semaphore(name))

        psum = ctx.enter_context(nc.psum_tensor("psum", [P, 8, 512], F32))

        xall = sb("xall", [P, NB, D])
        wa = sb("wa", [P, 6, P])
        cols = sb("cols", [P, 8])
        rope = sb("rope", [P, 2, D])
        eye = sb("eye", [P, P])
        eye16 = sb("eye16", [P, P], BF16)
        ctxb = [sb(f"ctx{i}", [P, D]) for i in range(2)]
        xn = [sb(f"xn{i}", [P, D]) for i in range(2)]
        stats = sb("stats", [P, NB, 6])
        mv = sb("mv", [P, NB, 2])
        rstd = sb("rstd", [P, NB])
        rs_v = sb("rs_v", [P, 64])
        rs_a = sb("rs_a", [P, 64])
        rope_ab = sb("rope_ab", [P, 2, 2, D])
        qk = sb("qk", [P, 2, D])
        qk_rest = sb("qk_rest", [P, 2, D])
        parts = [sb(f"parts{i}", [P, 2, 3, D], BF16) for i in range(2)]
        qstk = [sb(f"qstk{i}", [P, PAIRS, D], BF16) for i in range(2)]
        kstk = [sb(f"kstk{i}", [P, 2, PAIRS, D], BF16) for i in range(2)]
        fill = sb("fill", [P, 2, 2, D], BF16)
        mx = sb("mx", [P, 2, 2, 8])
        mneg = sb("mneg", [P, 2, 2, 8])
        zeros = sb("zeros", [P, 2, 8])
        mpart = sb("mpart", [P, 2, 2, 24], BF16)
        mT = sb("mT", [24, 2, D], BF16)
        prob = [sb(f"prob{i}", [P, 2 * 512]) for i in range(2)]
        vt = [sb(f"vt{i}", [P, 2, 16, 32]) for i in range(2)]
        pvT = [sb(f"pvT{i}", [P, 512]) for i in range(2)]
        den = [sb(f"den{i}", [P, 16]) for i in range(2)]
        o2 = sb("o2", [P, 2 * P])
        o3 = sb("o3", [P, 2 * P])
        cb = sb("cb", [P, 1])
        wup = sb("wup", [P, 2, NCH, INTER])
        wdn = sb("wdn", [P, NCH, D])
        wr = sb("wr", [P, 2, NE])
        rows = sb("rows", [P, 4 * NE + D])
        xnT = sb("xnT", [P, 2, TOK])
        lgT = sb("lgT", [NE, TOK])
        sc = sb("sc", [P, NB, NE])
        sel_s = sb("sel_s", [P, NB, NE])
        pair_sum = sb("pair_sum", [P, NB * 4, 6])
        gsum = sb("gsum", [P, NB, 4])
        hot = [sb(f"hot{i}", [P, NB, NE]) for i in range(2)]
        hot_t = sb("hot_t", [P, NB, NE])
        top = [sb(f"top{i}", [P, NB]) for i in range(2)]
        top_i = sb("top_i", [P, NB])
        comb = sb("comb", [P, NB, NE])
        rel = [sb(f"rel{i}", [P, HALF]) for i in range(2)]
        act2 = [sb(f"act2{i}", [P, HALF]) for i in range(2)]
        wc = sb("wc", [P, 2, 3 * D])
        ctxT = [sb(f"ctxT{i}", [P, 2, P]) for i in range(2)]
        xT1 = sb("xT1", [P, 2, P])
        sq = sb("sq", [P, 2 * D])
        ss = sb("ss", [P, 64])
        rs = sb("rs", [P, 64])
        qkn = sb("qkn", [P, 2, D])
        wd = sb("wd", [P, 2, 2 * D])
        wb = sb("wb", [P, 2, D])
        w1 = sb("w1", [P, 2, RH])
        w2 = sb("w2", [2 * RH, 2, NE])
        nrb1 = sb("nrb1", [2 * RH, 2])
        eh = sb("eh", [2 * RH, HALF // 2])
        zh = sb("zh", [2 * RH, HALF // 2])
        wxa = [sb(f"wxa{i}", [P, D]) for i in range(4)]
        wxaT = [sb(f"wxaT{i}", [P, 2, P]) for i in range(2)]
        scr = nc.dram_tensor("stack_scratch", (2, 2, P * 8, D), BF16, kind="Internal").ap()

        x_in = [sem(f"x_in{i}") for i in range(2)]
        w_in = sem("w_in")
        rope_in = sem("rope_in")
        eye_in = sem("eye_in")
        ctx_in = [sem(f"ctx_in{i}") for i in range(2)]
        xn_ready = sem("xn_ready")
        misc_full = sem("misc_full")
        misc_free = sem("misc_free")
        st_full = sem("st_full")
        exp_done = sem("exp_done")
        pv_done = sem("pv_done")
        pv_free = sem("pv_free")
        qk_ready = sem("qk_ready")
        hi_done = sem("hi_done")
        rest_done = sem("rest_done")
        mid_done = sem("mid_done")
        lo_done = sem("lo_done")
        parts_out = [sem(f"parts_out{i}") for i in range(2)]
        stack_in = [[sem(f"stack_in{i}{h}") for h in range(2)] for i in range(2)]
        neg_done = sem("neg_done")
        mrow_in = [sem(f"mrow_in{h}") for h in range(2)]
        o3_ready = sem("o3_ready")
        init = sem("init")
        fill_set = sem("fill_set")
        fill_out = sem("fill_out")
        out_done = sem("out_done")
        ffn_in = sem("ffn_in")
        w2_in = sem("w2_in")
        sig_ready = sem("sig_ready")
        h_full = sem("h_full")
        relu_done = sem("relu_done")
        a_done = sem("a_done")
        y_full = sem("y_full")
        y_free = sem("y_free")
        sq_done = sem("sq_done")
        eh_done = sem("eh_done")
        wide_done = sem("wide_done")
        wxa_done = sem("wxa_done")
        wt_full = sem("wt_full")
        wt_done = sem("wt_done")
        delta_done = sem("delta_done")
        result = sem("result")
        gap_done = sem("gap_done")
        egap_done = sem("egap_done")
        dve_step = sem("dve_step")
        pool_step = sem("pool_step")

        def misc(u):
            return psum[:, 4 + (u % 3 if u < A_END else u % 2), :]

        def exp_buf(k):
            return psum[:, 2 * (k % 2):2 * (k % 2) + 2, :]

        def pv_bank(i):
            return psum[:, 6 + i, :]

        def a_uses(spot, wm, m, pqk):
            u = [("max", spot // 2, spot % 2)] if m else []
            u += [("maxT", 1)] if spot == 2 else []
            u += [("v+wm",)] if (m or wm) and spot == 4 else []
            u += [("q",)] if pqk and spot == 9 else []
            u += [("maxT", 0)] if m and spot == 10 else []
            u += [("k",)] if pqk and spot == 12 else []
            return u

        def a_index(flags, use):
            return [x for spot in range(2 * PAIRS) for x in a_uses(spot, *flags)].index(use)

        def a_flags(b):
            return b > 0, b < NB - 1, b < NB - 3

        def count(uses, steps, flags, b):
            return sum(len(uses(spot, *flags(b))) for spot in range(2 * steps))

        PROLOGUE = [("cb", 0), ("k", 0), ("q", 0), ("v", 0), ("k", 1), ("q", 1), ("k", 2), ("q", 2)]
        FIRST = 2
        FIRST_MAX = list(range(13)) + [None] + list(range(13, 2 * PAIRS))
        N_PRO = len(PROLOGUE) + len(FIRST_MAX)
        PER_A = count(a_uses, PAIRS, a_flags, 1)
        assert PER_A % 3 == 0 and all(a_flags(b) == a_flags(1) for b in range(1, 5))

        def first_use(start, uses, steps, flags, b):
            if isinstance(b, int):
                return start + sum(count(uses, steps, flags, x) for x in range(b))
            per = count(uses, steps, flags, 1)
            return start + count(uses, steps, flags, 0) - per + per * b

        def a_base(b):
            return first_use(N_PRO, a_uses, PAIRS, a_flags, b)

        A_END = a_base(NB)

        CHUNK = NCH // 4
        FFN_IN = 16 * (2 * 4 + 2)
        B_EARLY = 6
        B_USES = ([("xT", b) for b in range(B_EARLY)] + [("wm",), ("lgT", 0)]
                  + [("xT", b) for b in range(B_EARLY, NB)] + [("lgT", 1), ("lg",)])
        BLOCKS = list(range(NE, NCH)) + list(range(NE))
        N_SHARED = NCH - NE
        GROUPS = 1 + NE
        B_END = A_END + len(B_USES)
        C_PRO = [("xT", 0), ("cT", 0), ("qk", 0), ("v", 0), ("qkT", 0), ("xT", 1), ("cT", 1), ("qk", 1), ("xT", 2),
                 ("qkT", 1), ("cT", 2), ("qk", 2)]
        C_AFTER = 4
        C_STEPS = 4
        AHEAD = {"v": 1, "o": -1, "xT": 3, "cT": 3, "qk": 3, "qkT": 2}

        D_EARLY = {(5, 6): ("dxT", 0), (5, 7): ("dxT", 1), (6, 1): ("dxT", 2), (6, 2): ("dxT", 3),
                   (6, 6): ("dh", 0), (7, 3): ("dlg", 0)}

        def c_uses(spot, o, m, t, pqk, late):
            u = [("v",)] if m and spot == 0 else []
            u += [("qkT",)] if t and spot == 3 else []
            u += [("o",)] if o and spot == 4 else []
            u += [("xT",)] if pqk and spot == 5 else []
            u += [("cT",)] if pqk and spot == 5 else []
            u += [("qk",)] if pqk and spot == 7 else []
            u += [D_EARLY[late, spot]] if (late, spot) in D_EARLY else []
            return u

        def c_flags(b):
            return b > 0, b < NB - 1, b < NB - 2, b < NB - 3, b * (b > 4)

        def c_index(flags, use):
            return [x for spot in range(2 * C_STEPS) for x in c_uses(spot, *flags)].index(use)

        C_FIRST = B_END + len(C_PRO)

        def c_base(b):
            return first_use(C_FIRST, c_uses, C_STEPS, c_flags, b)

        C_END = c_base(NB)
        D_USES = [("o",), ("dxT", 4), ("dxT", 5), ("dxT", 6), ("dxT", 7), ("dh", 1), ("dlg", 1)]

        def d_index(use):
            return C_END + D_USES.index(use)

        def y_banks(y):
            return psum[:, 2:4, :] if y % 2 == 0 else psum[:, 6:8, :]

        def add_factors(eng):
            eng.tensor_tensor(qk[:], rope_ab[:, 0], rope_ab[:, 1], ALU.add).then_inc(qk_ready, 1)

        def take_rest(eng, par):
            eng.tensor_tensor(qk_rest[:], qk[:], parts[par][:, :, 0, :], ALU.subtract).then_inc(rest_done, 1)

        def take_third(eng, par):
            eng.tensor_tensor(parts[par][:, :, 2, :], qk_rest[:], parts[par][:, :, 1, :], ALU.subtract
                              ).then_inc(lo_done, 1)

        block = ctx.enter_context(nc.Block())

        @block.sync
        def _(sp):
            def by_channel(par, ten, first, n):
                return scr[par, ten].rearrange("(c t) n -> c t n", t=8)[:, first:first + n, :]

            x_rows = t["x"].rearrange("b p d -> p b d")
            sp.dma_start(xall[:, 0:FIRST, :], x_rows[:, 0:FIRST, :]).then_inc(x_in[0], 16)
            sp.dma_start(wa[:], t["wa"].rearrange("p (w c) -> p w c", w=6)).then_inc(w_in, 16)
            sp.dma_start(rope[:], t["rope"].rearrange("p (w c) -> p w c", w=2)).then_inc(rope_in, 16)
            sp.dma_start(xall[:, FIRST:NB, :], x_rows[:, FIRST:NB, :]).then_inc(x_in[1], 16)
            sp.dma_start(ctxb[1][:], t["ctx"][1]).then_inc(ctx_in[1], 16)
            sp.wait_ge(fill_set, 1)
            for ten in range(2):
                for par in range(2):
                    sp.dma_start(by_channel(par, ten, TERMS, 2), fill[:, ten]).then_inc(fill_out, 16)

            def parts_to_dram(b0, i):
                par, nth = b0 % 2, b0 // 2 + i
                sp.wait_ge(lo_done, b0 + 2 * i + 1)
                if b0 >= 2:
                    for half in range(2):
                        sp.wait_ge(stack_in[par][half], nth * 48)
                src = parts[par]
                for part, (first, n) in enumerate(((0, 3), (3, 2), (5, 1))):
                    sp.dma_start(by_channel(par, 0, first, n), src[:, 0, part:part + 1, :].broadcast_to((P, n, D))
                                 ).then_inc(parts_out[par], 16)
                for first, n in ((0, 3), (3, 2), (5, 1)):
                    sp.dma_start(by_channel(par, 1, first, n), src[:, 1, 0:n, :]).then_inc(parts_out[par], 16)

            def stack_from_dram(b0, i, half):
                par, nth = b0 % 2, b0 // 2 + i
                sp.wait_ge(parts_out[par], nth * 96 + 96)
                src = [scr[par, ten].rearrange("(k r) n -> r k n", r=P)[:, 4 * half:4 * half + 4, :] for ten in range(2)]
                sp.dma_start(qstk[par][:, 4 * half:4 * half + 4, :], src[0]).then_inc(stack_in[par][half], 16)
                for s in range(2):
                    rows = slice(ROWS * s, ROWS * s + ROWS)
                    sp.dma_start(kstk[par][rows, s, 4 * half:4 * half + 4, :], src[1][rows]
                                 ).then_inc(stack_in[par][half], 16)

            def max_rows(ready, par, half):
                sp.wait_ge(misc_free, ready)
                sp.dma_start(qstk[par][MAX_ROW:MAX_ROW + 41:8, 4 * half:4 * half + 4, :],
                             mT[:, half, :]).then_inc(mrow_in[half], 16)

            def inner_weights(first):
                e = bass.ds(first, CHUNK)
                sp.dma_start(wup[:, :, e, :], t["wup"][:, :, e, :]).then_inc(ffn_in, 16)
                sp.dma_start(wdn[:, e, :], t["wdn"][:, e, :]).then_inc(ffn_in, 16)

            sp.wait_ge(fill_out, 64)
            sp.wait_ge(init, 2)
            sp.wait_ge(misc_free, PROLOGUE.index(("v", 0)) + 1)
            sp.dma_start(ctxb[0][:], t["ctx"][2]).then_inc(ctx_in[0], 16)
            for b in range(2):
                parts_to_dram(b, 0)
                for half in range(2):
                    stack_from_dram(b, 0, half)
            max_rows(len(PROLOGUE) + FIRST_MAX.index(None) + 1, 0, 0)

            def slot(b0, i, shape):
                b = b0 + 2 * i
                wm, m, pqk = flags = a_flags(shape)
                max_rows(a_base(b) + a_index(flags, ("maxT", 1)) + 1, b0 % 2, 1)
                if pqk:
                    sp.wait_ge(misc_free, a_base(b) + a_index(flags, ("v+wm",)) + 1)
                    sp.dma_start(ctxb[(b0 + 1) % 2][:], t["ctx"][b + 3]).then_inc(ctx_in[(b0 + 1) % 2], 16)
                if shape < NB - 2:
                    parts_to_dram(b0 + 2, i)
                    sp.wait_ge(st_full, b * PAIRS + 4)
                    stack_from_dram(b0 + 2, i, 0)
                if m:
                    max_rows(a_base(b) + a_index(flags, ("maxT", 0)) + 1, (b0 + 1) % 2, 0)
                if shape == 1:
                    inner_weights(CHUNK * (b - 1))
                if shape < NB - 2:
                    sp.wait_ge(st_full, b * PAIRS + 8)
                    stack_from_dram(b0 + 2, i, 1)

            slot(0, 0, 0)
            with sp.Fori(0, 2) as i:
                for b0 in (1, 2):
                    slot(b0, i, 1)
            slot(5, 0, 5)
            for dst, name in ((wr, "wr"), (rows, "rows")):
                sp.dma_start(dst[:], t[name]).then_inc(ffn_in, 16)
            slot(6, 0, 6)
            slot(7, 0, 7)
            for dst, name in ((wc[:], "wc"), (wd[:], "wd"), (wb[:], "wb"), (w1[:], "w1"), (w2[:], "w2"),
                              (nrb1[:, 0:1], "rb1")):
                sp.dma_start(dst, t[name]).then_inc(w2_in, 16)

            for b in range(2):
                sp.wait_ge(misc_free, a_base(5 + b) + a_index(a_flags(5 + b), ("v+wm",)) + 1)
                sp.dma_start(ctxb[b][:], t["ctx"][b]).then_inc(ctx_in[b], 16)
            sp.wait_ge(misc_free, B_END + C_PRO.index(("cT", 0)) + 1)
            sp.dma_start(ctxb[0][:], t["ctx"][2]).then_inc(ctx_in[0], 16)
            for b in range(2):
                parts_to_dram(NB + b, 0)
                for half in range(2):
                    stack_from_dram(NB + b, 0, half)

            def slot_c(b0, i, shape):
                b = b0 + 2 * i
                o, m, t2, pqk, late = c_flags(shape)
                if t2:
                    parts_to_dram(NB + b0 + 2, i)
                    sp.wait_ge(st_full, NB * PAIRS + b * C_STEPS + 4)
                    for half in range(2):
                        stack_from_dram(NB + b0 + 2, i, half)

            slot_c(0, 0, 0)
            with sp.Fori(0, 2) as i:
                for b0 in (1, 2):
                    slot_c(b0, i, 1)
            slot_c(5, 0, 5)

            for b in range(NB):
                sp.wait_ge(result, b + 1)
                sp.dma_start(out[b], xall[:, b, :]).then_inc(out_done, 16)
            sp.wait_ge(out_done, 16 * NB)

        @block.tensor
        def _(pe):
            def project(par, w, bank):
                src = xn[par] if w == 0 else ctxb[par]
                for r in range(2):
                    last = nc.tensor.matmul(bank[:, r * D:(r + 1) * D], wa[:, w + r, :], src[:],
                                            start=True, stop=True)
                last.then_inc(misc_full, 1)

            def values(par, bank):
                for mb in range(2):
                    last = nc.tensor.matmul(bank[:, mb * P:(mb + 1) * P], ctxb[par][:, mb * P:(mb + 1) * P],
                                            wa[:, 4, :], start=True, stop=True)
                return last

            def max_scores(par, pair, s, bank):
                for nb in range(2):
                    last = nc.tensor.matmul(bank[:, nb * D:(nb + 1) * D],
                                            qstk[par][:, pair, nb * P:(nb + 1) * P], kstk[par][:, s, pair, :],
                                            start=True, stop=True)
                last.then_inc(misc_full, 1)

            def max_transpose(half, bank):
                o = bank.bitcast(BF16)
                for nb in range(2):
                    last = nc.tensor.transpose(o[0:24, nb * P:(nb + 1) * P],
                                               mpart[:, half, nb, :], eye16[:])
                last.then_inc(misc_full, 1)

            def scores(b, par, k, first=False):
                if not first:
                    pe.wait_ge(exp_done, b * PAIRS + k)
                if k % 4 == 0:
                    pe.wait_ge(mrow_in[k // 4], 16 * (b + 1))
                for s in range(2):
                    for mb in range(2):
                        last = nc.tensor.matmul(exp_buf(k)[:, s, mb * D:(mb + 1) * D],
                                                kstk[par][:, s, k, mb * P:(mb + 1) * P], qstk[par][:, k, :],
                                                start=True, stop=True)
                last.then_inc(st_full, 1)

            def pv(b, par, k):
                pe.wait_ge(exp_done, b * PAIRS + k + 2)
                if k % 4 == 0:
                    pe.wait_ge(pv_free, 2 * b + 2 + k // 4)
                for s in range(2):
                    j, g = 2 * (k % 2) + s, k // 2
                    for mb in range(2):
                        last = nc.tensor.matmul(
                            pv_bank(1)[32 * j:32 * j + 32, (g % 2) * D:(g % 2 + 1) * D],
                            vt[par][:, mb, 2 * k + s, :],
                            prob[k % 2][:, (2 * s + mb) * D:(2 * s + mb + 1) * D],
                            start=(mb == 0), stop=(mb == 1))
                last.then_inc(pv_done, 1)

            def output(bank):
                return nc.tensor.matmul(bank, wa[:, 5, :], o3[:], start=True, stop=True)

            pe.wait_ge(w_in, 32)
            nc.tensor.matmul(misc(0)[:, 0:1], wa[:, 5, :], cols[:, 4:5], start=True, stop=True).then_inc(misc_full, 1)
            for u, (kind, b) in list(enumerate(PROLOGUE))[1:]:
                if u > 2:
                    pe.wait_ge(misc_free, u - 2)
                if kind == "q":
                    pe.wait_ge(xn_ready, b + 1)
                    project(b % 2, 0, misc(u))
                elif kind == "k":
                    pe.wait_ge(ctx_in[b % 2], 16 + 16 * (b // 2))
                    project(b % 2, 2, misc(u))
                else:
                    values(0, misc(u)).then_inc(misc_full, 1)
            u = len(PROLOGUE)
            pe.wait_ge(init, 2)
            pe.wait_ge(eye_in, 32)
            for n in FIRST_MAX:
                pe.wait_ge(misc_free, u - 2)
                if n is None:
                    pe.wait_ge(neg_done, 1)
                    max_transpose(0, misc(u))
                else:
                    if n % PAIRS == 0:
                        pe.wait_ge(stack_in[0][n // PAIRS], 48)
                    max_scores(0, n // 2, n % 2, misc(u))
                u += 1
            scores(0, 0, 0, first=True)

            def slot(b0, i, shape):
                b = b0 + 2 * i
                wm, m, pqk = flags = a_flags(shape)
                par, other = b0 % 2, (b0 + 1) % 2
                n = 0
                for spot in range(2 * PAIRS):
                    step = spot // 2
                    if spot % 2:
                        pv(b, par, step)
                    elif step < PAIRS - 1:
                        scores(b, par, step + 1)
                    elif m:
                        scores(b + 1, other, 0)
                    for use in a_uses(spot, *flags):
                        pe.wait_ge(misc_free, a_base(b) + n - 2)
                        bank = misc(a_base(b0) + n)
                        if use[0] == "max":
                            if use[1] % 4 == 0 and use[2] == 0:
                                pe.wait_ge(stack_in[other][use[1] // 4], 48 * ((b0 + 1) // 2 + i + 1))
                            max_scores(other, use[1], use[2], bank)
                        elif use[0] == "q":
                            pe.wait_ge(xn_ready, b + 4)
                            project(other, 0, bank)
                        elif use[0] == "k":
                            pe.wait_ge(ctx_in[other], 16 * ((b0 + 3) // 2 + i + 1))
                            project(other, 2, bank)
                        elif use[0] == "maxT":
                            pe.wait_ge(neg_done, 2 * b + (2 if use[1] else 3))
                            max_transpose(use[1], bank)
                        else:
                            if m:
                                last = values(other, bank[:, 0:D])
                            if wm:
                                pe.wait_ge(o3_ready, b)
                                last = output(bank[:, D:2 * D])
                            last.then_inc(misc_full, 1)
                        n += 1

            slot(0, 0, 0)
            with pe.Fori(0, 2) as i:
                for b0 in (1, 2):
                    slot(b0, i, 1)
            for b in (5, 6, 7):
                slot(b, 0, b)

            def transposes(blocks, bank):
                for n, blk in enumerate(blocks):
                    last = nc.tensor.transpose(bank[:, n * P:(n + 1) * P], blk, eye[:])
                last.then_inc(misc_full, 1)

            def up(c, g):
                n = c * NCH + g
                if n >= 2:
                    pe.wait_ge(relu_done, n - 1)
                elif n == 0:
                    pe.wait_ge(misc_free, A_END + 4)
                for f in range(2):
                    last = nc.tensor.matmul(psum[:, n % 2, :], wup[:, f, BLOCKS[g], :],
                                            xnT[:, f, c * HALF:(c + 1) * HALF], start=(f == 0), stop=(f == 1))
                last.then_inc(h_full, 1)

            def down(c, g):
                n = c * NCH + g
                first, final = g == 0 or g >= N_SHARED, g >= N_SHARED - 1
                y = c * GROUPS + max(0, g - N_SHARED + 1)
                pe.wait_ge(a_done, n + 1)
                if first and y >= 2:
                    pe.wait_ge(y_free, y - 1)
                for j in range(4):
                    last = nc.tensor.matmul(y_banks(y)[:, j // 2, (j % 2) * D:(j % 2 + 1) * D],
                                            act2[n % 2][:, j * P:(j + 1) * P], wdn[:, BLOCKS[g], :],
                                            start=(first and j % 2 == 0), stop=final, skip_group_check=True)
                if final:
                    last.then_inc(y_full, 1)

            pe.wait_ge(ffn_in, FFN_IN)
            for n, use in enumerate(B_USES):
                u = A_END + n
                pe.wait_ge(misc_free, u - 1 if n else u)
                bank = misc(u)
                if use[0] == "xT":
                    pe.wait_ge(xn_ready, NB + use[1] + 1)
                    transposes([xn[use[1] % 2][:, f * P:(f + 1) * P] for f in range(2)], bank)
                elif use[0] == "wm":
                    pe.wait_ge(o3_ready, NB)
                    output(bank[:, D:2 * D]).then_inc(misc_full, 1)
                    up(0, 0)
                    up(0, 1)
                    down(0, 0)
                elif use[0] == "lgT":
                    if use[1] == 1:
                        pe.wait_ge(misc_free, u)
                    for f in range(2):
                        last = nc.tensor.matmul(bank[0:NE, :], wr[:, f, :],
                                                xnT[:, f, use[1] * HALF:(use[1] + 1) * HALF],
                                                start=(f == 0), stop=(f == 1))
                    last.then_inc(misc_full, 1)
                    if use[1] == 1:
                        up(0, 2)
                        down(0, 1)
                else:
                    pe.wait_ge(misc_free, u)
                    for b in range(NB):
                        last = nc.tensor.transpose(bank[:, b * NE:(b + 1) * NE], lgT[:, b * P:(b + 1) * P],
                                                   eye[0:NE, 0:NE])
                    last.then_inc(misc_full, 1)

            for g in range(2, NCH):
                if g + 1 < NCH:
                    up(0, g + 1)
                else:
                    up(1, 0)
                down(0, g)

            def d_use(kind, n, bank):
                if kind == "dxT":
                    pe.wait_ge(xn_ready, 3 * NB + n + 1)
                    transposes([xn[n % 2][:, f * P:(f + 1) * P] for f in range(2)], bank)
                elif kind == "dh":
                    for s in range(2):
                        cols_of = slice(n * HALF + s * D, n * HALF + s * D + D)
                        for f in range(2):
                            last = nc.tensor.matmul(bank[RH * s:RH * s + RH, 0:D], w1[:, f, :], xnT[:, f, cols_of],
                                                    start=(f == 0), stop=(f == 1))
                    last.then_inc(misc_full, 1)
                else:
                    for j in range(4):
                        last = nc.tensor.matmul(bank[:, j * NE:(j + 1) * NE], eh[:, (j % 2) * P:(j % 2 + 1) * P],
                                                w2[:, j // 2, :], start=True, stop=True)
                    last.then_inc(misc_full, 1)

            def c_use(kind, b, par, bank, u):
                if kind == "xT":
                    pe.wait_ge(xn_ready, 2 * NB + b + 1)
                    transposes([xn[par][:, f * P:(f + 1) * P] for f in range(2)], bank)
                elif kind == "cT":
                    transposes([ctxb[par][:, f * P:(f + 1) * P] for f in range(2)], bank)
                elif kind == "qk":
                    pe.wait_ge(misc_free, u)
                    for ten, src in enumerate((xT1, ctxT[par])):
                        for f in range(2):
                            last = nc.tensor.matmul(bank[:, ten * D:(ten + 1) * D], src[:, f, :],
                                                    wc[:, f, ten * D:(ten + 1) * D], start=(f == 0), stop=(f == 1))
                    last.then_inc(misc_full, 1)
                elif kind == "qkT":
                    transposes([qkn[:, ten, f * P:(f + 1) * P] for ten in range(2) for f in range(2)], bank)
                elif kind == "v":
                    for f in range(2):
                        last = nc.tensor.matmul(bank[:, 0:D], ctxT[par][:, f, :], wc[:, f, 2 * D:3 * D],
                                                start=(f == 0), stop=(f == 1))
                    last.then_inc(misc_full, 1)
                else:
                    pe.wait_ge(o3_ready, NB + b + 1)
                    transposes([o3[:, f * P:(f + 1) * P] for f in range(2)], bank)

            def scores_c(b, par, k, first=False):
                if not first:
                    pe.wait_ge(exp_done, NB * PAIRS + b * C_STEPS + k)
                buf = exp_buf(k).rearrange("p a n -> p (a n)")
                for pp in range(2):
                    for ch in range(2):
                        for s in range(2):
                            h = 4 * pp + 2 * ch + s
                            last = nc.tensor.matmul(buf[:, h * P:(h + 1) * P],
                                                    kstk[par][:, s, 2 * k + pp, ch * P:(ch + 1) * P],
                                                    qstk[par][:, 2 * k + pp, ch * P:(ch + 1) * P],
                                                    start=True, stop=True)
                last.then_inc(st_full, 1)

            def pv_c(b, par, k):
                pe.wait_ge(exp_done, NB * PAIRS + b * C_STEPS + k + 2)
                if k % 2 == 0:
                    pe.wait_ge(pv_free, 2 * NB + 2 * b + k // 2 + 1)
                v = vt[par][:].rearrange("m a h r -> m (a h) r")
                for pp in range(2):
                    for j in range(4):
                        h = 4 * pp + j
                        g = 2 * (k % 2) + pp
                        last = nc.tensor.matmul(pv_bank(k // 2)[32 * j:32 * j + 32, g * P:(g + 1) * P],
                                                v[:, 8 * k + h, :], prob[k % 2][:, h * P:(h + 1) * P],
                                                start=True, stop=True)
                last.then_inc(pv_done, 1)

            pe.wait_ge(w2_in, 16 * 6)
            for g in range(NCH):
                if g + 1 < NCH:
                    up(1, g + 1)
                down(1, g)
                n = g - C_AFTER
                if 0 <= n < len(C_PRO):
                    kind, b = C_PRO[n]
                    u = B_END + n
                    pe.wait_ge(misc_free, u - 1)
                    if kind == "cT":
                        pe.wait_ge(ctx_in[b % 2], 16 * (5 + b // 2))
                    c_use(kind, b, b % 2, misc(u), u)
            for half in range(2):
                pe.wait_ge(stack_in[0][half], 48 * 5)
            pe.wait_ge(relu_done, 2 * NCH)
            pe.wait_ge(y_free, 2 * GROUPS)
            scores_c(0, 0, 0)

            def slot_c(b0, i, shape):
                b = b0 + 2 * i
                o, m, t2, pqk, late = flags = c_flags(shape)
                n = 0
                for spot in range(2 * C_STEPS):
                    step = spot // 2
                    if spot % 2:
                        pv_c(b, b0 % 2, step)
                    elif step < C_STEPS - 1:
                        scores_c(b, b0 % 2, step + 1)
                    elif m:
                        for half in range(2):
                            pe.wait_ge(stack_in[(b0 + 1) % 2][half], 48 * ((b0 + 1) // 2 + i + 5))
                        scores_c(b + 1, (b0 + 1) % 2, 0)
                    for kind, *what in c_uses(spot, *flags):
                        u = c_base(b) + n
                        if kind in ("dxT", "dh", "dlg"):
                            pe.wait_ge(misc_free, u - 1 if kind == "dxT" else u)
                            d_use(kind, what[0], misc(u))
                            n += 1
                            continue
                        pe.wait_ge(misc_free, u - 1)
                        if kind == "cT":
                            pe.wait_ge(ctx_in[(b0 + 1) % 2], 16 * ((b0 + 3) // 2 + i + 5))
                        c_use(kind, b + AHEAD[kind], (b0 + AHEAD[kind]) % 2, misc(c_base(b0) + n), u)
                        n += 1

            slot_c(0, 0, 0)
            with pe.Fori(0, 2) as i:
                for b0 in (1, 2):
                    slot_c(b0, i, 1)
            for b in (5, 6, 7):
                slot_c(b, 0, b)

            def ring(use):
                u = d_index(use)
                if use[0] == "o":
                    pe.wait_ge(misc_free, u - 1)
                    c_use("o", NB - 1, 1, misc(u), u)
                else:
                    pe.wait_ge(misc_free, u - 1 if use[0] == "dxT" else u)
                    d_use(*use, misc(u))

            def wide(b):
                if b >= 4:
                    pe.wait_ge(result, b - 3)
                for f in range(2):
                    last = nc.tensor.matmul(psum[:, b % 4, :], xnT[:, f, b * P:(b + 1) * P], wd[:, f, :],
                                            start=(f == 0), stop=(f == 1))
                last.then_inc(wide_done, 1)

            def flip_wxa(b):
                if b >= 2:
                    pe.wait_ge(wt_done, b - 1)
                pe.wait_ge(wxa_done, b + 1)
                for f in range(2):
                    last = nc.tensor.transpose(psum[:, 6 + b % 2, f * P:(f + 1) * P], wxa[b % 4][:, f * P:(f + 1) * P],
                                               eye[:])
                last.then_inc(wt_full, 1)

            def delta(b):
                pe.wait_ge(wt_done, b + 1)
                for f in range(2):
                    last = nc.tensor.matmul(psum[:, b % 4, 0:D], wxaT[b % 2][:, f, :], wb[:, f, :],
                                            start=False, stop=(f == 1), skip_group_check=True)
                last.then_inc(delta_done, 1)

            pe.wait_ge(exp_done, NB * (PAIRS + C_STEPS) + 1)
            pe.wait_ge(misc_free, C_END)
            wide(0)
            wide(1)
            ring(("o",))
            pe.wait_ge(pv_free, 4 * NB + 2)
            wide(2)
            wide(3)
            ring(("dxT", 4))
            flip_wxa(0)
            ring(("dxT", 5))
            flip_wxa(1)
            delta(0)
            ring(("dxT", 6))
            flip_wxa(2)
            delta(1)
            ring(("dxT", 7))
            ring(("dh", 1))
            flip_wxa(3)
            delta(2)
            delta(3)
            wide(4)
            wide(5)
            ring(("dlg", 1))
            wide(6)
            wide(7)
            flip_wxa(4)
            for b in range(4, NB):
                if b + 1 < NB:
                    flip_wxa(b + 1)
                delta(b)

        @block.scalar
        def _(act):
            def exps(b, k):
                act.wait_ge(st_full, b * PAIRS + k + 1)
                nc.scalar.activation(prob[k % 2][:], exp_buf(k).rearrange("p a n -> p (a n)"), ACT.Exp,
                                     scale=SCALE).then_inc(exp_done, 1)

            def first_parts(b, par, gone):
                act.wait_ge(qk_ready, b + 2)
                if gone is not None:
                    act.wait_ge(parts_out[par], gone * 96)
                nc.scalar.copy(parts[par][:, :, 0, :], qk[:]).then_inc(hi_done, 1)

            def second_parts(b, par):
                act.wait_ge(rest_done, b + 1)
                nc.scalar.copy(parts[par][:, :, 1, :], qk_rest[:]).then_inc(mid_done, 1)

            act.dma_start(cols[:], t["cols"]).then_inc(w_in, 16)
            act.dma_start(ctxb[0][:], t["ctx"][0]).then_inc(ctx_in[0], 16)
            act.dma_start(eye[:], t["eye"]).then_inc(eye_in, 16)
            act.dma_start(eye16[:], t["eye16"]).then_inc(eye_in, 16)
            act.drain().then_inc(exp_done, 1)
            for b in range(2):
                first_parts(b, b, None)
                second_parts(b, b)

            def slot(b0, i, shape):
                b = b0 + 2 * i
                for k in range(PAIRS):
                    exps(b, k)
                    if shape < NB - 2 and k == 0:
                        first_parts(b + 2, b0 % 2, (b0 + 2) // 2 + i)
                    if shape < NB - 2 and k == 2:
                        second_parts(b + 2, b0 % 2)

            slot(0, 0, 0)
            with act.Fori(0, 2) as i:
                for b0 in (1, 2):
                    slot(b0, i, 1)
            for b in (5, 6, 7):
                slot(b, 0, b)

            def activate(c, g):
                n = c * NCH + g
                act.wait_ge(h_full, n + 1)
                nc.scalar.activation(rel[n % 2][:], psum[:, n % 2, :], ACT.Relu).then_inc(relu_done, 1)
                act.wait_ge(relu_done, n + 1)
                nc.scalar.activation(act2[n % 2][:], rel[n % 2][:], ACT.Square).then_inc(a_done, 1)

            for g in range(3):
                activate(0, g)
            u = A_END + B_USES.index(("lg",))
            act.wait_ge(misc_full, u + 1)
            nc.scalar.activation(sc[:].rearrange("p b e -> p (b e)"), misc(u)[:, 0:NB * NE],
                                 ACT.Exp, scale=-1.0).then_inc(sig_ready, 1)
            for g in range(3, NCH):
                activate(0, g)

            def squares(b, u, bank):
                act.wait_ge(misc_full, u + 1)
                nc.scalar.activation(sq[:], bank, ACT.Square).then_inc(sq_done, 1)

            def first_parts_c(u, bank, par, gone):
                act.wait_ge(misc_full, u + 1)
                act.wait_ge(parts_out[par], gone * 96)
                nc.scalar.copy(parts[par][:, :, 0, :], bank.rearrange("p (t n) -> p t n", t=2)).then_inc(hi_done, 1)

            def second_parts_c(u, par):
                act.wait_ge(misc_free, u + 1)
                nc.scalar.copy(parts[par][:, :, 1, :], qk_rest[:]).then_inc(mid_done, 1)

            for g in range(NCH):
                activate(1, g)
                n = g - 1 - C_AFTER
                if 0 <= n < len(C_PRO) and C_PRO[n][0] in ("qk", "qkT"):
                    kind, b = C_PRO[n]
                    u = B_END + n
                    if kind == "qk":
                        squares(b, u, misc(u))
                    else:
                        first_parts_c(u, misc(u), b % 2, 4)
                if 0 < n <= len(C_PRO) and C_PRO[n - 1][0] == "qkT":
                    second_parts_c(B_END + n - 1, C_PRO[n - 1][1] % 2)

            def silu_exp(c, u):
                act.wait_ge(misc_full, u + 1)
                nc.scalar.activation(eh[:], misc(u)[:, 0:D], ACT.Exp, bias=nrb1[:, 1:2], scale=-1.0
                                     ).then_inc(eh_done, 1)

            def gap_exp(c):
                act.wait_ge(gap_done, c + 1)
                nc.scalar.activation(top_i[:, 0:4], top_i[:, 0:4], ACT.Exp).then_inc(egap_done, 1)

            def slot_c(b0, i, shape):
                b = b0 + 2 * i
                o, m, t2, pqk, late = flags = c_flags(shape)
                if pqk:
                    act.wait_ge(misc_free, B_END + C_PRO.index(("cT", 1)) + 1 if shape == 0 else c_base(b) - 1)
                    act.dma_start(ctxb[(b0 + 1) % 2][:], t["ctx"][b + 3]).then_inc(ctx_in[(b0 + 1) % 2], 16)
                for k in range(C_STEPS):
                    act.wait_ge(st_full, NB * PAIRS + b * C_STEPS + k + 1)
                    nc.scalar.activation(prob[k % 2][:], exp_buf(k).rearrange("p a n -> p (a n)"), ACT.Exp,
                                         scale=SCALE).then_inc(exp_done, 1)
                    if shape == 7 and k == 0:
                        silu_exp(0, c_base(6) + c_index(c_flags(6), ("dh", 0)))
                    if shape == 7 and k == 3:
                        gap_exp(0)
                    if t2 and k == 0 and shape:
                        squares(b + 2, c_base(b) - 1, misc(c_base(b0) - 1))
                    if t2 and k == 2:
                        n = c_index(flags, ("qkT",))
                        first_parts_c(c_base(b) + n, misc(c_base(b0) + n), b0 % 2, (b0 + 2) // 2 + i + 4)
                    if t2 and k == 3:
                        second_parts_c(c_base(b) + c_index(flags, ("qkT",)), b0 % 2)

            slot_c(0, 0, 0)
            with act.Fori(0, 2) as i:
                for b0 in (1, 2):
                    slot_c(b0, i, 1)
            for b in (5, 6, 7):
                slot_c(b, 0, b)

            def take_wxa(b):
                act.wait_ge(wt_full, b + 1)
                if b >= 2:
                    act.wait_ge(delta_done, b - 1)
                nc.scalar.copy(wxaT[b % 2][:], psum[:, 6 + b % 2, 0:D].rearrange("p (f n) -> p f n", f=2)
                               ).then_inc(wt_done, 1)

            for b in range(3):
                take_wxa(b)
            silu_exp(1, d_index(("dh", 1)))
            take_wxa(3)
            gap_exp(1)
            for b in range(4, NB):
                take_wxa(b)

        @block.gpsimd
        def _(pool):
            steps = Steps(pool, pool_step)
            for i in range(2):
                nc.gpsimd.memset(kstk[i][:].bitcast(F32), 0.0).then_inc(init, 1)

            def rotate(ready):
                pool.wait_ge(misc_free, ready)
                add_factors(nc.gpsimd)

            def rest(b, par):
                pool.wait_ge(hi_done, b + 1)
                take_rest(nc.gpsimd, par)

            def third(b, par):
                pool.wait_ge(mid_done, b + 1)
                take_third(nc.gpsimd, par)

            def negate(ready, half):
                pool.wait_ge(misc_free, ready)
                part = [mpart[:, half].rearrange("n b (s q p) -> n b s q p", s=2, q=3)[:, :, :, q, :] for q in range(3)]
                m, x, zero = (v.rearrange("n b (s p) -> n b s p", s=2) for v in (mneg[:, half], mx[:, half], zeros[:]))
                steps.then(nc.gpsimd.tensor_tensor(m, zero, x, ALU.subtract))
                for q in range(2):
                    steps.then(nc.gpsimd.tensor_tensor(part[q], m, zero, ALU.add))
                    steps.then(nc.gpsimd.tensor_tensor(m, m, part[q], ALU.subtract))
                nc.gpsimd.tensor_tensor(part[2], m, zero, ALU.add).then_inc(neg_done, 1)

            nc.gpsimd.memset(zeros[:], 0.0).then_inc(init, 1)
            pool.wait_ge(init, 3)
            nc.gpsimd.drain().then_inc(qk_ready, 1)
            for b in range(1, 3):
                rotate(PROLOGUE.index(("q", b)) + 1)
                if b < 2:
                    rest(b, b)
                    third(b, b)
            for half in range(2):
                negate(len(PROLOGUE) + FIRST_MAX.index(PAIRS * (half + 1) - 1) + 1, half)

            def slot(b0, i, shape):
                b = b0 + 2 * i
                wm, m, pqk = flags = a_flags(shape)
                if shape < NB - 2:
                    rest(b + 2, b0 % 2)
                    third(b + 2, b0 % 2)
                if m:
                    negate(a_base(b) + a_index(flags, ("max", 3, 1)) + 1, 0)
                if pqk:
                    rotate(a_base(b) + a_index(flags, ("k",)) + 1)
                if m:
                    negate(a_base(b) + a_index(flags, ("max", 7, 1)) + 1, 1)

            slot(0, 0, 0)
            with pool.Fori(0, 2) as i:
                steps.enter(i, 2 * 2 * 5)
                for b0 in (1, 2):
                    slot(b0, i, 1)
            steps.leave(2)
            for b in (5, 6):
                slot(b, 0, b)

            with pool.Fori(0, 4) as i:
                for par in range(2):
                    third(NB + 2 * i + par, par)

        @block.vector
        def _(dve):
            steps = Steps(dve, dve_step)

            def rsqrt(o, var, scale, eps, n):
                v, a = rs_v[:, 0:n], rs_a[:, 0:n]
                steps.then(nc.vector.tensor_scalar(v, var, scale, eps, ALU.mult, ALU.add))
                steps.then(nc.vector.tensor_scalar(a.bitcast(I32), v.bitcast(I32), 1, None,
                                                   ALU.logical_shift_right))
                steps.then(nc.vector.tensor_scalar(o.bitcast(I32), a.bitcast(I32), -1.0, float(RSQRT_GUESS),
                                                   ALU.mult, ALU.add))
                for _ in range(3):
                    steps.then(nc.vector.tensor_tensor(a, o, v, ALU.mult))
                    steps.then(nc.vector.scalar_tensor_tensor(out=a, in0=a, scalar=-0.5, in1=o,
                                                              op0=ALU.mult, op1=ALU.mult))
                    steps.then(nc.vector.scalar_tensor_tensor(out=o, in0=a, scalar=1.5, in1=o,
                                                              op0=ALU.add, op1=ALU.mult))

            def rows_of(b):
                return xall[:, b, :] if isinstance(b, int) else xall[:, bass.ds(b, 1), :].rearrange("p o n -> p (o n)")

            def norm_stats(first, n):
                for b in range(first, first + n):
                    last = nc.vector.bn_stats(stats[:, b, :], xall[:, b, :])
                steps.then(last)
                for b in range(first, first + n):
                    last = nc.vector.bn_aggr(mv[:, b, :], stats[:, b, :])
                steps.then(last)
                rsqrt(rstd[:, first:first + n], mv[:, first:first + n, 1], 1.0, LN_EPS, n)

            def normalize(b, par):
                nc.vector.tensor_scalar(xn[par][:], xall[:, b, :], mv[:, b, 0:1], rstd[:, b:b + 1] if isinstance(b, int)
                                        else rstd[:, bass.ds(b, 1)], ALU.subtract, ALU.mult).then_inc(xn_ready, 1)

            def factors(ten, bank):
                for r in range(2):
                    last = nc.vector.scalar_tensor_tensor(
                        out=rope_ab[:, r, ten, :], in0=bank[:, r * D:(r + 1) * D],
                        scalar=cols[:, 2 * ten + r:2 * ten + r + 1], in1=rope[:, r, :], op0=ALU.add, op1=ALU.mult)
                last.then_inc(misc_free, 1)

            def take_values(par, bank):
                return nc.vector.tensor_copy(vt[par][:, :, :, 0:HD],
                                             bank[:, 0:D].rearrange("m (a h d) -> m a h d", a=2, d=HD))

            def row_max(pair, s, bank):
                half, p4 = pair // 4, pair % 4
                nc.vector.tensor_reduce(mx[:, half, :, 4 * s + p4:4 * s + p4 + 1],
                                        bank.rearrange("n (b m) -> n b m", b=2), AX_X, ALU.max).then_inc(misc_free, 1)

            def take_maxT(half, bank):
                nc.vector.tensor_copy(mT[:, half, :], bank.bitcast(BF16)[0:24, 0:D]).then_inc(misc_free, 1)

            def add_output(b, bank):
                xb = rows_of(b)
                return nc.vector.scalar_tensor_tensor(out=xb, in0=bank[:, D:2 * D], scalar=cb[:], in1=xb,
                                                      op0=ALU.add, op1=ALU.add)

            def flip(b, i):
                dve.wait_ge(pv_done, b * PAIRS + 4 * (i + 1))
                nc.vector.transpose(pvT[i][:], pv_bank(1)).then_inc(pv_free, 1)

            def divide(b, i):
                dve.wait_ge(pv_free, 2 * b + i + 3)
                cells = pvT[i][:].rearrange("p (x r) -> p x r", r=32)
                steps.then(nc.vector.reciprocal(den[i][:], cells[:, :, HD]))
                o = o2[:].rearrange("p (n g d) -> p g n d", g=4, d=HD)
                for g in range(2):
                    last = nc.vector.tensor_tensor(
                        o[:, 2 * i + g], cells[:, 8 * g:8 * g + 8, 0:HD],
                        den[i][:, 8 * g:8 * g + 8].unsqueeze(2).broadcast_to((P, 8, HD)), ALU.mult)
                steps.then(last)
                if i == 1:
                    nc.vector.transpose(o3[:], o2[:]).then_inc(o3_ready, 1)

            for i in range(2):
                steps.then(nc.vector.memset(vt[i][:], 0.0))
                last = nc.vector.memset(vt[i][:, :, :, HD:HD + 1], 1.0)
                last.then_inc(pv_free, 1)
            dve.wait_ge(x_in[0], 16)
            norm_stats(0, FIRST)
            for b in range(FIRST):
                normalize(b, b)
            dve.wait_ge(w_in, 32)
            nc.vector.memset(fill[:, 0], 0.0)
            nc.vector.memset(fill[:, 1, 1], 0.0)
            nc.vector.tensor_copy(fill[:, 1, 0], cols[:, 7:8].broadcast_to((P, D))).then_inc(fill_set, 1)
            dve.wait_ge(rope_in, 16)
            steps.then(nc.vector.tensor_scalar(rope[:, 1, :], rope[:, 1, :], cols[:, 6:7], None, ALU.mult))
            for u, (kind, b) in enumerate(PROLOGUE):
                if (kind, b) == ("k", 2):
                    dve.wait_ge(x_in[1], 16)
                    norm_stats(FIRST, NB - FIRST)
                    normalize(2, 0)
                dve.wait_ge(misc_full, u + 1)
                if kind == "cb":
                    nc.vector.tensor_scalar(cb[:], misc(u)[:, 0:1], cols[:, 5:6], None, ALU.add).then_inc(misc_free, 1)
                elif kind == "v":
                    take_values(0, misc(u)).then_inc(misc_free, 1)
                else:
                    if b and kind == "k":
                        dve.wait_ge(qk_ready, b + 1)
                    factors(int(kind == "k"), misc(u))
                    if (kind, b) == ("q", 0):
                        dve.wait_ge(misc_free, u + 1)
                        dve.wait_ge(qk_ready, 1)
                        add_factors(nc.vector)
                        dve.wait_ge(hi_done, 1)
                        take_rest(nc.vector, 0)
                        dve.wait_ge(mid_done, 1)
                        take_third(nc.vector, 0)
            for u, n in enumerate(FIRST_MAX, len(PROLOGUE)):
                dve.wait_ge(misc_full, u + 1)
                if n is None:
                    take_maxT(0, misc(u))
                else:
                    row_max(n // 2, n % 2, misc(u))

            def slot(b0, i, shape):
                b = b0 + 2 * i
                wm, m, pqk = flags = a_flags(shape)
                if pqk:
                    normalize(b + 3, (b0 + 1) % 2)
                n = 0
                for spot in range(2 * PAIRS):
                    if spot in (7, 15):
                        flip(b, spot // 8)
                    for use in a_uses(spot, *flags):
                        dve.wait_ge(misc_full, a_base(b) + n + 1)
                        bank = misc(a_base(b0) + n)
                        if use[0] == "max":
                            if use[1] % 4 == 0 and use[2] == 0:
                                dve.wait_ge(neg_done, 2 * b + use[1] // 4 + 1)
                            row_max(use[1], use[2], bank)
                        elif use[0] == "q":
                            dve.wait_ge(qk_ready, b + 4)
                            factors(0, bank)
                        elif use[0] == "k":
                            factors(1, bank)
                        elif use[0] == "maxT":
                            if use[1] == 0 or shape:
                                dve.wait_ge(mrow_in[use[1]], 16 * b + (0 if use[1] else 16))
                            take_maxT(use[1], bank)
                        else:
                            if m:
                                if shape:
                                    dve.wait_ge(pv_done, b * PAIRS)
                                last = take_values((b0 + 1) % 2, bank)
                            if wm:
                                last = add_output(b - 1, bank)
                            last.then_inc(misc_free, 1)
                        n += 1
                    if spot == 1 and wm:
                        divide(b - 1, 1)
                    if spot == 8:
                        divide(b, 0)
                    if spot == 10 and shape == NB - 1:
                        norm_stats(0, B_EARLY)
                        for early in range(2):
                            normalize(early, early)

            slot(0, 0, 0)
            with dve.Fori(0, 2) as i:
                steps.enter(i, 8)
                for b0 in (1, 2):
                    slot(b0, i, 1)
            steps.leave(2)
            for b in (5, 6, 7):
                slot(b, 0, b)
            divide(NB - 1, 1)

            def spread(small, big, n):
                return small.unsqueeze(2).broadcast_to((P, big, n))

            def pick(hot_o, peak, v, groups, n):
                num = rows[:, 3 * NE:3 * NE + n] if n == NE else rows[:, 4 * NE - n:4 * NE]
                num = num.unsqueeze(1).broadcast_to((P, groups, n))
                th = hot_t[:].rearrange("p b e -> p (b e)")[:, 0:groups * n].rearrange("p (b e) -> p b e", e=n)
                low = top_i[:, 0:groups]
                steps.then(nc.vector.tensor_reduce(peak.unsqueeze(2), v, AX_X, ALU.max))
                steps.then(nc.vector.tensor_tensor(th, v, spread(peak, groups, n), ALU.is_equal))
                steps.then(nc.vector.tensor_tensor(th, th, num, ALU.mult))
                steps.then(nc.vector.tensor_reduce(low.unsqueeze(2), th, AX_X, ALU.min))
                steps.then(nc.vector.tensor_tensor(hot_o, num, spread(low, groups, n), ALU.is_equal))

            def drop(v, hot_i):
                steps.then(nc.vector.scalar_tensor_tensor(out=v, in0=hot_i, scalar=-3.0e38, in1=v,
                                                          op0=ALU.mult, op1=ALU.add))

            dve.wait_ge(ffn_in, FFN_IN)
            for n, use in enumerate(B_USES):
                u = A_END + n
                dve.wait_ge(misc_full, u + 1)
                bank = misc(u)
                if use[0] == "xT":
                    b = use[1]
                    nc.vector.tensor_copy(xnT[:, :, b * P:(b + 1) * P], bank[:, 0:D].rearrange("p (f n) -> p f n", f=2)
                                          ).then_inc(misc_free, 1)
                    if b + 2 < B_EARLY:
                        normalize(b + 2, b % 2)
                elif use[0] == "wm":
                    add_output(NB - 1, bank).then_inc(misc_free, 1)
                    dve.wait_ge(misc_free, u + 1)
                    norm_stats(B_EARLY, NB - B_EARLY)
                    for b in range(B_EARLY, NB):
                        normalize(b, b % 2)
                elif use[0] == "lgT":
                    nc.vector.tensor_copy(lgT[:, use[1] * HALF:(use[1] + 1) * HALF], bank[0:NE, :]
                                          ).then_inc(misc_free, 1)
                elif use[0] == "lg":
                    dve.wait_ge(sig_ready, 1)
                    steps.then(nc.vector.tensor_scalar(sc[:], sc[:], 1.0, None, ALU.add))
                    steps.then(nc.vector.reciprocal(sc[:], sc[:]))
                    steps.then(nc.vector.tensor_tensor(sel_s[:], sc[:], rows[:, 0:NE].unsqueeze(1).broadcast_to(
                        (P, NB, NE)), ALU.add))
                    s4 = sel_s[:].rearrange("p b (g e) -> p (b g) e", g=4)
                    nc.vector.tensor_tensor(pair_sum[:, :, 0:3], s4[:, :, 0:3], s4[:, :, 1:4], ALU.add)
                    nc.vector.tensor_tensor(pair_sum[:, :, 3:5], s4[:, :, 0:2], s4[:, :, 2:4], ALU.add)
                    steps.then(nc.vector.tensor_tensor(pair_sum[:, :, 5:6], s4[:, :, 0:1], s4[:, :, 3:4], ALU.add))
                    steps.then(nc.vector.tensor_reduce(gsum[:].rearrange("p b g -> p (b g)").unsqueeze(2),
                                                       pair_sum[:], AX_X, ALU.max))
                    g4 = [h[:].rearrange("p b e -> p (b e)")[:, 0:NB * 4].rearrange("p (b g) -> p b g", g=4)
                          for h in hot]
                    pick(g4[0], top[0][:], gsum[:], NB, 4)
                    drop(gsum[:], g4[0])
                    pick(g4[1], top[0][:], gsum[:], NB, 4)
                    steps.then(nc.vector.tensor_tensor(gsum[:], g4[0], g4[1], ALU.add))
                    steps.then(nc.vector.tensor_tensor(
                        s4, s4, spread(gsum[:].rearrange("p b g -> p (b g)"), NB * 4, 4), ALU.mult))
                    pick(hot[0][:], top[0][:], sel_s[:], NB, NE)
                    drop(sel_s[:], hot[0][:])
                    pick(hot[1][:], top[0][:], sel_s[:], NB, NE)
                    steps.then(nc.vector.tensor_tensor(comb[:], hot[0][:], hot[1][:], ALU.add))
                    steps.then(nc.vector.tensor_tensor(comb[:], comb[:], sc[:], ALU.mult))
                    steps.then(nc.vector.tensor_reduce(top[0][:].unsqueeze(2), comb[:], AX_X, ALU.add))
                    steps.then(nc.vector.tensor_scalar(top[0][:], top[0][:], 1e-20, None, ALU.add))
                    steps.then(nc.vector.reciprocal(top[1][:], top[0][:]))
                    nc.vector.tensor_tensor(comb[:], comb[:], spread(top[1][:], NB, NE), ALU.mult
                                            ).then_inc(misc_free, 1)

            dve.wait_ge(w2_in, 16 * 6)
            steps.then(nc.vector.tensor_scalar(nrb1[:, 1:2], nrb1[:, 0:1], -1.0, None, ALU.mult))

            dve.wait_ge(misc_free, B_END)

            def add_group(c, g):
                if g < N_SHARED - 1:
                    return
                y = c * GROUPS + g - N_SHARED + 1
                dve.wait_ge(y_full, y + 1)
                if y:
                    dve.wait_ge(y_free, y)
                for j in range(4):
                    b = 4 * c + j
                    src = y_banks(y)[:, j // 2, (j % 2) * D:(j % 2 + 1) * D]
                    if g < N_SHARED:
                        last = nc.vector.tensor_tensor(xall[:, b, :], src, xall[:, b, :], ALU.add)
                    else:
                        e = BLOCKS[g]
                        last = nc.vector.scalar_tensor_tensor(
                            out=xall[:, b, :], in0=src, scalar=comb[:, b, e:e + 1], in1=xall[:, b, :],
                            op0=ALU.mult, op1=ALU.add)
                last.then_inc(y_free, 1)

            for g in range(NCH):
                add_group(0, g)

            dve.wait_ge(y_free, GROUPS)
            norm_stats(0, 4)
            for b in range(2):
                normalize(b, b)

            def c_use(kind, par, bank, b):
                if kind == "xT":
                    nc.vector.tensor_copy(xT1[:], bank[:, 0:D].rearrange("p (f n) -> p f n", f=2)
                                          ).then_inc(misc_free, 1)
                elif kind == "cT":
                    nc.vector.tensor_copy(ctxT[par][:], bank[:, 0:D].rearrange("p (f n) -> p f n", f=2)
                                          ).then_inc(misc_free, 1)
                elif kind == "qk":
                    dve.wait_ge(sq_done, b + 1)
                    steps.then(nc.vector.tensor_reduce(
                        ss[:].unsqueeze(2), sq[:].rearrange("n (h d) -> n h d", d=HD), AX_X, ALU.add))
                    rsqrt(rs[:], ss[:], 1.0 / HD, RMS_EPS, 64)
                    for ten in range(2):
                        last = nc.vector.tensor_tensor(
                            qkn[:, ten].rearrange("n (h d) -> n h d", d=HD),
                            bank[:, ten * D:(ten + 1) * D].rearrange("n (h d) -> n h d", d=HD),
                            rs[:, 32 * ten:32 * ten + 32].unsqueeze(2).broadcast_to((P, 32, HD)), ALU.mult)
                    last.then_inc(misc_free, 1)
                elif kind == "qkT":
                    dve.wait_ge(hi_done, NB + b + 1)
                    dve.wait_ge(lo_done, NB + b)
                    nc.vector.tensor_tensor(qk_rest[:], bank.rearrange("p (t n) -> p t n", t=2),
                                            parts[par][:, :, 0, :], ALU.subtract).then_inc(misc_free, 1)
                elif kind == "v":
                    nc.vector.tensor_copy(vt[par][:].rearrange("m a h r -> m (a h) r")[:, :, 0:HD],
                                          bank[:, 0:D].rearrange("m (h d) -> m h d", d=HD)).then_inc(misc_free, 1)
                else:
                    nc.vector.tensor_tensor(rows_of(b), bank[:, 0:D], rows_of(b), ALU.add).then_inc(misc_free, 1)

            def divide_c(b, i):
                dve.wait_ge(pv_done, NB * PAIRS + b * C_STEPS + 2 * (i + 1))
                nc.vector.transpose(pvT[i][:], pv_bank(i)).then_inc(pv_free, 1)
                dve.wait_ge(pv_free, 2 * NB + 2 * b + i + 3)
                cells = pvT[i][:].rearrange("p (x r) -> p x r", r=32)
                steps.then(nc.vector.reciprocal(den[i][:], cells[:, :, HD]))
                steps.then(nc.vector.tensor_tensor(
                    o2[:, i * P:(i + 1) * P].rearrange("p (n g d) -> p g n d", n=4, d=HD),
                    cells[:, :, 0:HD].rearrange("p (g n) d -> p g n d", g=4),
                    den[i][:].rearrange("p (g n) -> p g n", g=4).unsqueeze(3).broadcast_to((P, 4, 4, HD)), ALU.mult))
                if i == 1:
                    nc.vector.transpose(o3[:], o2[:]).then_inc(o3_ready, 1)

            for g in range(NCH):
                add_group(1, g)
                n = g - C_AFTER
                if 0 <= n < len(C_PRO):
                    kind, b = C_PRO[n]
                    dve.wait_ge(misc_full, B_END + n + 1)
                    c_use(kind, b % 2, misc(B_END + n), b)
                    if kind == "xT" and b == 0:
                        normalize(2, 0)
            dve.wait_ge(y_free, 2 * GROUPS)
            norm_stats(4, 4)

            def d_use(kind, n, bank):
                if kind == "dxT":
                    nc.vector.tensor_copy(xnT[:, :, n * P:(n + 1) * P],
                                          bank[:, 0:D].rearrange("p (f n) -> p f n", f=2)).then_inc(misc_free, 1)
                    if n % 4 < 2:
                        normalize(n + 2, n % 2)
                elif kind == "dh":
                    dve.wait_ge(eh_done, n + 1)
                    nc.vector.tensor_scalar(zh[:], bank[:, 0:D], nrb1[:, 0:1], None, ALU.add)
                    steps.then(nc.vector.tensor_scalar(eh[:], eh[:], 1.0, None, ALU.add))
                    steps.then(nc.vector.reciprocal(eh[:], eh[:]))
                    nc.vector.tensor_tensor(eh[:], eh[:], zh[:], ALU.mult).then_inc(misc_free, 1)
                else:
                    lg = sel_s[:, 0:4, :]
                    h0, h1 = hot[0][:, 0:4, :], hot[1][:, 0:4, :]
                    for q in range(2):
                        row = rows[:, (q + 1) * NE:(q + 2) * NE].unsqueeze(1).broadcast_to((P, 4, NE))
                        src = bank[:, 0:4 * NE].rearrange("p (b e) -> p b e", e=NE) if q == 0 else lg
                        steps.then(nc.vector.tensor_tensor(lg, src, row, ALU.add))
                    pick(h0, top[0][:, 0:4], lg, 4, NE)
                    drop(lg, h0)
                    pick(h1, top[1][:, 0:4], lg, 4, NE)
                    nc.vector.tensor_tensor(top_i[:, 0:4], top[1][:, 0:4], top[0][:, 0:4], ALU.subtract
                                            ).then_inc(gap_done, 1)
                    if n == 0:
                        nc.vector.drain().then_inc(misc_free, 1)
                    else:
                        weights_of(1)

            def weights_of(c):
                h0, h1 = hot[0][:, 0:4, :], hot[1][:, 0:4, :]
                dve.wait_ge(egap_done, c + 1)
                steps.then(nc.vector.tensor_scalar(top[0][:, 0:4], top_i[:, 0:4], 1.0, None, ALU.add))
                steps.then(nc.vector.reciprocal(top[0][:, 0:4], top[0][:, 0:4]))
                steps.then(nc.vector.tensor_tensor(top[1][:, 0:4], top_i[:, 0:4], top[0][:, 0:4], ALU.mult))
                steps.then(nc.vector.tensor_tensor(h0, h0, spread(top[0][:, 0:4], 4, NE), ALU.mult))
                steps.then(nc.vector.tensor_tensor(h1, h1, spread(top[1][:, 0:4], 4, NE), ALU.mult))
                ins = nc.vector.tensor_tensor(comb[:, 4 * c:4 * c + 4, :], h0, h1, ALU.add)
                if c:
                    ins.then_inc(misc_free, 1)
                    dve.wait_ge(misc_free, d_index(("dlg", 1)) + 1)
                else:
                    steps.then(ins)

            def slot_c(b0, i, shape):
                b = b0 + 2 * i
                o, m, t2, pqk, late = flags = c_flags(shape)
                if pqk:
                    normalize(b + 3, (b0 + 1) % 2)
                n = 0
                for spot in range(2 * C_STEPS):
                    if spot in (3, 7):
                        divide_c(b, spot // 7)
                    for kind, *what in c_uses(spot, *flags):
                        dve.wait_ge(misc_full, c_base(b) + n + 1)
                        if what:
                            d_use(kind, what[0], misc(c_base(b) + n))
                            n += 1
                            continue
                        if kind == "v" and shape:
                            dve.wait_ge(pv_done, NB * PAIRS + b * C_STEPS)
                        c_use(kind, (b0 + AHEAD[kind]) % 2, misc(c_base(b0) + n), b + AHEAD[kind])
                        n += 1
                    if spot == 4 and shape == 5:
                        norm_stats(0, 4)
                        for early in range(2):
                            normalize(early, early)
                    if spot == 5 and shape == 7:
                        weights_of(0)

            slot_c(0, 0, 0)
            with dve.Fori(0, 2) as i:
                steps.enter(i, 2 * (1 + 12 + 4))
                for b0 in (1, 2):
                    slot_c(b0, i, 1)
            steps.leave(2)
            for b in (5, 6, 7):
                slot_c(b, 0, b)

            def ring(use):
                u = d_index(use)
                dve.wait_ge(misc_full, u + 1)
                if use[0] == "o":
                    c_use("o", 1, misc(u), NB - 1)
                else:
                    d_use(*use, misc(u))

            def weigh(b):
                dve.wait_ge(wide_done, b + 1)
                if b >= 4:
                    dve.wait_ge(wt_full, b - 3)
                nc.vector.tensor_tensor(wxa[b % 4][:].rearrange("p (e r) -> p e r", e=NE),
                                        psum[:, b % 4, D:2 * D].rearrange("p (e r) -> p e r", e=NE),
                                        spread(comb[:, b, :], NE, D // NE), ALU.mult).then_inc(wxa_done, 1)

            def add_bias(b):
                steps.then(nc.vector.tensor_tensor(xall[:, b, :], xall[:, b, :], rows[:, 4 * NE:4 * NE + D], ALU.add))

            def finish(b):
                dve.wait_ge(delta_done, b + 1)
                nc.vector.tensor_tensor(xall[:, b, :], psum[:, b % 4, 0:D], xall[:, b, :], ALU.add
                                        ).then_inc(result, 1)

            weigh(0)
            ring(("o",))
            dve.wait_ge(misc_free, d_index(("o",)) + 1)
            norm_stats(4, 4)
            normalize(4, 0)
            normalize(5, 1)
            weigh(1)
            ring(("dxT", 4))
            ring(("dxT", 5))
            weigh(2)
            ring(("dxT", 6))
            weigh(3)
            ring(("dxT", 7))
            for b in range(4):
                add_bias(b)
            finish(0)
            finish(1)
            ring(("dh", 1))
            finish(2)
            finish(3)
            for b in range(4, NB):
                add_bias(b)
            ring(("dlg", 1))
            for b in range(4, NB):
                weigh(b)
            for b in range(4, NB):
                finish(b)


def layouts(inp):
    a = {k: np.asarray(v) for k, v in inp.items()}
    half, p4, s, d = np.meshgrid(np.arange(2), np.arange(4), np.arange(2), np.arange(HD), indexing="ij")
    c0 = (16 * d + 8 * half + 4 * s + p4).ravel()
    c0_rot = (16 * (d ^ 1) + 8 * half + 4 * s + p4).ravel()
    dd = d.ravel()
    k_, s_, d_ = np.meshgrid(np.arange(PAIRS), np.arange(2), np.arange(HD), indexing="ij")
    v0 = (16 * d_ + 8 * (k_ // 4) + 4 * s_ + k_ % 4).ravel()
    j_, g_, e_ = np.meshgrid(np.arange(4), np.arange(4), np.arange(HD), indexing="ij")
    kk = 2 * g_ + j_ // 2
    o0 = (16 * e_ + 8 * (kk // 4) + 4 * (j_ % 2) + kk % 4).ravel()
    wq, wk, wv, wm = (a[f"L0_xattn_W{x}"] for x in "qkvm")
    bq, bk, bv, bm = (a[f"L0_xattn_b{x}"] for x in "qkvm")
    wa = np.concatenate([wq[c0].T, wq[c0_rot].T, wk[c0].T, wk[c0_rot].T, wv[v0].T, wm[:, o0].T], axis=1)
    sign = np.where(dd % 2, 1.0, -1.0).astype(np.float32)
    one = (((np.arange(P) % 16) >= 5) & ((np.arange(P) % 16) < 11)).astype(np.float32)
    cols = np.stack([bq[c0], bq[c0_rot], bk[c0], bk[c0_rot], bv[o0], bm, sign, one], axis=1)
    enc = a["L0_xattn_encoding"].reshape(2, D, HD)
    rope = np.concatenate([enc[0].T[dd], enc[1].T[dd]], axis=1)
    bf16 = mybir.dt.np(BF16)
    def blocks(w):
        return w.reshape(2, P, -1).transpose(1, 0, 2)

    up = a["L0_ffn_w_up"].reshape(NE, 2, P, INTER).transpose(2, 1, 0, 3)
    s_up = a["L0_ffn_shared_up"].reshape(2, P, NCH - NE, INTER).transpose(1, 0, 2, 3)
    dn = a["L0_ffn_w_down"].transpose(1, 0, 2)
    s_dn = a["L0_ffn_shared_down"].reshape(NCH - NE, INTER, D).transpose(1, 0, 2)
    row = np.concatenate([a["L0_ffn_e_bias"], a["L1_ffn_rb2"][:NE], a["L1_ffn_gates"],
                          np.arange(-NE, 0, dtype=np.float32), a["L1_ffn_bias"]])
    ch, hf, pm, sm, dm = np.meshgrid(np.arange(2), np.arange(2), np.arange(4), np.arange(2), np.arange(HD), indexing="ij")
    hd = 16 * hf + 4 * (2 * ch + sm) + pm
    q1, kv1 = (HD * hd + dm).ravel(), (2 * (HD * hd + dm)).ravel()
    pr, cv, sv, dv = np.meshgrid(np.arange(PAIRS), np.arange(2), np.arange(2), np.arange(HD), indexing="ij")
    v1 = (2 * (HD * (16 * (pr // 4) + 4 * (2 * cv + sv) + pr % 4) + dv) + 1).ravel()
    wkv = np.concatenate([a["L1_xattn_Wk"], a["L1_xattn_Wv"]], axis=0)
    wc = blocks(np.concatenate([a["L1_xattn_Wq"][q1].T, wkv[kv1].T, wkv[v1].T], axis=1))
    wA = a["L1_ffn_A"].reshape(D, D).T
    wB = a["L1_ffn_B"].transpose(0, 2, 1).reshape(D, D)
    rw2 = np.zeros((2, RH, 2, NE), np.float32)
    for s_ in range(2):
        rw2[s_, :, s_] = a["L1_ffn_rw2"][:NE].T
    rw2 = rw2.reshape(2 * RH, 2, NE)
    t = {"wr": blocks(a["L0_ffn_router_weight"].T), "rows": np.broadcast_to(row, (P, row.size)),
         "wup": np.concatenate([up, s_up], axis=2), "wdn": np.concatenate([dn, s_dn], axis=1),
         "wc": wc, "wd": blocks(np.concatenate([a["L1_ffn_W"].T, wA], axis=1)), "wb": blocks(wB),
         "w1": blocks(a["L1_ffn_rw1"].T), "w2": rw2, "rb1": np.tile(a["L1_ffn_rb1"], 2).reshape(2 * RH, 1),
         "x": a["x"], "ctx": a["ctx_2048"], "wa": wa, "cols": cols, "rope": rope,
         "eye": np.eye(P, dtype=np.float32), "eye16": np.eye(P).astype(bf16)}
    return {k: np.ascontiguousarray(v) for k, v in t.items()}


def kernel(**inputs):
    import concourse.bacc as bacc
    from concourse.bass_utils import run_bass_kernel_spmd

    nc = bacc.Bacc("TRN2", target_bir_lowering=False, num_devices=1)
    arrays = {f"in_{k}": v for k, v in layouts(inputs).items()}
    t = {k[3:]: nc.dram_tensor(k, v.shape, mybir.dt.from_np(v.dtype), kind="ExternalInput").ap()
         for k, v in arrays.items()}
    out = nc.dram_tensor("out_0", (NB, P, D), F32, kind="ExternalOutput").ap()
    build(nc, t, out)
    return run_bass_kernel_spmd(nc, [arrays], core_ids=[0]).results[0]["out_0"]
```
